# Optimizing a Trainium2 kernel written in Bass

```python
import numpy as np
import jax
import jax.numpy as jnp

def _softmax(x, axis=-1):
    return jax.nn.softmax(x, axis=axis)

def _gelu(x):
    return jax.nn.gelu(x, approximate=True)

def _silu(x):
    return jax.nn.silu(x)

def _sigmoid(x):
    return jax.nn.sigmoid(x)

def _layernorm(x, axis=-1, eps=1e-05):
    m = jnp.mean(x, axis=axis, keepdims=True)
    v = jnp.var(x, axis=axis, keepdims=True)
    return (x - m) / jnp.sqrt(v + eps)

def _scatter_add(tgt, idx, src, axis=0):
    return tgt.at[idx].add(src)

def _segment_sum(src, seg, n):
    return jax.ops.segment_sum(src, seg, n)
kernel_name = 'mk_hybrid_d1_jaxref_r8_b331dc'

def setup_inputs(seed: int=0):
    np.random.seed(seed)
    _w = jnp.asarray

    def _L0_attn_a_setup():
        import jax, jax.numpy as jnp
        import numpy as np
        import math
        D_MODEL = 128
        NUM_HEADS = 16
        HEAD_DIM = D_MODEL // NUM_HEADS
        key = jax.random.key(seed)
        k_x, k_qkv, k_o = jax.random.split(key, 3)
        B, S = (2, 256)
        x = jax.random.normal(k_x, (B, S, D_MODEL), dtype=jnp.float32)
        sigma_qkv = math.sqrt(2.0 / (D_MODEL + 3 * D_MODEL))
        w_qkv = jax.random.truncated_normal(k_qkv, -3.0, 3.0, (3 * D_MODEL, D_MODEL), dtype=jnp.float32) * sigma_qkv
        sigma_o = math.sqrt(2.0 / (D_MODEL + D_MODEL))
        w_out = jax.random.truncated_normal(k_o, -3.0, 3.0, (D_MODEL, D_MODEL), dtype=jnp.float32) * sigma_o
        return {'x': x, 'w_qkv': w_qkv, 'w_out': w_out}
    _L0_attn_a_in = _L0_attn_a_setup()

    def _L0_attn_b_setup():
        import jax, jax.numpy as jnp
        import numpy as np
        DIM = 128
        HEADS = 16
        GROUPS = 4
        DIM_HEAD = 64
        INNER = HEADS * DIM_HEAD
        KV_DIM = 2 * DIM_HEAD * GROUPS
        B, N = (4, 256)
        EPS = 1e-06

        def _layernorm(x, scale, bias, eps=EPS):
            mu = jnp.mean(x, axis=-1, keepdims=True)
            var = jnp.mean(jnp.square(x - mu), axis=-1, keepdims=True)
            return (x - mu) * jax.lax.rsqrt(var + eps) * scale + bias
        key = jax.random.key(seed)
        ks = jax.random.split(key, 10)
        lecun = lambda k, shape: jax.random.normal(k, shape, jnp.float32) * (1.0 / np.sqrt(shape[0]))
        return {'x': jax.random.normal(ks[0], (B, N, DIM), jnp.float32), 'ln_scale': jnp.ones((DIM,), jnp.float32), 'ln_bias': jnp.zeros((DIM,), jnp.float32), 'Wq': lecun(ks[1], (DIM, INNER)), 'Wkv': lecun(ks[2], (DIM, KV_DIM)), 'qn_scale': jnp.ones((DIM_HEAD,), jnp.float32), 'qn_bias': jnp.zeros((DIM_HEAD,), jnp.float32), 'kn_scale': jnp.ones((DIM_HEAD,), jnp.float32), 'kn_bias': jnp.zeros((DIM_HEAD,), jnp.float32), 'Wout': lecun(ks[3], (INNER, DIM))}
    _L0_attn_b_in = _L0_attn_b_setup()

    def _L0_ffn_setup():
        import jax, jax.numpy as jnp
        import numpy as np
        DIM = 128
        DEPTH = 6
        HEADS = 16
        DIM_HEAD = 64
        WINDOW = 32
        INNER = HEADS * DIM_HEAD
        DIM_INNER = int(DIM * 4 * 2 / 3)
        QK_SCALE = 8.0

        def shift_tokens(t):
            a, s = jnp.split(t, 2, -1)
            s = jnp.pad(s, ((0, 0), (1, 0), (0, 0)))[:, :-1]
            return jnp.concatenate([a, s], -1)

        def l2norm(t):
            return t / jnp.maximum(jnp.linalg.norm(t, axis=-1, keepdims=True), 1e-12)

        def rotate_half(x):
            x1, x2 = jnp.split(x, 2, -1)
            return jnp.concatenate([-x2, x1], -1)

        def rotary_tables(n):
            half = jnp.arange(0, DIM_HEAD, 2, dtype=jnp.float32)
            inv_freq = 1.0 / 10000.0 ** (half / DIM_HEAD)
            t = jnp.arange(n, dtype=jnp.float32)
            freqs = t[:, None] * inv_freq[None, :]
            freqs = jnp.concatenate([freqs, freqs], -1)
            base_scale = (half + 0.4 * DIM_HEAD) / (1.4 * DIM_HEAD)
            power = (t - n // 2) / (WINDOW // 2)
            scale = base_scale[None, :] ** power[:, None]
            scale = jnp.concatenate([scale, scale], -1)
            return (freqs, scale)

        def local_attention(q, k, v):
            b, h, n, d = q.shape
            w = WINDOW
            nw = n // w
            bq = q.reshape(b, h, nw, w, d)
            bk = k.reshape(b, h, nw, w, d)
            bv = v.reshape(b, h, nw, w, d)

            def look(t):
                p = jnp.pad(t, ((0, 0), (0, 0), (1, 0), (0, 0), (0, 0)))
                return jnp.concatenate([p[:, :, :nw], p[:, :, 1:]], axis=3)
            bk2, bv2 = (look(bk), look(bv))
            seq = jnp.arange(n).reshape(nw, w)
            seq_p = jnp.pad(seq, ((1, 0), (0, 0)), constant_values=-1)
            jt = jnp.concatenate([seq_p[:nw], seq_p[1:]], axis=1)
            it = seq[:, :, None]
            jb = jt[:, None, :]
            mask = (it < jb) | (it > jb + w) | (jb == -1)
            sim = jnp.einsum('bhwie,bhwje->bhwij', bq, bk2) * QK_SCALE
            sim = jnp.where(mask, -jnp.finfo(sim.dtype).max, sim)
            attn = jax.nn.softmax(sim, -1)
            out = jnp.einsum('bhwij,bhwje->bhwie', attn, bv2)
            return out.reshape(b, h, n, d)

        def attn_layer(x, Wqkv, qs, ksc, Wo):
            b, n, _ = x.shape
            qkv = x @ Wqkv
            q, k, v = jnp.split(qkv, 3, -1)
            sh = lambda t: t.reshape(b, n, HEADS, DIM_HEAD).transpose(0, 2, 1, 3)
            q, k, v = (sh(q), sh(k), sh(v))
            q = l2norm(q) * qs
            k = l2norm(k) * ksc
            freqs, scale = rotary_tables(n)
            cos, sin = (jnp.cos(freqs), jnp.sin(freqs))
            q = q * cos * scale + rotate_half(q) * sin * scale
            inv = 1.0 / scale
            k = k * cos * inv + rotate_half(k) * sin * inv
            out = local_attention(q, k, v)
            out = out.transpose(0, 2, 1, 3).reshape(b, n, INNER)
            return out @ Wo

        def ffn_layer(x, g, bln, W1, b1, W2, b2):
            mu = x.mean(-1, keepdims=True)
            var = ((x - mu) ** 2).mean(-1, keepdims=True)
            xn = (x - mu) / jnp.sqrt(var + 1e-05) * g + bln
            hg = xn @ W1 + b1
            a, gate = jnp.split(hg, 2, -1)
            return a * jax.nn.gelu(gate, approximate=False) @ W2 + b2
        key = jax.random.key(seed)
        ks = jax.random.split(key, 8)
        B, N = (2, 256)
        init = lambda k, shape: jax.random.normal(k, shape, jnp.float32) * 0.02
        return {'x': jax.random.normal(ks[0], (B, N, DIM), jnp.float32), 'Wqkv': init(ks[1], (DEPTH, DIM, 3 * INNER)), 'q_scale': jnp.ones((DEPTH, DIM_HEAD), jnp.float32), 'k_scale': jnp.ones((DEPTH, DIM_HEAD), jnp.float32), 'Wo': init(ks[2], (DEPTH, INNER, DIM)), 'ln_g': jnp.ones((DEPTH, DIM), jnp.float32), 'ln_b': jnp.zeros((DEPTH, DIM), jnp.float32), 'W1': init(ks[3], (DEPTH, DIM, 2 * DIM_INNER)), 'b1': jnp.zeros((DEPTH, 2 * DIM_INNER), jnp.float32), 'W2': init(ks[4], (DEPTH, DIM_INNER, DIM)), 'b2': jnp.zeros((DEPTH, DIM), jnp.float32)}
    _L0_ffn_in = _L0_ffn_setup()
    _d = {'L0_attn_a_x': _L0_attn_a_in['x'], 'L0_attn_a_w_qkv': _L0_attn_a_in['w_qkv'], 'L0_attn_a_w_out': _L0_attn_a_in['w_out'], 'L0_attn_b_ln_scale': _L0_attn_b_in['ln_scale'], 'L0_attn_b_ln_bias': _L0_attn_b_in['ln_bias'], 'L0_attn_b_Wq': _L0_attn_b_in['Wq'], 'L0_attn_b_Wkv': _L0_attn_b_in['Wkv'], 'L0_attn_b_qn_scale': _L0_attn_b_in['qn_scale'], 'L0_attn_b_qn_bias': _L0_attn_b_in['qn_bias'], 'L0_attn_b_kn_scale': _L0_attn_b_in['kn_scale'], 'L0_attn_b_kn_bias': _L0_attn_b_in['kn_bias'], 'L0_attn_b_Wout': _L0_attn_b_in['Wout'], 'L0_ffn_Wqkv': _L0_ffn_in['Wqkv'], 'L0_ffn_q_scale': _L0_ffn_in['q_scale'], 'L0_ffn_k_scale': _L0_ffn_in['k_scale'], 'L0_ffn_Wo': _L0_ffn_in['Wo'], 'L0_ffn_ln_g': _L0_ffn_in['ln_g'], 'L0_ffn_ln_b': _L0_ffn_in['ln_b'], 'L0_ffn_W1': _L0_ffn_in['W1'], 'L0_ffn_b1': _L0_ffn_in['b1'], 'L0_ffn_W2': _L0_ffn_in['W2'], 'L0_ffn_b2': _L0_ffn_in['b2']}
    _x0 = _d['L0_attn_a_x']
    _d['L0_attn_a_x'] = jax.random.normal(jax.random.fold_in(jax.random.key(seed), 1), (1, 2048, 128), dtype=_x0.dtype)
    del _x0
    return _d

def reference(L0_attn_a_x, L0_attn_a_w_qkv, L0_attn_a_w_out, L0_attn_b_ln_scale, L0_attn_b_ln_bias, L0_attn_b_Wq, L0_attn_b_Wkv, L0_attn_b_qn_scale, L0_attn_b_qn_bias, L0_attn_b_kn_scale, L0_attn_b_kn_bias, L0_attn_b_Wout, L0_ffn_Wqkv, L0_ffn_q_scale, L0_ffn_k_scale, L0_ffn_Wo, L0_ffn_ln_g, L0_ffn_ln_b, L0_ffn_W1, L0_ffn_b1, L0_ffn_W2, L0_ffn_b2):

    def _L0_attn_a_ref(x, w_qkv, w_out):
        import jax, jax.numpy as jnp
        import numpy as np
        import math
        D_MODEL = 128
        NUM_HEADS = 16
        HEAD_DIM = D_MODEL // NUM_HEADS
        B, S, _ = x.shape
        qkv = jnp.einsum('bsi,oi->bso', x, w_qkv)
        q, k, v = jnp.split(qkv, 3, axis=-1)

        def to_heads(t):
            return t.reshape(B, S, NUM_HEADS, HEAD_DIM).transpose(0, 2, 1, 3)
        q, k, v = (to_heads(q), to_heads(k), to_heads(v))
        scale = 1.0 / math.sqrt(HEAD_DIM)
        logits = jnp.einsum('bhsd,bhtd->bhst', q, k) * scale
        mask = jnp.tril(jnp.ones((S, S), dtype=bool))
        neg_inf = jnp.finfo(jnp.float32).min
        logits = jnp.where(mask, logits, neg_inf)
        probs = jax.nn.softmax(logits, axis=-1)
        probs = probs * mask.astype(probs.dtype)
        out = jnp.einsum('bhst,bhtd->bhsd', probs, v)
        out = out.transpose(0, 2, 1, 3).reshape(B, S, D_MODEL)
        return jnp.einsum('bsi,oi->bso', out, w_out)

    def _L0_attn_b_ref(x, ln_scale, ln_bias, Wq, Wkv, qn_scale, qn_bias, kn_scale, kn_bias, Wout):
        import jax, jax.numpy as jnp
        import numpy as np
        DIM = 128
        HEADS = 16
        GROUPS = 4
        DIM_HEAD = 64
        INNER = HEADS * DIM_HEAD
        KV_DIM = 2 * DIM_HEAD * GROUPS
        B, N = (4, 256)
        EPS = 1e-06

        def _layernorm(x, scale, bias, eps=EPS):
            mu = jnp.mean(x, axis=-1, keepdims=True)
            var = jnp.mean(jnp.square(x - mu), axis=-1, keepdims=True)
            return (x - mu) * jax.lax.rsqrt(var + eps) * scale + bias
        b, n, _ = x.shape
        g, hg, d = (GROUPS, HEADS // GROUPS, DIM_HEAD)
        scale = d ** (-0.5)
        xn = _layernorm(x, ln_scale, ln_bias)
        q = (xn @ Wq).reshape(b, n, HEADS, d).transpose(0, 2, 1, 3)
        kv = xn @ Wkv
        k, v = jnp.split(kv, 2, axis=-1)
        k = k.reshape(b, n, g, d).transpose(0, 2, 1, 3)
        v = v.reshape(b, n, g, d).transpose(0, 2, 1, 3)
        q = _layernorm(q, qn_scale, qn_bias)
        k = _layernorm(k, kn_scale, kn_bias)
        qg = q.reshape(b, g, hg, n, d)
        dots = jnp.einsum('bghqd,bgkd->bghqk', qg, k) * scale
        attn = jax.nn.softmax(dots, axis=-1)
        out = jnp.einsum('bghqk,bgkd->bghqd', attn, v)
        out = out.transpose(0, 3, 1, 2, 4).reshape(b, n, g * hg * d)
        return out @ Wout

    def _L0_ffn_ref(x, Wqkv, q_scale, k_scale, Wo, ln_g, ln_b, W1, b1, W2, b2):
        import jax, jax.numpy as jnp
        import numpy as np
        DIM = 128
        DEPTH = 6
        HEADS = 16
        DIM_HEAD = 64
        WINDOW = 32
        INNER = HEADS * DIM_HEAD
        DIM_INNER = int(DIM * 4 * 2 / 3)
        QK_SCALE = 8.0

        def shift_tokens(t):
            a, s = jnp.split(t, 2, -1)
            s = jnp.pad(s, ((0, 0), (1, 0), (0, 0)))[:, :-1]
            return jnp.concatenate([a, s], -1)

        def l2norm(t):
            return t / jnp.maximum(jnp.linalg.norm(t, axis=-1, keepdims=True), 1e-12)

        def rotate_half(x):
            x1, x2 = jnp.split(x, 2, -1)
            return jnp.concatenate([-x2, x1], -1)

        def rotary_tables(n):
            half = jnp.arange(0, DIM_HEAD, 2, dtype=jnp.float32)
            inv_freq = 1.0 / 10000.0 ** (half / DIM_HEAD)
            t = jnp.arange(n, dtype=jnp.float32)
            freqs = t[:, None] * inv_freq[None, :]
            freqs = jnp.concatenate([freqs, freqs], -1)
            base_scale = (half + 0.4 * DIM_HEAD) / (1.4 * DIM_HEAD)
            power = (t - n // 2) / (WINDOW // 2)
            scale = base_scale[None, :] ** power[:, None]
            scale = jnp.concatenate([scale, scale], -1)
            return (freqs, scale)

        def local_attention(q, k, v):
            b, h, n, d = q.shape
            w = WINDOW
            nw = n // w
            bq = q.reshape(b, h, nw, w, d)
            bk = k.reshape(b, h, nw, w, d)
            bv = v.reshape(b, h, nw, w, d)

            def look(t):
                p = jnp.pad(t, ((0, 0), (0, 0), (1, 0), (0, 0), (0, 0)))
                return jnp.concatenate([p[:, :, :nw], p[:, :, 1:]], axis=3)
            bk2, bv2 = (look(bk), look(bv))
            seq = jnp.arange(n).reshape(nw, w)
            seq_p = jnp.pad(seq, ((1, 0), (0, 0)), constant_values=-1)
            jt = jnp.concatenate([seq_p[:nw], seq_p[1:]], axis=1)
            it = seq[:, :, None]
            jb = jt[:, None, :]
            mask = (it < jb) | (it > jb + w) | (jb == -1)
            sim = jnp.einsum('bhwie,bhwje->bhwij', bq, bk2) * QK_SCALE
            sim = jnp.where(mask, -jnp.finfo(sim.dtype).max, sim)
            attn = jax.nn.softmax(sim, -1)
            out = jnp.einsum('bhwij,bhwje->bhwie', attn, bv2)
            return out.reshape(b, h, n, d)

        def attn_layer(x, Wqkv, qs, ksc, Wo):
            b, n, _ = x.shape
            qkv = x @ Wqkv
            q, k, v = jnp.split(qkv, 3, -1)
            sh = lambda t: t.reshape(b, n, HEADS, DIM_HEAD).transpose(0, 2, 1, 3)
            q, k, v = (sh(q), sh(k), sh(v))
            q = l2norm(q) * qs
            k = l2norm(k) * ksc
            freqs, scale = rotary_tables(n)
            cos, sin = (jnp.cos(freqs), jnp.sin(freqs))
            q = q * cos * scale + rotate_half(q) * sin * scale
            inv = 1.0 / scale
            k = k * cos * inv + rotate_half(k) * sin * inv
            out = local_attention(q, k, v)
            out = out.transpose(0, 2, 1, 3).reshape(b, n, INNER)
            return out @ Wo

        def ffn_layer(x, g, bln, W1, b1, W2, b2):
            mu = x.mean(-1, keepdims=True)
            var = ((x - mu) ** 2).mean(-1, keepdims=True)
            xn = (x - mu) / jnp.sqrt(var + 1e-05) * g + bln
            hg = xn @ W1 + b1
            a, gate = jnp.split(hg, 2, -1)
            return a * jax.nn.gelu(gate, approximate=False) @ W2 + b2
        for i in range(DEPTH):
            x = attn_layer(shift_tokens(x), Wqkv[i], q_scale[i], k_scale[i], Wo[i]) + x
            x = ffn_layer(shift_tokens(x), ln_g[i], ln_b[i], W1[i], b1[i], W2[i], b2[i]) + x
        return x
    x = L0_attn_a_x
    x = x + _L0_attn_a_ref(_layernorm(x, axis=-1), L0_attn_a_w_qkv, L0_attn_a_w_out)
    x = x + _L0_ffn_ref(_layernorm(x, axis=-1), L0_ffn_Wqkv, L0_ffn_q_scale, L0_ffn_k_scale, L0_ffn_Wo, L0_ffn_ln_g, L0_ffn_ln_b, L0_ffn_W1, L0_ffn_b1, L0_ffn_W2, L0_ffn_b2)
    x = x + _L0_attn_b_ref(_layernorm(x, axis=-1), L0_attn_b_ln_scale, L0_attn_b_ln_bias, L0_attn_b_Wq, L0_attn_b_Wkv, L0_attn_b_qn_scale, L0_attn_b_qn_bias, L0_attn_b_kn_scale, L0_attn_b_kn_bias, L0_attn_b_Wout)
    x = x + _L0_ffn_ref(_layernorm(x, axis=-1), L0_ffn_Wqkv, L0_ffn_q_scale, L0_ffn_k_scale, L0_ffn_Wo, L0_ffn_ln_g, L0_ffn_ln_b, L0_ffn_W1, L0_ffn_b1, L0_ffn_W2, L0_ffn_b2)
    return x

_drawn_inputs = setup_inputs


def setup_inputs(seed=0):
    import zlib

    import numpy as np

    out = dict(_drawn_inputs(seed))
    spreads = {'L0_attn_b_ln_scale': (1.0, 0.6),
     'L0_attn_b_ln_bias': (0.0, 0.1),
     'L0_attn_b_qn_scale': (1.0, 0.6),
     'L0_attn_b_qn_bias': (0.0, 0.8),
     'L0_attn_b_kn_scale': (1.0, 0.6),
     'L0_attn_b_kn_bias': (0.0, 0.8),
     'L0_ffn_q_scale': (1.0, 0.6),
     'L0_ffn_k_scale': (1.0, 0.6),
     'L0_ffn_ln_g': (1.0, 0.6),
     'L0_ffn_ln_b': (0.0, 0.8),
     'L0_ffn_b1': (0.0, 0.576),
     'L0_ffn_b2': (0.0, 0.1)}
    factors = {}
    for name, (base, spread) in spreads.items():
        noise = np.random.default_rng([zlib.crc32(name.encode()), seed]).standard_normal(out[name].shape)
        drawn = base * np.exp(spread * noise) if base else spread * noise
        out[name] = jnp.asarray(drawn.astype(out[name].dtype))
    for name, factor in factors.items():
        out[name] = (out[name] * factor).astype(out[name].dtype)
    return out
```

```python
from contextlib import ExitStack

import numpy as np

import concourse.bass as bass
from concourse import mybir

F32 = mybir.dt.float32
F32R = mybir.dt.float32r
BF16 = mybir.dt.bfloat16
ALU = mybir.AluOpType
ACT = mybir.ActivationFunctionType
AX = mybir.AxisListType

S = 2048
D = 128
NCH = S // 128
NB = S // 512
DEPTH = 6
H, DH = 16, 64
WIN = 32
INNER = H * DH
DFF = 341
FT = [(0, 128), (128, 128), (256, DFF - 256)]
AH = 8
START = 1
NEG = -1.0e30


def shape_constants():
    f = np.float32
    parts = {}
    parts["ident"] = np.eye(128, dtype=f)
    parts["mean128"] = np.full((128, 128), 1.0 / 128, f)
    i = np.arange(128)
    parts["mask_qk"] = np.where(i[None, :] <= i[:, None], 0, NEG).astype(f)
    parts["mask_kq"] = np.where(i[:, None] <= i[None, :], 0, NEG).astype(f)
    q = (i % WIN)[:, None]
    m = np.arange(2 * WIN)[None, :]
    ok = np.where(m < WIN, q <= m, m - WIN <= q)
    win = np.repeat(np.where(ok, 0, NEG)[:, None, :], 2, 1)
    win[:WIN, 0, :WIN] = NEG
    parts["mask_win"] = win.reshape(128, 2 * 2 * WIN).astype(f)
    half = np.arange(0, DH, 2, dtype=f)
    inv_freq = (f(1.0) / np.power(f(10000.0), half / f(DH))).astype(f)
    t = np.arange(S, dtype=f)
    ang = (t[:, None] * inv_freq[None, :]).astype(f)
    ang = np.concatenate([ang, ang], -1).astype(np.float64)
    base = (half.astype(np.float64) + 0.4 * DH) / (1.4 * DH)
    base = np.concatenate([base, base])
    power = (np.arange(S) % 128) / (WIN // 2)
    scale = base[None, :] ** power[:, None]
    sign = np.where(np.arange(DH) < DH // 2, -1.0, 1.0)

    def chunked(a):
        return a.reshape(NCH, 128, DH).transpose(1, 0, 2).reshape(128, NCH * DH).astype(f)

    parts["rot_q_cos"] = chunked(np.cos(ang) * scale * 8.0)
    parts["rot_q_sin"] = chunked(np.sin(ang) * scale * 8.0 * sign)
    parts["rot_k_cos"] = chunked(np.cos(ang) / scale)
    parts["rot_k_sin"] = chunked(np.sin(ang) / scale * sign)
    parts["cross"] = np.tile(base ** 8.0, 2).reshape(128, 1).astype(f)
    r = i % 32
    hi_q, lo_q = (r < 8) | ((r >= 16) & (r < 24)), (r >= 8) & (r < 16)
    hi_k, lo_k = r < 16, (r >= 16) & (r < 24)
    cols = [hi_q * 1.0 - lo_q, lo_q * 1.0, hi_k * 1.0 - lo_k, lo_k * 1.0,
            ((r == 24) | (r == 25)) * 1.0,
            np.where(i < 64, 1.0, -1.0), np.where(i < 64, 0.0, 1.0)]
    parts["rows"] = np.stack(cols, 1).astype(f)
    parts["sum_rows"] = ((i[:, None] // 32 == i[None, :] // 32) & (i[:, None] % 32 == 8)).astype(f)
    at, place = 0, {}
    for name, a in parts.items():
        place[name] = (at, a.shape[1])
        at += a.shape[1]
    return np.concatenate(list(parts.values()), 1), place


def build(nc, A, out, place, stages=("A", "S0", "B", "S1")):
    n_const = A["shape_constants"].shape[1]
    ctx = ExitStack()
    with ctx:
        def sem(name):
            return ctx.enter_context(nc.semaphore(name))

        def sb(name, shape, dt=F32, at=ctx):
            return at.enter_context(nc.sbuf_tensor(name, shape, dt))

        consts = sb("consts", [128, n_const])

        def const(name):
            a, n = place[name]
            return consts[:, a:a + n]

        ident = const("ident")
        ident_b = sb("ident_b", [128, 128], BF16)
        mask_qk = sb("mask_qk", [128, 128], BF16)
        mask_kq = sb("mask_kq", [128, 128], BF16)
        mask_win = sb("mask_win", [128, 2, 2 * WIN], BF16)
        minus_half = sb("minus_half", [128, H])
        ones = sb("ones", [128, 128])
        XM = sb("XM", [128, S])
        XA = sb("XA", [128, S + 1])
        XB = sb("XB", [128, S + 1])
        centred = sb("centred", [128, S])
        normed = sb("normed", [128, S])
        squares = sb("squares", [128, S])
        variance = sb("variance", [128, NCH])
        rstd = sb("rstd", [128, NCH])
        diag = sb("diag", [128, 2, 512])
        slot = [ctx.enter_context(nc.psum_tensor(f"slot{i}", [128, 1024], F32)) for i in range(4)]

        rows_dram = nc.dram_tensor("rows_dram", (2, 64, 128), F32).ap()

        mem = ExitStack()
        x_nat = sb("x_nat", [128, NCH, D], F32, mem)
        wqkv_nat = sb("wqkv_nat", [128, 3, D], F32, mem)
        wout_nat = sb("wout_nat", [128, D], F32, mem)
        wq_rows = sb("wq_rows", [128, 16, 32], F32, mem)
        wk_rows = sb("wk_rows", [128, 16, 32], F32, mem)
        wv_cols = sb("wv_cols", [128, D], F32, mem)
        wout_pad = sb("wout_pad", [128, 16, 32], F32, mem)
        wout_rows = sb("wout_rows", [128, 4, D], F32, mem)
        gq_w = sb("gq_w", [128, D], F32, mem)
        gk_w = sb("gk_w", [128, D], F32, mem)
        gv_w = sb("gv_w", [128, 32], F32, mem)
        go_w = sb("go_w", [128, D], F32, mem)
        rounded = sb("rounded", [128, 2, 1024], F32R, mem)
        scaled = sb("scaled", [128, 2, 1024], F32, mem)
        QT = sb("QT", [128, S], F32R, mem)
        KT = sb("KT", [128, S], F32R, mem)
        V4 = sb("V4", [128, NCH, 4, 32], F32, mem)
        part_max = sb("part_max", [128, 64, 2], F32, mem)
        neg_max = sb("neg_max", [128, 128], F32, mem)
        neg_hi = sb("neg_hi", [64, 128], F32R, mem)
        neg_lo = sb("neg_lo", [64, 128], F32R, mem)
        Pa = sb("Pa", [128, 4, 1024], F32, mem)
        Oa = sb("Oa", [128, 512], F32, mem)
        sum_inv = sb("sum_inv", [128, 512], F32, mem)
        On = sb("On", [128, 512], F32, mem)
        out_nat = sb("out_nat", [128, NCH, D], F32, mem)
        mem.close()

        mem = ExitStack()
        b_wq = sb("b_wq", [128, INNER], F32, mem)
        b_wkv = sb("b_wkv", [128, 512], F32, mem)
        b_wout = sb("b_wout", [128, 8, D], F32, mem)
        b_cols = sb("b_cols", [128, 6], F32, mem)
        b_w = sb("b_w", [128, 3, 128], F32, mem)
        b_wo = sb("b_wo", [128, D], F32, mem)
        z2 = sb("z2", [128, S], F32, mem)
        b_round = sb("b_round", [128, S], F32R, mem)
        b_part = sb("b_part", [128, S], F32, mem)
        QA = [sb(f"QA{i}", [128, S], F32R, mem) for i in range(2)]
        QB = [sb(f"QB{i}", [66, S], F32R, mem) for i in range(2)]
        KA = sb("KA", [128, S], F32R, mem)
        KB = sb("KB", [66, S], F32R, mem)
        Vb = sb("Vb", [128, NCH, 64], F32, mem)
        ones32 = sb("ones32", [128, 32], F32, mem)
        b_pmax = sb("b_pmax", [128, 32, 2], F32, mem)
        b_nmax = sb("b_nmax", [128, 128], F32, mem)
        b_hi = sb("b_hi", [32, 128], F32R, mem)
        b_lo = sb("b_lo", [32, 128], F32R, mem)
        Pb = sb("Pb", [128, 3, 1024], F32, mem)
        Oc = sb("Oc", [128, 1024], F32, mem)
        b_inv = sb("b_inv", [128, 512], F32, mem)
        Ob = sb("Ob", [128, 512], F32, mem)
        mem.close()

        mem = ExitStack()
        Wqkv = sb("Wqkv", [128, 3 * INNER], F32, mem)
        Wo = sb("Wo", [128, 8, D], F32, mem)
        W1 = sb("W1", [128, 2 * DFF], F32, mem)
        W2 = sb("W2", [128, 3, D], F32, mem)
        b1 = sb("b1", [128, 2, 3], F32, mem)
        ffn_cols = sb("ffn_cols", [128, 3], F32, mem)
        qk_scales = sb("qk_scales", [128, 4, DH], F32, mem)
        rot = [sb(f"rot{i}", [128, NCH * DH], F32, mem) for i in range(4)]
        xc = [sb(f"xc{i}", [128, 128], F32, mem) for i in range(2)]
        raw = [sb(f"raw{i}", [128, INNER], F32, mem) for i in range(2)]
        sq = [sb(f"sq{i}", [128, INNER], F32, mem) for i in range(2)]
        rot_out = [sb(f"rot_out{i}", [128, INNER], F32, mem) for i in range(2)]
        rot_sin = [sb(f"rot_sin{i}", [128, INNER], F32, mem) for i in range(2)]
        norm2 = [sb(f"norm2_{i}", [128, H], F32, mem) for i in range(2)]
        norm2c = [sb(f"norm2c_{i}", [128, H], F32, mem) for i in range(2)]
        inv_norm = [sb(f"inv_norm{i}", [128, H], F32, mem) for i in range(2)]
        qT = sb("qT", [128, 8, 128], F32, mem)
        kT = sb("kT", [128, 8, 160], F32, mem)
        V = [sb(f"V{i}", [128, INNER], F32, mem) for i in range(2)]
        Vs = [sb(f"Vs{i}", [128, INNER], F32, mem) for i in range(2)]
        row_max = sb("row_max", [128, H], F32, mem)
        row_sum = sb("row_sum", [128, H], F32, mem)
        row_inv = sb("row_inv", [128, H], F32, mem)
        probs = sb("probs", [128, INNER], F32, mem)
        probsT = sb("probsT", [128, H, 2, WIN], F32, mem)
        Os = sb("Os", [128, INNER], F32, mem)
        OT = sb("OT", [128, 8, 128], F32, mem)
        gate = sb("gate", [128, 3, 512], F32, mem)
        hidden = sb("hidden", [128, 3, 512], F32, mem)
        mem.close()

        names = ("consts_in x_in wa_in setup_pool setup_dve setup_act xm_done "
                 "ln_mean ln_centred ln_square ln_var ln_eps ln_pow ln_diag ln_bc ln_half ln_done "
                 "wqkv_in scales_in wo_in ffn_in tables_done xc_done "
                 "q_mm k_mm v_mm tq_mm tk_mm s_mm ot_mm y_mm pv_mm "
                 "q_evac k_evac qT_sb kT_cross kT_sb v_sb probs_exp ot_sb vs_in "
                 "nq_done nk_done aq_done ak_done bq_done bk_done cq_done ck_done iq_done ik_done "
                 "rq_done rk_done qn_done kn_done max_done sub_done pt_done sum_done inv_done on_done xb_done "
                 "w1_mm gelu_done hid_done w2_mm f_done stack_in stack_out "
                 "tr_x tr_wo wa_rows a_w a_qk a_round a_scaled a_split a_v a_vsb a_s1 a_max a_comb a_neg a_nt "
                 "a_hi a_lo a_dma a_s a_exp a_pv a_osb a_bc a_inv a_on a_y a_yadd "
                 "wb_in b_w_done b_mm b_ln b_rnd b_prt b_split b_v b_vsb b_s1 b_max b_comb b_neg b_nt b_his b_los b_dma b_s a_rows b_rows passed "
                 "b_exp b_pv b_invd b_on b_y b_yadd b_qb b_ones tr_out out_sb out_done self_act").split()
        s = {n: sem(n) for n in names}

        LN_A, LN_S0 = 0, int("A" in stages)
        LN_B = LN_S0 + (1 + DEPTH) * ("S0" in stages)
        LN_S1 = LN_B + 2 + 4 * 5
        block = ctx.enter_context(nc.Block())

        def pe_norm(pe, idx, src, ready):
            n = idx * NB
            for b in range(NB):
                ready(b)
                pe.matmul(slot[b][:, 0:512], const("mean128"), src(b), start=True, stop=True)\
                  .then_inc(s["ln_mean"], 1)
            for b in range(NB):
                pe.wait_ge(s["ln_square"], START + n + b + 1)
                for c in range(4 * b, 4 * b + 4):
                    mm = pe.matmul(slot[0][:, 512 + c:513 + c], squares[:, c * 128:c * 128 + 128],
                                   const("mean128")[:, 0:1], start=True, stop=True)
            mm.then_inc(s["ln_var"], 1)
            for b in range(NB):
                pe.wait_ge(s["ln_diag"], START + n + b + 1)
                pe.matmul(slot[b][:, 512:1024], ones[:, :], diag[:, b % 2, :], start=True, stop=True)\
                  .then_inc(s["ln_bc"], 1)

        def act_norm(act, idx):
            n = idx * NB
            act.wait_ge(s["ln_var"], START + idx)
            for b in range(NB):
                act.wait_ge(s["ln_centred"], START + n + b + 1)
                act.activation(squares[:, b * 512:b * 512 + 512], centred[:, b * 512:b * 512 + 512], ACT.Square)\
                   .then_inc(s["ln_square"], 1)

        def pool_norm(pool, idx):
            pool.wait_ge(s["ln_eps"], START + idx + 1)
            pool.wait_ge(s["ln_diag"], START + idx * NB)
            pool.tensor_tensor(rstd[:, :], variance[:, :], minus_half[:, :], ALU.pow).then_inc(s["ln_pow"], 1)

        def dve_norm(dve, idx, src, eps, finish):
            n = idx * NB
            for b in range(NB):
                dve.wait_ge(s["ln_mean"], START + n + b + 1)
                dve.tensor_tensor(centred[:, b * 512:b * 512 + 512], src(b), slot[b][:, 0:512], ALU.subtract)\
                   .then_inc(s["ln_centred"], 1)
            dve.wait_ge(s["ln_var"], START + idx + 1)
            dve.tensor_scalar(variance[:, :], slot[0][:, 512:512 + NCH], eps, None, ALU.add).then_inc(s["ln_eps"], 1)

            def spread(b):
                dve.wait_ge(s["ln_pow"], START + idx + 1)
                dve.wait_ge(s["ln_bc"], START + n + max(b - 1, 0))
                dve.tensor_tensor(diag[:, b % 2, :].rearrange("p (c t) -> p c t", c=4),
                                  ident.unsqueeze(1).to_broadcast([128, 4, 128]),
                                  rstd[:, 4 * b:4 * b + 4].unsqueeze(2).to_broadcast([128, 4, 128]), ALU.mult)\
                   .then_inc(s["ln_diag"], 1)
            spread(0)
            for b in range(NB):
                if b + 1 < NB:
                    spread(b + 1)
                dve.wait_ge(s["ln_bc"], START + n + b + 1)
                finish(b, centred[:, b * 512:b * 512 + 512], slot[b][:, 512:1024])

        def dve_affine(dve, idx, dst, g, bias):
            def finish(b, c, r):
                cols = slice(b * 512, b * 512 + 512)
                dve.tensor_tensor(dst[:, cols], c, r, ALU.mult).then_inc(s["ln_half"], 1)
                dve.wait_ge(s["ln_half"], START + idx * NB + b + 1)
                dve.tensor_scalar(dst[:, cols], dst[:, cols], g, bias, ALU.mult, ALU.add)\
                   .then_inc(s["ln_done"], 1)
            return finish

        def dve_plain(dve, idx, dst):
            def finish(b, c, r):
                dve.tensor_tensor(dst[:, b * 512:b * 512 + 512], c, r, ALU.mult).then_inc(s["ln_half"], 1)
                dve.wait_ge(s["ln_half"], START + idx * NB + b + 1)
                dve.sem_inc(s["ln_done"], 1)
            return finish

        def steps(eng, lam, body):
            g0 = lam * NCH
            body(g0, 0, 0, True, False, False)
            body(g0 + 1, 1, 1, True, True, False)
            with eng.Fori(0, NCH // 2 - 1) as half:
                c = half * 2 + 2
                body(g0 + c, c, 0, True, True, True)
                body(g0 + c + 1, c + 1, 1, True, True, True)
            body(g0 + NCH, NCH, 0, False, True, True)
            body(g0 + NCH + 1, NCH + 1, 1, False, False, True)

        def sp_stack(sp, call):
            with sp.Fori(0, DEPTH) as L:
                lam = L + DEPTH * call
                sp.wait_ge(s["v_mm"], START + lam * NCH)
                for i in range(3):
                    sp.dma_start(Wqkv[:, i * INNER:(i + 1) * INNER],
                                 A["Wqkv"][bass.ds(L, 1), :, i * INNER:(i + 1) * INNER]
                                 .rearrange("a p n -> p (a n)")).then_inc(s["wqkv_in"], 16)
                sp.wait_ge(s["tables_done"], START + lam * 4)
                for i, name in enumerate(("q_scale", "k_scale")):
                    row = A[name][bass.ds(L, 1), :].rearrange("a n -> (a n)")
                    sp.dma_start(qk_scales[:, 2 * i, :], row.partition_broadcast(128)).then_inc(s["scales_in"], 16)
                    sp.dma_start(qk_scales[:, 2 * i + 1, 0:32], row[32:64].partition_broadcast(128))\
                      .then_inc(s["scales_in"], 16)
                    sp.dma_start(qk_scales[:, 2 * i + 1, 32:64], row[0:32].partition_broadcast(128))\
                      .then_inc(s["scales_in"], 16)
                sp.wait_ge(s["y_mm"], START + lam * NCH)
                sp.dma_start(Wo[:, :, :], A["Wo"][bass.ds(L, 1), :, :].rearrange("a (j p) n -> p (a j) n", p=128))\
                  .then_inc(s["wo_in"], 16)
                sp.wait_ge(s["f_done"], START + lam * NB * 2)
                sp.dma_start(W1[:, :], A["W1"][bass.ds(L, 1), :, :].rearrange("a p n -> p (a n)"))\
                  .then_inc(s["ffn_in"], 16)
                for j, (a, n) in enumerate(FT):
                    sp.dma_start(W2[0:n, j, :], A["W2"][bass.ds(L, 1), a:a + n, :].rearrange("a p n -> p (a n)"))\
                      .then_inc(s["ffn_in"], 16)
                    for i in range(2):
                        sp.dma_start(b1[0:n, i, j:j + 1], A["b1"][bass.ds(L, 1), i * DFF + a:i * DFF + a + n]
                                     .rearrange("a p -> p a")).then_inc(s["ffn_in"], 16)
                for j, name in enumerate(("ln_g", "ln_b", "b2")):
                    sp.dma_start(ffn_cols[:, j:j + 1], A[name][bass.ds(L, 1), :].rearrange("a p -> p a"))\
                      .then_inc(s["ffn_in"], 16)

                def shift_values(g, c, par, front, mid, back):
                    if not front:
                        return
                    sp.wait_ge(s["v_sb"], START + g + 1)
                    sp.sem_inc(s["passed"], 1)
                    sp.wait_ge(s["pv_mm"], START + (g - 1 if back else lam * NCH))
                    sp.dma_start(Vs[par][32:128, :], V[par][0:96, :]).then_inc(s["vs_in"], 16)
                    sp.dma_start(Vs[par][0:32, :], V[1 - par][96:128, :]).then_inc(s["vs_in"], 16)
                steps(sp, lam, shift_values)

        def pe_stack(pe, call):
            n0 = LN_S0 if call == 0 else LN_S1
            with pe.Fori(0, DEPTH) as L:
                lam = L + DEPTH * call
                pe.wait_ge(s["wqkv_in"], START + (lam + 1) * 48)

                def step(g, c, par, front, mid, back):
                    if front:
                        pe.wait_ge(s["xc_done"], START + g + 1)
                        pe.wait_ge(s["v_sb"], START + g)
                        for i in range(2):
                            mm = pe.matmul(slot[0][:, i * 512:(i + 1) * 512], xc[par][:, :],
                                           Wqkv[:, i * 512:(i + 1) * 512], start=True, stop=True)
                        mm.then_inc(s["q_mm"], 1)
                    if mid:
                        pe.wait_ge(s["qn_done"], START + g)
                        pe.wait_ge(s["sub_done"], START + g - 1)
                        for j in range(8):
                            mm = pe.transpose(slot[2][:, j * 128:(j + 1) * 128],
                                              rot_out[0][:, j * 128:(j + 1) * 128], ident)
                        mm.then_inc(s["tq_mm"], 1)
                        pe.wait_ge(s["kn_done"], START + g)
                        pe.wait_ge(s["on_done"], START + g - 1)
                        for j in range(8):
                            mm = pe.transpose(slot[3][:, j * 128:(j + 1) * 128],
                                              rot_out[1][:, j * 128:(j + 1) * 128], ident)
                        mm.then_inc(s["tk_mm"], 1)
                    if front:
                        pe.wait_ge(s["k_evac"], START + g)
                        for i in range(2):
                            mm = pe.matmul(slot[1][:, i * 512:(i + 1) * 512], xc[par][:, :],
                                           Wqkv[:, INNER + i * 512:INNER + (i + 1) * 512], start=True, stop=True)
                        mm.then_inc(s["k_mm"], 1)
                    if mid:
                        pe.wait_ge(s["qT_sb"], START + g)
                        pe.wait_ge(s["kT_sb"], START + g)
                        first = 0 if isinstance(c, int) and c == 1 else 1
                        for i in range(2):
                            pe.matmul(slot[2][:, i * 512:(i + 1) * 512], ident_b[:, :],
                                      mask_win[:, first:first + 1, :].to_broadcast([128, 8, 2 * WIN]),
                                      start=True, stop=False, skip_group_check=True)
                        for h in range(H):
                            r = 64 * (h % 2)
                            for w in range(4):
                                at = (h % 2) * 512 + (h // 2) * 64
                                mm = pe.matmul(slot[2][32 * w:32 * w + 32, at:at + 64],
                                               qT[r:r + 64, h // 2, 32 * w:32 * w + 32],
                                               kT[r:r + 64, h // 2, 32 * w:32 * w + 64],
                                               start=False, stop=True, skip_group_check=True)
                        mm.then_inc(s["s_mm"], 1)
                    if back:
                        pe.wait_ge(s["on_done"], START + g - 1)
                        for j in range(8):
                            mm = pe.transpose(slot[3][:, j * 128:(j + 1) * 128],
                                              Os[:, j * 128:(j + 1) * 128], ident)
                        mm.then_inc(s["ot_mm"], 1)
                    if front:
                        pe.wait_ge(s["q_evac"], START + g + 1)
                        for i in range(2):
                            mm = pe.matmul(slot[0][:, i * 512:(i + 1) * 512], xc[par][:, :],
                                           Wqkv[:, 2 * INNER + i * 512:2 * INNER + (i + 1) * 512],
                                           start=True, stop=True)
                        mm.then_inc(s["v_mm"], 1)
                    if back:
                        pe.wait_ge(s["wo_in"], START + (lam + 1) * 16)
                        pe.wait_ge(s["ot_sb"], START + g - 1)
                        for j in range(8):
                            mm = pe.matmul(slot[3][:, 0:128], Wo[:, j, :], OT[:, j, :], start=(j == 0), stop=(j == 7))
                        mm.then_inc(s["y_mm"], 1)
                    if mid:
                        pe.wait_ge(s["pt_done"], START + g)
                        pe.wait_ge(s["v_sb"], START + g)
                        pe.wait_ge(s["vs_in"], START + 32 * g)
                        if back:
                            pe.wait_ge(s["xb_done"], START + 2 * (g - 1))
                        pe.sem_inc(s["passed"], 1)
                        for h in range(H):
                            for kb, vals in ((0, Vs[1 - par]), (1, V[1 - par])):
                                for w in range(4):
                                    r = slice(32 * w, 32 * w + 32)
                                    mm = pe.matmul(slot[3][r, h * 64:h * 64 + 64], probsT[r, (h % 2) * 8 + h // 2, kb, :],
                                                   vals[r, h * 64:h * 64 + 64], start=(kb == 0), stop=(kb == 1),
                                                   skip_group_check=True)
                        mm.then_inc(s["pv_mm"], 1)
                steps(pe, lam, step)

                idx = n0 + 1 + L
                n = idx * NB
                pe.wait_ge(s["k_evac"], START + (lam + 1) * NCH)
                pe.wait_ge(s["sub_done"], START + (lam + 1) * NCH)
                pe_norm(pe, idx, lambda b: XB[:, b * 512:b * 512 + 512],
                        lambda b: pe.wait_ge(s["xb_done"], START + 2 * (lam * NCH) + 2 * NCH))
                pe.wait_ge(s["ffn_in"], START + (lam + 1) * 16 * 13)
                for b in range(NB):
                    pe.wait_ge(s["ln_done"], START + n + b + 1)
                    f = lam * NB + b
                    for j, (a, m) in enumerate(FT):
                        if b == 0:
                            pe.wait_ge(s["ln_done"], START + n + j + 2)
                        if b >= 1:
                            pe.wait_ge(s["hid_done"], START + (f - 1) * 3 + j + 1)
                            if j == 0:
                                pe.wait_ge(s["f_done"], START + 2 * f)
                        for i in range(2):
                            mm = pe.matmul(slot[j + 1][0:m, i * 512:(i + 1) * 512],
                                           W1[:, i * DFF + a:i * DFF + a + m], normed[:, b * 512:b * 512 + 512],
                                           start=True, stop=True)
                        mm.then_inc(s["w1_mm"], 1)
                    for j, (a, m) in enumerate(FT):
                        pe.wait_ge(s["hid_done"], START + f * 3 + j + 1)
                        mm = pe.matmul(slot[1][:, 0:512], W2[0:m, j, :], hidden[0:m, j, :],
                                       start=(j == 0), stop=(j == 2))
                    mm.then_inc(s["w2_mm"], 1)

        def act_stack(act, call):
            n0 = LN_S0 if call == 0 else LN_S1
            with act.Fori(0, DEPTH) as L:
                lam = L + DEPTH * call

                def raw_and_squares(i, g, mm, used):
                    act.wait_ge(s[mm], START + g + 1)
                    for u in used:
                        act.wait_ge(s[u], START + g)
                    act.activation(raw[i][:, :], slot[i][:, :], ACT.Copy)
                    act.activation(sq[i][:, :], slot[i][:, :], ACT.Square).then_inc(s[("q_evac", "k_evac")[i]], 1)

                def step(g, c, par, front, mid, back):
                    if front:
                        raw_and_squares(0, g, "q_mm", ("aq_done", "bq_done", "nq_done"))
                    if mid:
                        act.wait_ge(s["tq_mm"], START + g)
                        act.wait_ge(s["s_mm"], START + g - 1)
                        act.activation(qT[:, :, :].rearrange("p j t -> p (j t)"), slot[2][:, :], ACT.Copy)\
                           .then_inc(s["qT_sb"], 1)
                        act.wait_ge(s["kT_sb"], START + g - 1)
                        act.activation(kT[:, :, 0:32], kT[:, :, 128:160], ACT.Copy, scale=const("cross"))\
                           .then_inc(s["kT_cross"], 1)
                        act.wait_ge(s["tk_mm"], START + g)
                        act.wait_ge(s["kT_cross"], START + g)
                        act.activation(kT[:, :, 32:160], slot[3][:, :].rearrange("p (j t) -> p j t", j=8), ACT.Copy)\
                           .then_inc(s["kT_sb"], 1)
                    if front:
                        raw_and_squares(1, g, "k_mm", ("ak_done", "bk_done", "nk_done"))
                    if back:
                        act.wait_ge(s["ot_mm"], START + g - 1)
                        act.wait_ge(s["y_mm"], START + g - 2)
                        act.activation(OT[:, :, :].rearrange("p j t -> p (j t)"), slot[3][:, :], ACT.Copy)\
                           .then_inc(s["ot_sb"], 1)
                    if mid:
                        act.wait_ge(s["sub_done"], START + g)
                        act.activation(probs[:, :], probs[:, :], ACT.Exp).then_inc(s["probs_exp"], 1)
                    if front:
                        act.wait_ge(s["v_mm"], START + g + 1)
                        if back:
                            act.wait_ge(s["pv_mm"], START + g - 1)
                        act.wait_ge(s["vs_in"], START + 32 * g)
                        act.activation(V[par][:, :], slot[0][:, :], ACT.Copy).then_inc(s["v_sb"], 1)
                steps(act, lam, step)

                act_norm(act, n0 + 1 + L)
                act.wait_ge(s["ffn_in"], START + (lam + 1) * 16 * 13)
                for b in range(NB):
                    f = lam * NB + b
                    for j, (a, m) in enumerate(FT):
                        act.wait_ge(s["w1_mm"], START + f * 3 + j + 1)
                        if b >= 1:
                            act.wait_ge(s["hid_done"], START + (f - 1) * 3 + j + 1)
                        act.activation(gate[0:m, j, :], slot[j + 1][0:m, 512:1024], ACT.Gelu,
                                       bias=b1[0:m, 1, j:j + 1]).then_inc(s["gelu_done"], 1)

        def pool_stack(pool, call):
            n0 = LN_S0 if call == 0 else LN_S1
            with pool.Fori(0, DEPTH) as L:
                lam = L + DEPTH * call
                pool.wait_ge(s["tables_done"], START + 4 * (lam + 1))

                def rotate(i, g, c, evac, n_done, a_done, b_done, i_done, r_done, inv_used):
                    pool.wait_ge(s[evac], START + g + 1)
                    src = raw[i][:, :].rearrange("p (h x d) -> p h x d", h=H, x=2)
                    dst = rot_sin[i][:, :].rearrange("p (h x d) -> p h x d", h=H, x=2)
                    for x in range(2):
                        tab = rot[2 * i + 1][:, bass.ds(c * DH + 32 * x, 32)].unsqueeze(1).to_broadcast([128, H, 32])
                        ins = pool.tensor_tensor(dst[:, :, x, :], src[:, :, 1 - x, :], tab, ALU.mult)
                    ins.then_inc(s[b_done], 1)
                    pool.wait_ge(s[n_done], START + g + 1)
                    pool.wait_ge(s[inv_used], START + g)
                    pool.tensor_tensor(inv_norm[i][:, :], norm2c[i][:, :], minus_half[:, 0:H], ALU.pow)\
                        .then_inc(s[i_done], 1)
                    pool.wait_ge(s[a_done], START + g + 1)
                    pool.wait_ge(s[b_done], START + g + 1)
                    pool.tensor_tensor(rot_out[i][:, :], rot_out[i][:, :], rot_sin[i][:, :], ALU.add)\
                        .then_inc(s[r_done], 1)

                def step(g, c, par, front, mid, back):
                    if front:
                        rotate(0, g, c, "q_evac", "nq_done", "aq_done", "bq_done", "iq_done",
                               "rq_done", "qn_done")
                        rotate(1, g, c, "k_evac", "nk_done", "ak_done", "bk_done", "ik_done",
                               "rk_done", "kn_done")
                steps(pool, lam, step)
                pool_norm(pool, n0 + 1 + L)

        def dve_stack(dve, call):
            n0 = LN_S0 if call == 0 else LN_S1
            with dve.Fori(0, DEPTH) as L:
                lam = L + DEPTH * call

                def take_chunk(c, par):
                    dve.tensor_copy(xc[par][:, :], XA[:, bass.ds(c * 128, 128)]).then_inc(s["xc_done"], 1)
                dve.wait_ge(s["stack_in"], START + NB * (call + 1) * 2)
                dve.wait_ge(s["f_done"], START + 2 * NB * lam)
                take_chunk(0, 0)
                dve.wait_ge(s["scales_in"], START + (lam + 1) * 96)
                dve.wait_ge(s["bk_done"], START + lam * NCH)
                for i, name in enumerate(("rot_q_cos", "rot_q_sin", "rot_k_cos", "rot_k_sin")):
                    dve.tensor_tensor(rot[i][:, :].rearrange("p (c d) -> p c d", d=DH),
                                      const(name).rearrange("p (c d) -> p c d", d=DH),
                                      qk_scales[:, i:i + 1, :].to_broadcast([128, NCH, DH]), ALU.mult)\
                       .then_inc(s["tables_done"], 1)
                dve.wait_ge(s["tables_done"], START + 4 * (lam + 1))

                def cos_half(i, g, c, evac, sum_of, n_done, a_done, t_mm, i_done):
                    dve.wait_ge(s[evac], START + g + 1)
                    dve.wait_ge(s[i_done], START + g)
                    dve.tensor_reduce(norm2[i][:, :], sq[i][:, :].rearrange("p (h d) -> p h d", h=H), AX.X, ALU.add)\
                       .then_inc(s[sum_of], 1)
                    dve.wait_ge(s[t_mm], START + g)
                    tab = rot[2 * i][:, bass.ds(c * DH, DH)].unsqueeze(1).to_broadcast([128, H, DH])
                    dve.tensor_tensor(rot_out[i][:, :].rearrange("p (h d) -> p h d", h=H),
                                      raw[i][:, :].rearrange("p (h d) -> p h d", h=H), tab, ALU.mult)\
                       .then_inc(s[a_done], 1)
                    dve.wait_ge(s[sum_of], START + g + 1)
                    dve.tensor_scalar(norm2c[i][:, :], norm2[i][:, :], 1e-24, None, ALU.max)\
                       .then_inc(s[n_done], 1)

                def normalise(i, g, r_done, i_done, done):
                    dve.wait_ge(s[r_done], START + g + 1)
                    dve.wait_ge(s[i_done], START + g + 1)
                    v = rot_out[i][:, :].rearrange("p (h d) -> p h d", h=H)
                    dve.tensor_tensor(v, v, inv_norm[i][:, :].unsqueeze(2).to_broadcast([128, H, DH]), ALU.mult)\
                       .then_inc(s[done], 1)

                def step(g, c, par, front, mid, back):
                    p3 = probs[:, :].rearrange("p (h k) -> p h k", h=H)
                    if front and mid:
                        dve.wait_ge(s["v_mm"], START + g - 1)
                        take_chunk(c, par)
                    if back:
                        dve.wait_ge(s["pv_mm"], START + g - 1)
                        dve.wait_ge(s["inv_done"], START + g - 1)
                        dve.wait_ge(s["ot_mm"], START + g - 2)
                        inv = row_inv[:, :].rearrange("p (x j) -> p j x", x=2)
                        dve.tensor_tensor(Os[:, :].rearrange("p (j x d) -> p j x d", x=2, d=DH),
                                          slot[3][:, :].rearrange("p (j x d) -> p j x d", x=2, d=DH),
                                          inv.unsqueeze(3).to_broadcast([128, 8, 2, DH]), ALU.mult)\
                           .then_inc(s["on_done"], 1)
                    if front:
                        cos_half(0, g, c, "q_evac", "cq_done", "nq_done", "aq_done", "tq_mm", "iq_done")
                        cos_half(1, g, c, "k_evac", "ck_done", "nk_done", "ak_done", "tk_mm", "ik_done")
                    if mid:
                        dve.wait_ge(s["s_mm"], START + g)
                        s3 = slot[2][:, :].rearrange("p (h k) -> p h k", h=H)
                        dve.tensor_reduce(row_max[:, :], s3, AX.X, ALU.max).then_inc(s["max_done"], 1)
                        dve.wait_ge(s["max_done"], START + g)
                        dve.tensor_tensor(p3, s3, row_max[:, :].unsqueeze(2).to_broadcast([128, H, 64]), ALU.subtract)\
                           .then_inc(s["sub_done"], 1)
                        dve.wait_ge(s["probs_exp"], START + g)
                        dve.transpose(probsT[:, :, :, :].rearrange("p h k q -> p (h k q)"), probs[:, :])\
                           .then_inc(s["pt_done"], 1)
                    if back:
                        dve.wait_ge(s["y_mm"], START + g - 1)
                        t0 = (c - 2) * 128
                        for p, o in ((slice(0, 64), 0), (slice(64, 128), 1)):
                            dve.tensor_tensor(XB[p, bass.ds(t0 + o, 128)], XA[p, bass.ds(t0 + o, 128)],
                                              slot[3][p, 0:128], ALU.add).then_inc(s["xb_done"], 1)
                    if mid:
                        dve.tensor_reduce(row_sum[:, :], p3, AX.X, ALU.add).then_inc(s["sum_done"], 1)
                        dve.wait_ge(s["sum_done"], START + g)
                        dve.reciprocal(row_inv[:, :], row_sum[:, :]).then_inc(s["inv_done"], 1)
                    if front:
                        normalise(0, g, "rq_done", "iq_done", "qn_done")
                        normalise(1, g, "rk_done", "ik_done", "kn_done")
                steps(dve, lam, step)

                idx = n0 + 1 + L
                dve.wait_ge(s["ffn_in"], START + (lam + 1) * 16 * 13)
                dve.wait_ge(s["xb_done"], START + 2 * (lam + 1) * NCH)
                dve_norm(dve, idx, lambda b: XB[:, b * 512:b * 512 + 512], 1e-5,
                         dve_affine(dve, idx, normed, ffn_cols[:, 0:1], ffn_cols[:, 1:2]))
                for b in range(NB):
                    f = lam * NB + b
                    for j, (a, m) in enumerate(FT):
                        dve.wait_ge(s["gelu_done"], START + f * 3 + j + 1)
                        dve.wait_ge(s["w2_mm"], START + f)
                        dve.scalar_tensor_tensor(out=hidden[0:m, j, :], in0=slot[j + 1][0:m, 0:512],
                                                 scalar=b1[0:m, 0, j:j + 1], in1=gate[0:m, j, :],
                                                 op0=ALU.add, op1=ALU.mult).then_inc(s["hid_done"], 1)
                    dve.wait_ge(s["w2_mm"], START + f + 1)
                    for p, o in ((slice(0, 64), 0), (slice(64, 128), 1)):
                        cols = slice(b * 512 + o, b * 512 + o + 512)
                        dve.scalar_tensor_tensor(out=XA[p, cols], in0=slot[1][p, 0:512], scalar=ffn_cols[p, 2:3],
                                                 in1=XB[p, cols], op0=ALU.add, op1=ALU.add).then_inc(s["f_done"], 1)
            dve.wait_ge(s["f_done"], START + 2 * NB * DEPTH * (call + 1))
            for b in range(NB):
                for p, o in ((slice(0, 64), 0), (slice(64, 128), 1)):
                    dve.tensor_tensor(XM[p, b * 512:b * 512 + 512], XM[p, b * 512:b * 512 + 512],
                                      XA[p, b * 512 + o:b * 512 + o + 512], ALU.add).then_inc(s["xm_done"], 1)

        A_PE_ROWS = 24
        XM0 = 8 * ("S0" in stages)
        QB_UNITS = [4 * q + 4 for q in range(NB)]
        A_UNITS = sum(QB_UNITS)
        A_TILES = [(i, u) for i in range(NCH) for u in range(1 + (i >= 8))]
        PER_HEAD = len(A_TILES)

        def sp_setup(sp):
            sp.dma_start(consts[:, :], A["shape_constants"]).then_inc(s["consts_in"], 16)
            sp.dma_start(x_nat[:, :, :], A["x"][0].rearrange("(c p) d -> p c d", p=128)).then_inc(s["x_in"], 16)
            sp.dma_start(wqkv_nat[:, :, :], A["w_qkv"].rearrange("(c p) d -> p c d", p=128)).then_inc(s["wa_in"], 16)
            sp.dma_start(wout_nat[:, :], A["w_out"]).then_inc(s["wa_in"], 16)

        def pool_setup(pool):
            pool.memset(minus_half[:, :], -0.5).then_inc(s["setup_pool"], 1)
            pool.memset(ones[:, :], 1.0).then_inc(s["setup_pool"], 1)
            pool.memset(V4[:, :, :, :], 0.0).then_inc(s["setup_pool"], 1)
            pool.wait_ge(s["setup_pool"], START + 3)
            pool.memset(V4[:, :, :, 8:9], 1.0).then_inc(s["setup_pool"], 1)
            pool.wait_ge(s["setup_pool"], START + 4)

        def pe_setup(pe):
            pe.wait_ge(s["consts_in"], START + 16)
            pe.wait_ge(s["x_in"], START + 16)
            for c in range(NCH):
                mm = pe.transpose(slot[c // 8][:, (c % 8) * 128:(c % 8) * 128 + 128], x_nat[:, c, :], ident)
            mm.then_inc(s["tr_x"], 1)
            pe.wait_ge(s["wa_in"], START + 32)
            for c in range(3):
                mm = pe.transpose(slot[2][:, c * 128:(c + 1) * 128], wqkv_nat[:, c, :], ident)
            mm.then_inc(s["tr_x"], 1)
            pe.wait_ge(s["wa_rows"], START + 1)
            for g in range(4):
                mm = pe.transpose(slot[3][:, g * 128:(g + 1) * 128],
                                  wout_pad[:, 4 * g:4 * g + 4, :].rearrange("p h r -> p (h r)"), ident)
            mm.then_inc(s["tr_wo"], 1)

        def act_setup(act):
            act.wait_ge(s["tr_x"], START + 1)
            for i in range(2):
                act.activation(XM[:, i * 1024:(i + 1) * 1024], slot[i][:, :], ACT.Copy).then_inc(s["setup_act"], 1)
            act.wait_ge(s["tr_wo"], START + 1)
            act.activation(wout_rows[:, :, :].rearrange("p g n -> p (g n)"), slot[3][:, 0:512], ACT.Copy)\
               .then_inc(s["setup_act"], 1)

        def dve_setup(dve):
            dve.memset(wq_rows[:, :, :], 0.0)
            dve.memset(wk_rows[:, :, :], 0.0)
            dve.memset(wout_pad[:, :, :], 0.0)
            dve.memset(part_max[:, :, :], -3.0e38)
            dve.memset(neg_max[:, :], 0.0)
            dve.memset(XA[64:128, 0:1], 0.0)
            dve.memset(XB[64:128, 0:1], 0.0).then_inc(s["setup_dve"], 1)
            dve.wait_ge(s["setup_dve"], START + 1)
            dve.wait_ge(s["wa_in"], START + 32)
            dve.tensor_copy(wout_pad[:, :, 0:AH], wout_nat[:, :].rearrange("p (h d) -> p h d", d=AH))\
               .then_inc(s["wa_rows"], 1)
            dve.wait_ge(s["consts_in"], START + 16)
            dve.tensor_copy(ident_b[:, :], ident)
            dve.tensor_copy(mask_qk[:, :], const("mask_qk"))
            dve.tensor_copy(mask_kq[:, :], const("mask_kq"))
            dve.tensor_copy(mask_win[:, :, :], const("mask_win").rearrange("p (a k) -> p a k", a=2))\
               .then_inc(s["setup_dve"], 1)
            dve.wait_ge(s["tr_x"], START + 2)
            wt = slot[2][:, 0:384].rearrange("p (c h d) -> p c h d", c=3, d=AH)
            for rep in range(3):
                rows = slice(AH * rep, AH * rep + AH)
                dve.tensor_scalar(wq_rows[:, :, rows], wt[:, 0], AH ** -0.5, None, ALU.mult)
                dve.tensor_copy(wk_rows[:, :, rows], wt[:, 1])
            dve.tensor_copy(wv_cols[:, :], slot[2][:, 256:384]).then_inc(s["setup_dve"], 1)

        def sp_first(sp):
            with sp.Fori(0, 4) as g:
                sp.wait_ge(s["a_hi"], START + g + 1)
                sp.sem_inc(s["passed"], 1)
                sp.wait_ge(s["a_lo"], START + g + 1)
                for j, src in enumerate((neg_hi, neg_lo)):
                    sp.dma_start(rows_dram[j], src[:, :].bitcast(F32)).then_inc(s["a_rows"], 16)
                sp.wait_ge(s["a_rows"], START + 32 * (g + 1))
                for hh in range(4):
                    for j in range(2):
                        r = 32 * hh + A_PE_ROWS + j
                        sp.dma_start(QT[r:r + 1, :].bitcast(F32),
                                     rows_dram[j:j + 1, 16 * hh:16 * hh + 16, :].rearrange("a i t -> a (i t)"))\
                          .then_inc(s["a_dma"], 16)

        def pe_first(pe):
            pe_norm(pe, LN_A, lambda b: XM[:, b * 512:b * 512 + 512],
                    lambda b: (pe.wait_ge(s["setup_act"], START + 3), pe.wait_ge(s["setup_dve"], START + 3),
                               pe.wait_ge(s["setup_pool"], START + 4)))
            pe.wait_ge(s["ln_done"], START + NB)
            with pe.Fori(0, 4) as g:
                pe.wait_ge(s["a_w"], START + g + 1)
                for b in range(NB):
                    if b == 3:
                        pe.wait_ge(s["a_yadd"], START + 4 * g)
                    for i, w in enumerate((gq_w, gk_w)):
                        mm = pe.matmul(slot[b][:, i * 512:(i + 1) * 512], w[:, :], normed[:, b * 512:b * 512 + 512],
                                       start=True, stop=True)
                    mm.then_inc(s["a_qk"], 1)
                pe.wait_ge(s["a_split"], START + 4 * g + 1)
                for k in range(NCH):
                    mm = pe.matmul(slot[0][:, 32 * k:32 * k + 32], normed[:, k * 128:k * 128 + 128], gv_w[:, :],
                                   start=True, stop=True)
                mm.then_inc(s["a_v"], 1)
                pe.wait_ge(s["a_vsb"], START + g + 1)
                pe.wait_ge(s["a_split"], START + 4 * g + 4)
                n = 0
                for hh in range(4):
                    rows = slice(32 * hh, 32 * hh + A_PE_ROWS)
                    for i, u in A_TILES:
                        if n >= 4:
                            pe.wait_ge(s["a_max"], START + 4 * PER_HEAD * g + n - 3)
                        width = min(1024, 128 * (i + 1) - 1024 * u)
                        last = 128 * (i + 1) - 1024 * u <= 1024
                        for a in range(0, width, 512):
                            m = min(512, width - a)
                            diag = last and a + m == width
                            mm = pe.matmul(slot[n % 4][:, a:a + m], QT[rows, 128 * i:128 * i + 128],
                                           KT[rows, 1024 * u + a:1024 * u + a + m], start=True, stop=True)
                            if diag:
                                mm = pe.matmul(slot[n % 4][:, width - 128:width], ident_b[:, :], mask_qk[:, :],
                                               start=False, stop=True, skip_group_check=True)
                        mm.then_inc(s["a_s1"], 1)
                        n += 1
                pe.wait_ge(s["a_neg"], START + g + 1)
                pe.transpose(slot[0][:, 0:128], neg_max[:, :], ident).then_inc(s["a_nt"], 1)
                pe.wait_ge(s["a_dma"], START + 128 * (g + 1))
                units = [(qb, k) for qb in range(NB) for k in range(QB_UNITS[qb])]

                def scores(n):
                    qb, k = units[n]
                    c0 = max(0, 128 * (k - 4 * qb))
                    for half in range(2):
                        h2 = 2 * n + half
                        if h2 >= 3:
                            pe.wait_ge(s["a_exp"], START + 2 * A_UNITS * g + h2 - 2)
                        for e in range(2):
                            hh = 2 * half + e
                            rows = slice(32 * hh, 32 * hh + A_PE_ROWS + 2)
                            diag = k >= 4 * qb
                            o = slot[h2 % 3]
                            mm = pe.matmul(o[:, 512 * e + c0:512 * e + 512], KT[rows, 128 * k:128 * k + 128],
                                           QT[rows, 512 * qb + c0:512 * qb + 512], start=True, stop=True)
                            if diag:
                                mm = pe.matmul(o[:, 512 * e + c0:512 * e + c0 + 128], ident_b[:, :], mask_kq[:, :],
                                               start=False, stop=True, skip_group_check=True)
                        mm.then_inc(s["a_s"], 1)

                def values(n):
                    qb, k = units[n]
                    c0 = max(0, 128 * (k - 4 * qb))
                    pe.wait_ge(s["a_exp"], START + 2 * A_UNITS * g + 2 * n + 2)
                    if k == 0:
                        pe.wait_ge(s["a_osb"], START + 4 * g + qb)
                    for hh in range(4):
                        mm = pe.matmul(slot[3][32 * hh:32 * hh + 32, c0:512], V4[:, k, hh, :],
                                       Pa[:, (2 * n + hh // 2) % 4, 512 * (hh % 2) + c0:512 * (hh % 2) + 512],
                                       start=(k == 0), stop=(k >= 4 * qb), skip_group_check=True)
                    mm.then_inc(s["a_pv"], 1)

                def sums(qb):
                    pe.wait_ge(s["a_osb"], START + 4 * g + qb + 1)
                    pe.wait_ge(s["a_yadd"], START + 4 * g + qb)
                    pe.matmul(slot[3][:, 512:1024], const("sum_rows"), Oa[:, :], start=True, stop=True)\
                      .then_inc(s["a_bc"], 1)

                def project(qb):
                    pe.wait_ge(s["a_on"], START + 4 * g + qb + 1)
                    pe.matmul(slot[3][:, 512:1024], go_w[:, :], On[:, :], start=True, stop=True)\
                      .then_inc(s["a_y"], 1)

                scores(0)
                for n, (qb, k) in enumerate(units):
                    if n + 1 < len(units):
                        scores(n + 1)
                    values(n)
                    if qb >= 1 and k == 1:
                        sums(qb - 1)
                    if qb >= 1 and k == 5:
                        project(qb - 1)
                sums(NB - 1)
                project(NB - 1)

        def act_first(act):
            act.wait_ge(s["setup_pool"], START + 4)
            act_norm(act, LN_A)
            with act.Fori(0, 4) as g:
                for b in range(NB):
                    act.wait_ge(s["a_qk"], START + 4 * g + b + 1)
                    act.activation(rounded[:, b % 2, :], slot[b][:, :], ACT.Copy).then_inc(s["a_round"], 1)
                    act.wait_ge(s["a_round"], START + 4 * g + b + 1)
                    act.wait_ge(s["a_split"], START + 4 * g + (b - 1 if b >= 2 else 0))
                    act.activation(scaled[:, b % 2, 0:512], rounded[:, b % 2, 0:512].bitcast(F32), ACT.Copy,
                                   scale=const("rows")[:, 0:1])
                    act.activation(scaled[:, b % 2, 512:1024], rounded[:, b % 2, 512:1024].bitcast(F32),
                                   ACT.Identity, scale=const("rows")[:, 2:3], bias=const("rows")[:, 4:5])\
                       .then_inc(s["a_scaled"], 1)
                act.wait_ge(s["a_v"], START + g + 1)
                act.wait_ge(s["a_pv"], START + A_UNITS * g)
                act.activation(V4[:, :, :, 0:AH].rearrange("p k h d -> p (k h) d"),
                               slot[0][:, 0:512].rearrange("p (x d) -> p x d", d=AH), ACT.Copy)\
                   .then_inc(s["a_vsb"], 1)
                act.wait_ge(s["a_nt"], START + g + 1)
                act.wait_ge(s["a_dma"], START + 128 * g)
                act.activation(neg_hi[:, :], slot[0][0:64, 0:128], ACT.Copy).then_inc(s["a_hi"], 1)
                units = [(qb, k) for qb in range(NB) for k in range(QB_UNITS[qb])]

                def take_output(qb):
                    act.wait_ge(s["a_pv"], START + A_UNITS * g + sum(QB_UNITS[:qb + 1]))
                    act.wait_ge(s["a_on"], START + 4 * g + qb)
                    act.activation(Oa[:, :], slot[3][:, 0:512], ACT.Copy).then_inc(s["a_osb"], 1)
                for n, (qb, k) in enumerate(units):
                    c0 = max(0, 128 * (k - 4 * qb))
                    for half in range(2):
                        h2 = 2 * n + half
                        act.wait_ge(s["a_s"], START + 2 * A_UNITS * g + h2 + 1)
                        if n >= 2:
                            act.wait_ge(s["a_pv"], START + A_UNITS * g + n - 1)
                        act.activation(Pa[:, h2 % 4, :].rearrange("p (e q) -> p e q", e=2)[:, :, c0:512],
                                       slot[h2 % 3][:, :].rearrange("p (e q) -> p e q", e=2)[:, :, c0:512],
                                       ACT.Exp).then_inc(s["a_exp"], 1)
                    if qb >= 1 and k == 0:
                        take_output(qb - 1)
                take_output(NB - 1)

        def dve_first(dve):
            dve.wait_ge(s["setup_act"], START + 2)
            dve_norm(dve, LN_A, lambda b: XM[:, b * 512:b * 512 + 512], 1e-5, dve_plain(dve, LN_A, normed))
            dve.wait_ge(s["setup_act"], START + 3)
            dve.wait_ge(s["setup_dve"], START + 3)
            with dve.Fori(0, 4) as g:
                dve.wait_ge(s["a_y"], START + 4 * g)
                dve.tensor_copy(gq_w[:, :], wq_rows[:, :, :].rearrange("p h r -> p (h r)")[:, bass.ds(g * 128, 128)])
                dve.tensor_copy(gk_w[:, :], wk_rows[:, :, :].rearrange("p h r -> p (h r)")[:, bass.ds(g * 128, 128)])
                dve.tensor_copy(gv_w[:, :], wv_cols[:, bass.ds(g * 32, 32)])
                dve.tensor_copy(go_w[:, :], wout_rows[:, :, :].rearrange("p g n -> p (g n)")[:, bass.ds(g * 128, 128)])\
                   .then_inc(s["a_w"], 1)
                for b in range(NB):
                    dve.wait_ge(s["a_scaled"], START + 4 * g + b + 1)
                    cols = slice(b * 512, b * 512 + 512)
                    dve.scalar_tensor_tensor(out=QT[:, cols], in0=slot[b][:, 0:512], scalar=const("rows")[:, 1:2],
                                             in1=scaled[:, b % 2, 0:512], op0=ALU.mult, op1=ALU.add)
                    dve.scalar_tensor_tensor(out=KT[:, cols], in0=slot[b][:, 512:1024], scalar=const("rows")[:, 3:4],
                                             in1=scaled[:, b % 2, 512:1024], op0=ALU.mult, op1=ALU.add)\
                       .then_inc(s["a_split"], 1)
                n = 0
                for hh in range(4):
                    for i, u in A_TILES:
                        width = min(1024, 128 * (i + 1) - 1024 * u)
                        dve.wait_ge(s["a_s1"], START + 4 * PER_HEAD * g + n + 1)
                        dve.tensor_reduce(part_max[:, 16 * hh + i, u:u + 1], slot[n % 4][:, 0:width], AX.X, ALU.max)\
                           .then_inc(s["a_max"], 1)
                        n += 1
                dve.wait_ge(s["a_max"], START + 4 * PER_HEAD * (g + 1))
                dve.wait_ge(s["a_nt"], START + g)
                dve.tensor_tensor(neg_max[:, 0:64], part_max[:, :, 0], part_max[:, :, 1], ALU.max)\
                   .then_inc(s["a_comb"], 1)
                dve.wait_ge(s["a_comb"], START + g + 1)
                dve.tensor_scalar(neg_max[:, 0:64], neg_max[:, 0:64], -1.0, None, ALU.mult).then_inc(s["a_neg"], 1)
                dve.wait_ge(s["a_hi"], START + g + 1)
                dve.tensor_tensor(neg_lo[:, :], slot[0][0:64, 0:128], neg_hi[:, :].bitcast(F32), ALU.subtract)\
                   .then_inc(s["a_lo"], 1)
                for qb in range(NB):
                    dve.wait_ge(s["a_bc"], START + 4 * g + qb + 1)
                    dve.reciprocal(sum_inv[:, :], slot[3][:, 512:1024]).then_inc(s["a_inv"], 1)
                    dve.wait_ge(s["a_inv"], START + 4 * g + qb + 1)
                    dve.tensor_tensor(On[:, :], Oa[:, :], sum_inv[:, :], ALU.mult).then_inc(s["a_on"], 1)
                    dve.wait_ge(s["a_y"], START + 4 * g + qb + 1)
                    cols = slice(qb * 512, qb * 512 + 512)
                    dve.tensor_tensor(XM[:, cols], XM[:, cols], slot[3][:, 512:1024], ALU.add)\
                       .then_inc(s["a_yadd"], 1)

        def xm_ready(eng, call):
            if call == 0:
                eng.wait_ge(s["a_yadd"], START + (16 if "A" in stages else 0))
                eng.wait_ge(s["setup_act"], START + 3)
                eng.wait_ge(s["setup_dve"], START + 3)
            else:
                eng.wait_ge(s["b_yadd"], START + (32 if "B" in stages else 0))
                eng.wait_ge(s["xm_done"], START + XM0)

        def ln_into(call):
            return LN_S0 if call == 0 else LN_S1

        def pe_into(pe, call):
            pe_norm(pe, ln_into(call), lambda b: XM[:, b * 512:b * 512 + 512],
                    lambda b: xm_ready(pe, call))

        def dve_into(dve, call):
            n = ln_into(call)
            xm_ready(dve, call)

            def finish(b, c, r):
                dve.wait_ge(s["stack_in"], START + 8 * call)
                for p, o in ((slice(0, 64), 0), (slice(64, 128), 1)):
                    ins = dve.tensor_tensor(XA[p, b * 512 + o:b * 512 + o + 512], c[p], r[p], ALU.mult)
                    ins.then_inc(s["stack_in"], 1)
                dve.wait_ge(s["stack_in"], START + 8 * call + 2 * b + 2)
                dve.sem_inc(s["ln_half"], 1)
                dve.sem_inc(s["ln_done"], 1)
            dve_norm(dve, n, lambda b: XM[:, b * 512:b * 512 + 512], 1e-5, finish)
            dve.memset(kT[:, :, :], 0.0)
            dve.memset(V[1][:, :], 0.0).then_inc(s["stack_out"], 1)

        def sp_grouped(sp):
            sp.wait_ge(s["xm_done"], START + XM0)
            sp.dma_start(b_wq[:, :], A["Wq"]).then_inc(s["wb_in"], 16)
            sp.dma_start(b_wkv[:, :], A["Wkv"]).then_inc(s["wb_in"], 16)
            sp.dma_start(b_wout[:, :, :], A["Wout"].rearrange("(j p) n -> p j n", p=128)).then_inc(s["wb_in"], 16)
            for j, name in enumerate(("b_ln_scale", "b_ln_bias")):
                sp.dma_start(b_cols[:, j:j + 1], A[name].rearrange("(p a) -> p a", a=1)).then_inc(s["wb_in"], 16)
            for j, name in enumerate(("qn_scale", "qn_bias", "kn_scale", "kn_bias")):
                for r in range(2):
                    sp.dma_start(b_cols[64 * r:64 * r + 64, j + 2:j + 3], A[name].rearrange("(p a) -> p a", a=1))\
                      .then_inc(s["wb_in"], 16)
            with sp.Fori(0, 8) as p:
                sp.wait_ge(s["b_his"], START + p + 1)
                sp.sem_inc(s["passed"], 1)
                sp.wait_ge(s["b_los"], START + p + 1)
                for j, src in enumerate((b_hi, b_lo)):
                    sp.dma_start(rows_dram[j, 0:32, :], src[:, :].bitcast(F32)).then_inc(s["b_rows"], 16)
                sp.wait_ge(s["b_rows"], START + 32 * (p + 1))
                for hh in range(2):
                    for j in range(2):
                        sp.dma_start(QB[hh][64 + j:65 + j, :].bitcast(F32),
                                     rows_dram[j:j + 1, 16 * hh:16 * hh + 16, :].rearrange("a i t -> a (i t)"))\
                          .then_inc(s["b_dma"], 16)

        WB_IN = 16 * 13
        def ln_k(kv):
            return LN_B + 2 + 5 * kv

        def ln_q(kv, pr, hh):
            return LN_B + 2 + 5 * kv + 1 + 2 * pr + hh

        def b_ring():
            entries = []
            for n in range(64):
                entries.append(("s", n))
                if n % 16 == 6 and n >= 16:
                    entries.append(("y", n // 16 - 1))
            entries.append(("y", NB - 1))
            place_of, before = {}, {}
            for m, e in enumerate(entries):
                place_of[e] = m % 3
                before[e] = entries[m - 3] if m >= 3 else None
            return entries, place_of, before

        B_ENTRIES, B_PLACE, B_BEFORE = b_ring()

        def ring_free(pe, e, p):
            b = B_BEFORE[e]
            if b is not None:
                pe.wait_ge(s["b_exp"] if b[0] == "s" else s["b_yadd"],
                           START + (64 if b[0] == "s" else NB) * p + b[1] + 1)

        def pe_head(pe, n, mm_before, which):
            for b in range(NB):
                mm = pe.matmul(slot[b][:, 0:512], b_w[:, which, :], z2[:, b * 512:b * 512 + 512],
                               start=True, stop=True)
                mm.then_inc(s["b_mm"], 1)
            pe_norm(pe, n, lambda b: b_part[:, b * 512:b * 512 + 512],
                    lambda b: pe.wait_ge(s["b_qb"], START + mm_before + b + 1))

        def pe_grouped(pe):
            pe_norm(pe, LN_B, lambda b: XM[:, b * 512:b * 512 + 512],
                    lambda b: pe.wait_ge(s["xm_done"], START + XM0))
            pe_norm(pe, LN_B + 1, lambda b: normed[:, b * 512:b * 512 + 512],
                    lambda b: pe.wait_ge(s["ln_done"], START + (LN_B + 1) * NB))
            pe.wait_ge(s["ln_done"], START + (LN_B + 2) * NB)
            with pe.Fori(0, 4) as kv:
                pe.wait_ge(s["b_w_done"], START + kv * 3 + 1)
                pe.wait_ge(s["b_yadd"], START + 8 * NB * 0 + 2 * NB * kv)
                pe_head(pe, ln_k(kv), (5 * kv) * NB, 0)
                pe.wait_ge(s["ln_done"], START + (ln_k(kv) + 1) * NB)
                for k in range(NCH):
                    mm = pe.matmul(slot[0][:, 64 * k:64 * k + 64], z2[:, k * 128:k * 128 + 128], b_w[:, 2, 0:64],
                                   start=True, stop=True)
                mm.then_inc(s["b_v"], 1)
                with pe.Fori(0, 2) as pr:
                    p = pe.snap(kv * 2 + pr)
                    pe.wait_ge(s["b_w_done"], START + kv * 3 + pr + 2)
                    pe.wait_ge(s["b_vsb"], START + kv + 1)
                    pe.wait_ge(s["b_yadd"], START + NB * p)
                    for hh in range(2):
                        pe_head(pe, ln_q(kv, pr, hh), (5 * kv + 1 + 2 * pr + hh) * NB, hh)
                        pe.wait_ge(s["ln_done"], START + (ln_q(kv, pr, hh) + 1) * NB)
                    pe.wait_ge(s["b_split"], START + 5 * kv + 2 * pr + 3)
                    n = 0
                    for hh in range(2):
                        for i in range(NCH):
                            for u in range(2):
                                if n >= 4:
                                    pe.wait_ge(s["b_max"], START + 64 * p + n - 3)
                                for a in (0, 512):
                                    keys = slice(1024 * u + a, 1024 * u + a + 512)
                                    pe.matmul(slot[n % 4][:, a:a + 512], QA[hh][:, 128 * i:128 * i + 128],
                                              KA[:, keys], start=True, stop=False)
                                    mm = pe.matmul(slot[n % 4][:, a:a + 512], QB[hh][0:64, 128 * i:128 * i + 128],
                                                   KB[0:64, keys], start=False, stop=True)
                                mm.then_inc(s["b_s1"], 1)
                                n += 1
                    pe.wait_ge(s["b_neg"], START + p + 1)
                    pe.transpose(slot[0][:, 0:128], b_nmax[:, :], ident).then_inc(s["b_nt"], 1)
                    pe.wait_ge(s["b_dma"], START + 64 * (p + 1))

                    def scores(n):
                        ring_free(pe, ("s", n), p)
                        qb, k = n // 16, n % 16
                        o = slot[B_PLACE[("s", n)]]
                        for hh in range(2):
                            pe.matmul(o[:, 512 * hh:512 * hh + 512], KA[:, 128 * k:128 * k + 128],
                                      QA[hh][:, 512 * qb:512 * qb + 512], start=True, stop=False)
                            mm = pe.matmul(o[:, 512 * hh:512 * hh + 512], KB[:, 128 * k:128 * k + 128],
                                           QB[hh][:, 512 * qb:512 * qb + 512], start=False, stop=True)
                        mm.then_inc(s["b_s"], 1)

                    def values(n):
                        qb, k = n // 16, n % 16
                        pe.wait_ge(s["b_exp"], START + 64 * p + n + 1)
                        if k == 0:
                            pe.wait_ge(s["b_rnd"], START + NB * p + qb)
                        for hh in range(2):
                            pe.matmul(slot[3][64 * hh:64 * hh + 64, 0:512], Vb[:, k, :],
                                      Pb[:, n % 3, 512 * hh:512 * hh + 512], start=(k == 0), stop=(k == 15),
                                      skip_group_check=True)
                        for hh in range(2):
                            mm = pe.matmul(slot[3][64 * hh:64 * hh + 32, 512:1024], ones32[:, :],
                                           Pb[:, n % 3, 512 * hh:512 * hh + 512], start=(k == 0), stop=(k == 15),
                                           skip_group_check=True)
                        mm.then_inc(s["b_pv"], 1)

                    def project(qb):
                        ring_free(pe, ("y", qb), p)
                        pe.wait_ge(s["b_on"], START + NB * p + qb + 1)
                        pe.matmul(slot[B_PLACE[("y", qb)]][:, 0:512], b_wo[:, :], Ob[:, :], start=True, stop=True)\
                          .then_inc(s["b_y"], 1)

                    scores(0)
                    done = 0
                    for kind, n in B_ENTRIES[1:]:
                        if kind == "s":
                            scores(n)
                            values(n - 1)
                            done = n
                        else:
                            if n == NB - 1:
                                values(done)
                            project(n)

        def act_head(act, mm_before, n):
            for b in range(NB):
                act.wait_ge(s["b_mm"], START + mm_before + b + 1)
                act.activation(b_part[:, b * 512:b * 512 + 512], slot[b][:, 0:512], ACT.Copy).then_inc(s["b_qb"], 1)
            act_norm(act, n)

        def act_grouped(act):
            act_norm(act, LN_B)
            act_norm(act, LN_B + 1)
            with act.Fori(0, 4) as kv:
                act.wait_ge(s["b_split"], START + 5 * kv)
                act_head(act, (5 * kv) * NB, ln_k(kv))
                act.wait_ge(s["ln_done"], START + (ln_k(kv) + 1) * NB)
                act.activation(KA[:, :], normed[:, :], ACT.Copy).then_inc(s["b_prt"], 1)
                act.wait_ge(s["b_v"], START + kv + 1)
                act.activation(Vb[:, :, :].rearrange("p k d -> p (k d)"), slot[0][:, :], ACT.Copy)\
                   .then_inc(s["b_vsb"], 1)
                with act.Fori(0, 2) as pr:
                    p = act.snap(kv * 2 + pr)
                    for hh in range(2):
                        act.wait_ge(s["b_split"], START + 5 * kv + 2 * pr + hh + 1)
                        act_head(act, (5 * kv + 1 + 2 * pr + hh) * NB, ln_q(kv, pr, hh))
                        act.wait_ge(s["ln_done"], START + (ln_q(kv, pr, hh) + 1) * NB)
                        act.activation(b_round[:, :], normed[:, :], ACT.Copy).then_inc(s["b_ln"], 1)
                        act.wait_ge(s["b_ln"], START + 4 * kv + 2 * pr + hh + 1)
                        act.activation(b_part[:, :], b_round[:, :].bitcast(F32), ACT.Copy,
                                       scale=const("rows")[:, 5:6])
                        act.activation(QB[hh][0:64, :], b_round[0:64, :].bitcast(F32), ACT.Copy)\
                           .then_inc(s["b_prt"], 1)
                    act.wait_ge(s["b_nt"], START + p + 1)
                    act.wait_ge(s["b_dma"], START + 64 * p)
                    act.activation(b_hi[:, :], slot[0][0:32, 0:128], ACT.Copy).then_inc(s["b_his"], 1)

                    def take_output(qb):
                        act.wait_ge(s["b_pv"], START + 64 * p + 16 * (qb + 1))
                        act.wait_ge(s["b_on"], START + NB * p + qb)
                        act.activation(Oc[:, :], slot[3][:, :], ACT.Copy).then_inc(s["b_rnd"], 1)
                    for n in range(64):
                        act.wait_ge(s["b_s"], START + 64 * p + n + 1)
                        act.wait_ge(s["b_pv"], START + 64 * p + (n - 2 if n >= 3 else 0))
                        act.activation(Pb[:, n % 3, :], slot[B_PLACE[("s", n)]][:, :], ACT.Exp)\
                           .then_inc(s["b_exp"], 1)
                        if n % 16 == 0 and n:
                            take_output(n // 16 - 1)
                    take_output(NB - 1)

        def pool_grouped(pool):
            for n in (LN_B, LN_B + 1):
                pool_norm(pool, n)
            with pool.Fori(0, 4) as kv:
                pool_norm(pool, ln_k(kv))
                with pool.Fori(0, 2) as pr:
                    for hh in range(2):
                        pool_norm(pool, ln_q(kv, pr, hh))

        def dve_grouped(dve):
            dve.wait_ge(s["xm_done"], START + XM0)
            dve.memset(ones32[:, :], 1.0)
            dve.memset(b_nmax[:, :], 0.0)
            dve.memset(KB[64:66, :].bitcast(F32), 1.0).then_inc(s["b_ones"], 1)
            dve_norm(dve, LN_B, lambda b: XM[:, b * 512:b * 512 + 512], 1e-5, dve_plain(dve, LN_B, normed))
            dve.wait_ge(s["wb_in"], START + WB_IN)
            dve_norm(dve, LN_B + 1, lambda b: normed[:, b * 512:b * 512 + 512], 1e-6,
                     dve_affine(dve, LN_B + 1, z2, b_cols[:, 0:1], b_cols[:, 1:2]))
            dve.tensor_scalar(b_cols[:, 2:4], b_cols[:, 2:4], DH ** -0.5, None, ALU.mult).then_inc(s["b_ones"], 1)
            dve.wait_ge(s["b_ones"], START + 2)

            def head(n, g, bias):
                dve_norm(dve, n, lambda b: b_part[:, b * 512:b * 512 + 512], 1e-6, dve_affine(dve, n, normed, g, bias))

            with dve.Fori(0, 4) as kv:
                dve.wait_ge(s["b_y"], START + 2 * NB * kv)
                for i in range(2):
                    dve.tensor_copy(b_w[:, 0, 64 * i:64 * i + 64], b_wkv[:, bass.ds(kv * 64, 64)])
                dve.tensor_copy(b_w[:, 2, 0:64], b_wkv[:, bass.ds(kv * 64 + 256, 64)]).then_inc(s["b_w_done"], 1)
                dve.wait_ge(s["b_prt"], START + 5 * kv)
                head(ln_k(kv), b_cols[:, 4:5], b_cols[:, 5:6])
                dve.wait_ge(s["b_prt"], START + 5 * kv + 1)
                dve.tensor_tensor(KB[0:64, :], normed[0:64, :], KA[0:64, :].bitcast(F32), ALU.subtract)\
                   .then_inc(s["b_split"], 1)
                with dve.Fori(0, 2) as pr:
                    p = dve.snap(kv * 2 + pr)
                    dve.wait_ge(s["b_mm"], START + 5 * NB * kv + NB + 2 * NB * pr)
                    dve.wait_ge(s["b_y"], START + NB * p)
                    dve.wait_ge(s["b_v"], START + kv + 1)
                    for hh in range(2):
                        for i in range(2):
                            dve.tensor_copy(b_w[:, hh, 64 * i:64 * i + 64],
                                            b_wq[:, bass.ds(kv * 256 + pr * 128 + hh * 64, 64)])
                    dve.tensor_copy(b_wo[:, :], b_wout[:, :, :].rearrange("p j n -> p (j n)")[:, bass.ds(p * 128, 128)])\
                       .then_inc(s["b_w_done"], 1)
                    for hh in range(2):
                        head(ln_q(kv, pr, hh), b_cols[:, 2:3], b_cols[:, 3:4])
                        dve.wait_ge(s["b_prt"], START + 5 * kv + 1 + 2 * pr + hh + 1)
                        dve.scalar_tensor_tensor(out=QA[hh][:, :], in0=normed[:, :], scalar=const("rows")[:, 6:7],
                                                 in1=b_part[:, :], op0=ALU.mult, op1=ALU.add)\
                           .then_inc(s["b_split"], 1)
                    n = 0
                    for hh in range(2):
                        for i in range(NCH):
                            for u in range(2):
                                dve.wait_ge(s["b_s1"], START + 64 * p + n + 1)
                                dve.tensor_reduce(b_pmax[:, 16 * hh + i, u:u + 1], slot[n % 4][:, :], AX.X, ALU.max)\
                                   .then_inc(s["b_max"], 1)
                                n += 1
                    dve.wait_ge(s["b_max"], START + 64 * (p + 1))
                    dve.wait_ge(s["b_nt"], START + p)
                    dve.tensor_tensor(b_nmax[:, 0:32], b_pmax[:, :, 0], b_pmax[:, :, 1], ALU.max)\
                       .then_inc(s["b_comb"], 1)
                    dve.wait_ge(s["b_comb"], START + p + 1)
                    dve.tensor_scalar(b_nmax[:, 0:32], b_nmax[:, 0:32], -1.0, None, ALU.mult).then_inc(s["b_neg"], 1)
                    dve.wait_ge(s["b_his"], START + p + 1)
                    dve.tensor_tensor(b_lo[:, :], slot[0][0:32, 0:128], b_hi[:, :].bitcast(F32), ALU.subtract)\
                       .then_inc(s["b_los"], 1)
                    for qb in range(NB):
                        dve.wait_ge(s["b_rnd"], START + NB * p + qb + 1)
                        for hh in range(2):
                            r = slice(64 * hh, 64 * hh + 32)
                            ins = dve.reciprocal(b_inv[r, :], Oc[r, 512:1024])
                        ins.then_inc(s["b_invd"], 1)
                        dve.wait_ge(s["b_invd"], START + NB * p + qb + 1)
                        for hh in range(2):
                            r = slice(64 * hh, 64 * hh + 32)
                            q = slice(64 * hh + 32, 64 * hh + 64)
                            dve.tensor_tensor(Ob[r, :], Oc[r, 0:512], b_inv[r, :], ALU.mult)
                            ins = dve.tensor_tensor(Ob[q, :], Oc[q, 0:512], b_inv[r, :], ALU.mult)
                        ins.then_inc(s["b_on"], 1)
                        dve.wait_ge(s["b_y"], START + NB * p + qb + 1)
                        cols = slice(qb * 512, qb * 512 + 512)
                        dve.tensor_tensor(XM[:, cols], XM[:, cols], slot[B_PLACE[("y", qb)]][:, 0:512], ALU.add)\
                           .then_inc(s["b_yadd"], 1)

        def final_ready(eng):
            if "S1" in stages:
                eng.wait_ge(s["xm_done"], START + 16)
            elif "B" in stages:
                eng.wait_ge(s["b_yadd"], START + 32)
            elif "S0" in stages:
                eng.wait_ge(s["xm_done"], START + XM0)
            else:
                eng.wait_ge(s["a_yadd"], START + 16)

        def pe_out(pe):
            final_ready(pe)
            for c in range(NCH):
                mm = pe.transpose(slot[c // 8][:, (c % 8) * 128:(c % 8) * 128 + 128], XM[:, c * 128:c * 128 + 128],
                                  ident)
                if c % 8 == 7:
                    mm.then_inc(s["tr_out"], 1)

        def act_out(act):
            final_ready(act)
            for i in range(2):
                act.wait_ge(s["tr_out"], START + i + 1)
                act.activation(out_nat[:, 8 * i:8 * i + 8, :].rearrange("p c d -> p (c d)"), slot[i][:, :], ACT.Copy)\
                   .then_inc(s["out_sb"], 1)

        def sp_out(sp):
            for i in range(2):
                sp.wait_ge(s["out_sb"], START + i + 1)
                sp.dma_start(out[0, 1024 * i:1024 * i + 1024, :].rearrange("(c p) d -> p c d", p=128),
                             out_nat[:, 8 * i:8 * i + 8, :]).then_inc(s["out_done"], 16)
            sp.wait_ge(s["out_done"], START + 32)

        def start_counts(eng, which):
            for name in names[which::5]:
                eng.sem_inc(s[name], START)

        @block.sync
        def _(sp):
            start_counts(sp, 0)
            sp_setup(sp)
            if "A" in stages:
                sp_first(sp)
            if "S0" in stages:
                sp.wait_ge(s["stack_in"], START + 8)
                sp_stack(sp, 0)
            if "B" in stages:
                sp_grouped(sp)
            if "S1" in stages:
                sp.wait_ge(s["stack_in"], START + 16)
                sp_stack(sp, 1)
            sp_out(sp)

        @block.gpsimd
        def _(pool):
            start_counts(pool, 1)
            pool_setup(pool)
            if "A" in stages:
                pool_norm(pool, LN_A)
            if "S0" in stages:
                pool_norm(pool, LN_S0)
                pool_stack(pool, 0)
            if "B" in stages:
                pool_grouped(pool)
            if "S1" in stages:
                pool_norm(pool, LN_S1)
                pool_stack(pool, 1)

        @block.scalar
        def _(act):
            start_counts(act, 2)
            act_setup(act)
            if "A" in stages:
                act_first(act)
            if "S0" in stages:
                act.wait_ge(s["setup_pool"], START + 4)
                act_norm(act, LN_S0)
                act.wait_ge(s["stack_out"], START + 1)
                act_stack(act, 0)
            if "B" in stages:
                act_grouped(act)
            if "S1" in stages:
                act_norm(act, LN_S1)
                act.wait_ge(s["stack_out"], START + 2)
                act_stack(act, 1)
            act_out(act)

        @block.vector
        def _(dve):
            start_counts(dve, 3)
            dve_setup(dve)
            if "A" in stages:
                dve_first(dve)
            if "S0" in stages:
                dve_into(dve, 0)
                dve_stack(dve, 0)
            if "B" in stages:
                dve_grouped(dve)
            if "S1" in stages:
                dve_into(dve, 1)
                dve_stack(dve, 1)

        @block.tensor
        def _(pe):
            start_counts(pe, 4)
            pe_setup(pe)
            if "A" in stages:
                pe_first(pe)
            if "S0" in stages:
                pe_into(pe, 0)
                pe_stack(pe, 0)
            if "B" in stages:
                pe_grouped(pe)
            if "S1" in stages:
                pe_into(pe, 1)
                pe_stack(pe, 1)
            pe_out(pe)


_INS = {"x": "L0_attn_a_x", "w_qkv": "L0_attn_a_w_qkv", "w_out": "L0_attn_a_w_out",
        "b_ln_scale": "L0_attn_b_ln_scale", "b_ln_bias": "L0_attn_b_ln_bias", "Wq": "L0_attn_b_Wq",
        "Wkv": "L0_attn_b_Wkv", "qn_scale": "L0_attn_b_qn_scale", "qn_bias": "L0_attn_b_qn_bias",
        "kn_scale": "L0_attn_b_kn_scale", "kn_bias": "L0_attn_b_kn_bias", "Wout": "L0_attn_b_Wout",
        "Wqkv": "L0_ffn_Wqkv", "q_scale": "L0_ffn_q_scale", "k_scale": "L0_ffn_k_scale", "Wo": "L0_ffn_Wo",
        "ln_g": "L0_ffn_ln_g", "ln_b": "L0_ffn_ln_b", "W1": "L0_ffn_W1", "b1": "L0_ffn_b1",
        "W2": "L0_ffn_W2", "b2": "L0_ffn_b2"}


def kernel(**inputs):
    import concourse.bacc as bacc
    from concourse.bass_utils import run_bass_kernel_spmd

    nc = bacc.Bacc("TRN2", target_bir_lowering=False, num_devices=1)
    nc.disable_value_cache = True
    table, place = shape_constants()
    arrays = {"in_shape_constants": np.ascontiguousarray(table)}
    for short, name in _INS.items():
        arrays[f"in_{short}"] = np.ascontiguousarray(inputs[name])
    A = {k[3:]: nc.dram_tensor(k, a.shape, mybir.dt.from_np(a.dtype), kind="ExternalInput").ap()
         for k, a in arrays.items()}
    out = nc.dram_tensor("out", (1, S, D), F32, kind="ExternalOutput").ap()
    build(nc, A, out, place)
    r = run_bass_kernel_spmd(nc, [arrays], core_ids=[0])
    return r.results[0]["out"]
```

```python
from contextlib import ExitStack

import numpy as np

import concourse.bass as bass
from concourse import mybir

F32 = mybir.dt.float32
F32R = mybir.dt.float32r
BF16 = mybir.dt.bfloat16
ALU = mybir.AluOpType
ACT = mybir.ActivationFunctionType
AX = mybir.AxisListType

S = 2048
D = 128
NCH = S // 128
NB = S // 512
DEPTH = 6
H, DH = 16, 64
WIN = 32
INNER = H * DH
DFF = 341
FT = [(0, 128), (128, 128), (256, DFF - 256)]
AH = 8
START = 1
NEG = -1.0e30


def shape_constants():
    f = np.float32
    parts = {}
    parts["ident"] = np.eye(128, dtype=f)
    parts["mean128"] = np.full((128, 128), 1.0 / 128, f)
    i = np.arange(128)
    parts["mask_qk"] = np.where(i[None, :] <= i[:, None], 0, NEG).astype(f)
    parts["mask_kq"] = np.where(i[:, None] <= i[None, :], 0, NEG).astype(f)
    q = (i % WIN)[:, None]
    m = np.arange(2 * WIN)[None, :]
    ok = np.where(m < WIN, q <= m, m - WIN <= q)
    win = np.repeat(np.where(ok, 0, NEG)[:, None, :], 2, 1)
    win[:WIN, 0, :WIN] = NEG
    parts["mask_win"] = win.reshape(128, 2 * 2 * WIN).astype(f)
    half = np.arange(0, DH, 2, dtype=f)
    inv_freq = (f(1.0) / np.power(f(10000.0), half / f(DH))).astype(f)
    t = np.arange(S, dtype=f)
    ang = (t[:, None] * inv_freq[None, :]).astype(f)
    ang = np.concatenate([ang, ang], -1).astype(np.float64)
    base = (half.astype(np.float64) + 0.4 * DH) / (1.4 * DH)
    base = np.concatenate([base, base])
    power = (np.arange(S) % 128) / (WIN // 2)
    scale = base[None, :] ** power[:, None]
    sign = np.where(np.arange(DH) < DH // 2, -1.0, 1.0)

    def chunked(a):
        return a.reshape(NCH, 128, DH).transpose(1, 0, 2).reshape(128, NCH * DH).astype(f)

    parts["rot_q_cos"] = chunked(np.cos(ang) * scale * 8.0)
    parts["rot_q_sin"] = chunked(np.sin(ang) * scale * 8.0 * sign)
    parts["rot_k_cos"] = chunked(np.cos(ang) / scale)
    parts["rot_k_sin"] = chunked(np.sin(ang) / scale * sign)
    parts["cross"] = np.tile(base ** 8.0, 2).reshape(128, 1).astype(f)
    r = i % 32
    hi_q, lo_q = (r < 8) | ((r >= 16) & (r < 24)), (r >= 8) & (r < 16)
    hi_k, lo_k = r < 16, (r >= 16) & (r < 24)
    cols = [hi_q * 1.0 - lo_q, lo_q * 1.0, hi_k * 1.0 - lo_k, lo_k * 1.0,
            ((r == 24) | (r == 25)) * 1.0,
            np.where(i < 64, 1.0, -1.0), np.where(i < 64, 0.0, 1.0)]
    parts["rows"] = np.stack(cols, 1).astype(f)
    parts["sum_rows"] = ((i[:, None] // 32 == i[None, :] // 32) & (i[:, None] % 32 == 8)).astype(f)
    at, place = 0, {}
    for name, a in parts.items():
        place[name] = (at, a.shape[1])
        at += a.shape[1]
    return np.concatenate(list(parts.values()), 1), place


def build(nc, A, out, place, stages=("A", "S0", "B", "S1")):
    n_const = A["shape_constants"].shape[1]
    ctx = ExitStack()
    with ctx:
        def sem(name):
            return ctx.enter_context(nc.semaphore(name))

        def sb(name, shape, dt=F32, at=ctx):
            return at.enter_context(nc.sbuf_tensor(name, shape, dt))

        consts = sb("consts", [128, n_const])

        def const(name):
            a, n = place[name]
            return consts[:, a:a + n]

        ident = const("ident")
        ident_b = sb("ident_b", [128, 128], BF16)
        mask_qk = sb("mask_qk", [128, 128], BF16)
        mask_kq = sb("mask_kq", [128, 128], BF16)
        mask_win = sb("mask_win", [128, 2, 2 * WIN], BF16)
        minus_half = sb("minus_half", [128, H])
        ones = sb("ones", [128, 128])
        XM = sb("XM", [128, S])
        XA = sb("XA", [128, S + 1])
        XB = sb("XB", [128, S + 1])
        centred = sb("centred", [128, S])
        normed = sb("normed", [128, S])
        squares = sb("squares", [128, 2, 512])
        variance = sb("variance", [128, NCH])
        rstd = sb("rstd", [128, NCH])
        diag = sb("diag", [128, 2, 512])
        slot = [ctx.enter_context(nc.psum_tensor(f"slot{i}", [128, 1024], F32)) for i in range(4)]

        rows_dram = nc.dram_tensor("rows_dram", (2, 64, 128), F32).ap()

        mem = ExitStack()
        x_nat = sb("x_nat", [128, NCH, D], F32, mem)
        wqkv_nat = sb("wqkv_nat", [128, 3, D], F32, mem)
        wout_nat = sb("wout_nat", [128, D], F32, mem)
        wq_rows = sb("wq_rows", [128, 16, 32], F32, mem)
        wk_rows = sb("wk_rows", [128, 16, 32], F32, mem)
        wv_cols = sb("wv_cols", [128, D], F32, mem)
        wout_pad = sb("wout_pad", [128, 16, 32], F32, mem)
        wout_rows = sb("wout_rows", [128, 4, D], F32, mem)
        gq_w = sb("gq_w", [128, D], F32, mem)
        gk_w = sb("gk_w", [128, D], F32, mem)
        gv_w = sb("gv_w", [128, 32], F32, mem)
        go_w = sb("go_w", [128, D], F32, mem)
        rounded = sb("rounded", [128, 2, 1024], F32R, mem)
        scaled = sb("scaled", [128, 2, 1024], F32, mem)
        QT = sb("QT", [128, S], F32R, mem)
        KT = sb("KT", [128, S], F32R, mem)
        V4 = sb("V4", [128, NCH, 4, 32], F32, mem)
        part_max = sb("part_max", [128, 64, 2], F32, mem)
        neg_max = sb("neg_max", [128, 128], F32, mem)
        neg_hi = sb("neg_hi", [64, 128], F32R, mem)
        neg_lo = sb("neg_lo", [64, 128], F32R, mem)
        Pa = sb("Pa", [128, 4, 1024], F32, mem)
        Oa = sb("Oa", [128, 512], F32, mem)
        sum_inv = sb("sum_inv", [128, 512], F32, mem)
        On = sb("On", [128, 512], F32, mem)
        out_nat = sb("out_nat", [128, NCH, D], F32, mem)
        mem.close()

        mem = ExitStack()
        b_wq = sb("b_wq", [128, INNER], F32, mem)
        b_wkv = sb("b_wkv", [128, 512], F32, mem)
        b_wout = sb("b_wout", [128, 8, D], F32, mem)
        b_cols = sb("b_cols", [128, 6], F32, mem)
        b_w = sb("b_w", [128, 3, 128], F32, mem)
        b_wo = sb("b_wo", [128, D], F32, mem)
        z2 = sb("z2", [128, S], F32, mem)
        b_round = sb("b_round", [128, S], F32R, mem)
        b_part = sb("b_part", [128, S], F32, mem)
        QA = [sb(f"QA{i}", [128, S], F32R, mem) for i in range(2)]
        QB = [sb(f"QB{i}", [66, S], F32R, mem) for i in range(2)]
        KA = sb("KA", [128, S], F32R, mem)
        KB = sb("KB", [66, S], F32R, mem)
        Vb = sb("Vb", [128, NCH, 64], F32, mem)
        ones32 = sb("ones32", [128, 32], F32, mem)
        b_pmax = sb("b_pmax", [128, 32, 2], F32, mem)
        b_nmax = sb("b_nmax", [128, 128], F32, mem)
        b_hi = sb("b_hi", [32, 128], F32R, mem)
        b_lo = sb("b_lo", [32, 128], F32R, mem)
        Pb = sb("Pb", [128, 3, 1024], F32, mem)
        Oc = sb("Oc", [128, 1024], F32, mem)
        b_inv = sb("b_inv", [128, 512], F32, mem)
        Ob = sb("Ob", [128, 512], F32, mem)
        mem.close()

        mem = ExitStack()
        w_raw = sb("w_raw", [128, INNER], F32, mem)
        w_hi = sb("w_hi", [128, 3 * INNER], F32R, mem)
        w_lo = sb("w_lo", [128, 3 * INNER], F32R, mem)
        Wo = sb("Wo", [128, 8, D], F32, mem)
        W1 = sb("W1", [128, 2 * DFF], F32, mem)
        W2 = sb("W2", [128, 3, D], F32, mem)
        b1 = sb("b1", [128, 2, 3], F32, mem)
        ffn_cols = sb("ffn_cols", [128, 3], F32, mem)
        qk_scales = sb("qk_scales", [128, 4, DH], F32, mem)
        rot = [sb(f"rot{i}", [128, NCH * DH], F32, mem) for i in range(4)]
        x_hi = [sb(f"x_hi{i}", [128, 128], F32R, mem) for i in range(2)]
        x_lo = [sb(f"x_lo{i}", [128, 128], F32R, mem) for i in range(2)]
        raw_qk = sb("raw_qk", [128, 2 * INNER], F32, mem)
        raw = [raw_qk[:, 0:INNER], raw_qk[:, INNER:2 * INNER]]
        sq = sb("sq", [128, INNER], F32, mem)
        rot_out = [sb(f"rot_out{i}", [128, INNER], F32, mem) for i in range(2)]
        sin_qk = sb("sin_qk", [128, 2 * INNER], F32, mem)
        rot_sin = [sin_qk[:, 0:INNER], sin_qk[:, INNER:2 * INNER]]
        norm2 = [sb(f"norm2_{i}", [128, H], F32, mem) for i in range(2)]
        norm2c = [sb(f"norm2c_{i}", [128, H], F32, mem) for i in range(2)]
        inv_norm = [sb(f"inv_norm{i}", [128, H], F32, mem) for i in range(2)]
        qT = sb("qT", [128, 8, 128], F32, mem)
        kT = sb("kT", [128, 8, 160], F32, mem)
        V = [sb(f"V{i}", [128, INNER], F32, mem) for i in range(2)]
        VW = [sb(f"VW{i}", [128, 4, 512], F32, mem) for i in range(2)]
        row_max = sb("row_max", [128, H], F32, mem)
        row_sum = sb("row_sum", [128, H], F32, mem)
        row_inv = sb("row_inv", [128, H], F32, mem)
        probs = sb("probs", [128, INNER], F32, mem)
        probsT = sb("probsT", [128, 8, 128], F32, mem)
        Os = sb("Os", [128, INNER], F32, mem)
        OT = sb("OT", [128, 8, 128], F32, mem)
        gate = raw_qk[:, 0:1536].rearrange("p (j t) -> p j t", j=3)
        hidden = sin_qk[:, 0:1536].rearrange("p (j t) -> p j t", j=3)
        mem.close()

        names = ("consts_in x_in wa_in setup_pool setup_dve setup_act xm_done "
                 "ln_mean ln_centred ln_square ln_var ln_eps ln_pow ln_diag ln_bc ln_half ln_done "
                 "w_raw_in w_hi_done w_lo_done xh_done scales_in wo_in ffn_in tables_done xc_done "
                 "q_mm k_mm v_mm tq_mm tk_mm s_mm ot_mm y_mm pv_mm "
                 "q_copy k_copy q_evac k_evac qT_sb kT_cross kT_sb v_sb probs_exp ot_sb vs_in "
                 "nq_done nk_done aq_done ak_done bq_done bk_done cq_done ck_done iq_done ik_done "
                 "rq_done rk_done qn_done kn_done max_done sub_done pt_mm pt_sb sum_done inv_done on_done xb_done "
                 "w1_mm gelu_done hid_done w2_mm f_done stack_in stack_out "
                 "tr_x tr_wo wa_rows a_w a_qk a_round a_scaled a_split a_v a_vsb a_s1 a_max a_comb a_neg a_nt "
                 "a_hi a_lo a_dma a_s a_exp a_pv a_osb a_bc a_inv a_on a_y a_yadd "
                 "wb_in b_w_done b_mm b_ln b_rnd b_prt b_split b_v b_vsb b_s1 b_max b_comb b_neg b_nt b_his b_los b_dma b_s a_rows b_rows passed "
                 "b_exp b_pv b_invd b_on b_y b_yadd b_qb b_ones tr_out out_sb out_done self_act").split()
        s = {n: sem(n) for n in names}

        LN_A, LN_S0 = 0, int("A" in stages)
        LN_B = LN_S0 + (1 + DEPTH) * ("S0" in stages)
        LN_S1 = LN_B + 2 + 4 * 5
        block = ctx.enter_context(nc.Block())

        def pe_mean(pe, o, src):
            pe.matmul(o[:, 0:512], const("mean128"), src, start=True, stop=True).then_inc(s["ln_mean"], 1)

        def pe_var(pe, o, m, b):
            pe.wait_ge(s["ln_square"], START + m + 1)
            for c in range(4):
                mm = pe.matmul(o[:, 512 + c:513 + c], squares[:, b % 2, c * 128:c * 128 + 128],
                               const("mean128")[:, 0:1], start=True, stop=True)
            mm.then_inc(s["ln_var"], 1)

        def pe_spread(pe, o, m, b):
            pe.wait_ge(s["ln_diag"], START + m + 1)
            pe.matmul(o[:, 512:1024], ones[:, :], diag[:, b % 2, :], start=True, stop=True).then_inc(s["ln_bc"], 1)

        def act_square(act, m, b):
            act.wait_ge(s["ln_centred"], START + m + 1)
            act.wait_ge(s["ln_var"], START + (m - 1 if b >= 2 else m - b))
            act.activation(squares[:, b % 2, :], centred[:, b * 512:b * 512 + 512], ACT.Square)\
               .then_inc(s["ln_square"], 1)

        def pool_rstd(pool, m, b):
            pool.wait_ge(s["ln_eps"], START + m + 1)
            pool.tensor_tensor(rstd[:, 4 * b:4 * b + 4], variance[:, 4 * b:4 * b + 4], minus_half[:, 0:4], ALU.pow)\
                .then_inc(s["ln_pow"], 1)

        def dve_centre(dve, o, m, b, src):
            dve.wait_ge(s["ln_mean"], START + m + 1)
            dve.tensor_tensor(centred[:, b * 512:b * 512 + 512], src, o[:, 0:512], ALU.subtract)\
               .then_inc(s["ln_centred"], 1)

        def dve_eps(dve, o, m, b, eps):
            dve.wait_ge(s["ln_var"], START + m + 1)
            dve.tensor_scalar(variance[:, 4 * b:4 * b + 4], o[:, 512:516], eps, None, ALU.add)\
               .then_inc(s["ln_eps"], 1)

        def dve_diag(dve, m, b):
            dve.wait_ge(s["ln_pow"], START + m + 1)
            dve.wait_ge(s["ln_bc"], START + (m - 1 if b >= 2 else m - b))
            dve.tensor_tensor(diag[:, b % 2, :].rearrange("p (c t) -> p c t", c=4),
                              ident.unsqueeze(1).to_broadcast([128, 4, 128]),
                              rstd[:, 4 * b:4 * b + 4].unsqueeze(2).to_broadcast([128, 4, 128]), ALU.mult)\
               .then_inc(s["ln_diag"], 1)

        def dve_finish(dve, o, m, b, finish):
            dve.wait_ge(s["ln_bc"], START + m + 1)
            finish(b, centred[:, b * 512:b * 512 + 512], o[:, 512:1024])

        def pe_norm(pe, idx, src, ready):
            for b in range(NB):
                ready(b)
                pe_mean(pe, slot[b], src(b))
            for b in range(NB):
                pe_var(pe, slot[b], idx * NB + b, b)
            for b in range(NB):
                pe_spread(pe, slot[b], idx * NB + b, b)

        def act_norm(act, idx):
            for b in range(NB):
                act_square(act, idx * NB + b, b)

        def pool_norm(pool, idx):
            for b in range(NB):
                pool_rstd(pool, idx * NB + b, b)

        def dve_norm(dve, idx, src, eps, finish):
            n = idx * NB
            for b in range(NB):
                dve_centre(dve, slot[b], n + b, b, src(b))
            dve_eps(dve, slot[0], n, 0, eps)
            dve_eps(dve, slot[1], n + 1, 1, eps)
            dve_diag(dve, n, 0)
            dve_eps(dve, slot[2], n + 2, 2, eps)
            dve_diag(dve, n + 1, 1)
            dve_eps(dve, slot[3], n + 3, 3, eps)
            for b in range(NB):
                dve_finish(dve, slot[b], n + b, b, finish)
                if b + 2 < NB:
                    dve_diag(dve, n + b + 2, b + 2)

        def dve_affine(dve, idx, dst, g, bias):
            def finish(b, c, r):
                cols = slice(b * 512, b * 512 + 512)
                dve.tensor_tensor(dst[:, cols], c, r, ALU.mult).then_inc(s["ln_half"], 1)
                dve.wait_ge(s["ln_half"], START + idx * NB + b + 1)
                dve.tensor_scalar(dst[:, cols], dst[:, cols], g, bias, ALU.mult, ALU.add)\
                   .then_inc(s["ln_done"], 1)
            return finish

        def dve_plain(dve, idx, dst):
            def finish(b, c, r):
                dve.tensor_tensor(dst[:, b * 512:b * 512 + 512], c, r, ALU.mult).then_inc(s["ln_half"], 1)
                dve.wait_ge(s["ln_half"], START + idx * NB + b + 1)
                dve.sem_inc(s["ln_done"], 1)
            return finish

        LAST = NCH + 2

        def steps(eng, lam, step, start=0, end=LAST):
            def one(c, at=None):
                static = isinstance(c, int)
                at = c if static else at
                step(lam * NCH + c, c, at % 2, at < NCH, 1 <= at <= NCH, 2 <= at <= NCH + 1, at >= 3)
            if start < 3:
                for c in range(start, 3):
                    one(c)
                with eng.Fori(0, 6) as half:
                    one(half * 2 + 3, 3)
                    one(half * 2 + 4, 4)
                for c in range(15, end + 1):
                    one(c)
            else:
                for c in range(start, end + 1):
                    one(c)

        def back_to(g, c, k):
            return g - min(c, k) if isinstance(c, int) else g - k

        def sp_stack(sp, call):
            with sp.Fori(0, DEPTH) as L:
                lam = L + DEPTH * call
                for i in range(3):
                    if i == 0:
                        sp.wait_ge(s["w_lo_done"], START + 3 * lam)
                    else:
                        sp.wait_ge(s["w_lo_done"], START + 3 * lam + i)
                    sp.dma_start(w_raw[:, :], A["Wqkv"][bass.ds(L, 1), :, i * INNER:(i + 1) * INNER]
                                 .rearrange("a p n -> p (a n)")).then_inc(s["w_raw_in"], 16)
                    if i == 0:
                        sp.wait_ge(s["tables_done"], START + lam * 4)
                        for j, name in enumerate(("q_scale", "k_scale")):
                            row = A[name][bass.ds(L, 1), :].rearrange("a n -> (a n)")
                            sp.dma_start(qk_scales[:, 2 * j, :], row.partition_broadcast(128))\
                              .then_inc(s["scales_in"], 16)
                            for x in range(2):
                                sp.dma_start(qk_scales[:, 2 * j + 1, 32 * x:32 * x + 32],
                                             row[32 - 32 * x:64 - 32 * x].partition_broadcast(128))\
                                  .then_inc(s["scales_in"], 16)
                sp.wait_ge(s["y_mm"], START + lam * NCH)
                sp.dma_start(Wo[:, :, :], A["Wo"][bass.ds(L, 1), :, :].rearrange("a (j p) n -> p (a j) n", p=128))\
                  .then_inc(s["wo_in"], 16)
                sp.wait_ge(s["f_done"], START + lam * NB * 2)
                sp.dma_start(W1[:, :], A["W1"][bass.ds(L, 1), :, :].rearrange("a p n -> p (a n)"))\
                  .then_inc(s["ffn_in"], 16)
                for j, (a, n) in enumerate(FT):
                    sp.dma_start(W2[0:n, j, :], A["W2"][bass.ds(L, 1), a:a + n, :].rearrange("a p n -> p (a n)"))\
                      .then_inc(s["ffn_in"], 16)
                    for i in range(2):
                        sp.dma_start(b1[0:n, i, j:j + 1], A["b1"][bass.ds(L, 1), i * DFF + a:i * DFF + a + n]
                                     .rearrange("a p -> p a")).then_inc(s["ffn_in"], 16)
                for j, name in enumerate(("ln_g", "ln_b", "b2")):
                    sp.dma_start(ffn_cols[:, j:j + 1], A[name][bass.ds(L, 1), :].rearrange("a p -> p a"))\
                      .then_inc(s["ffn_in"], 16)

                def window_values(g, c, par, front, mid, late, back):
                    if not front:
                        return
                    sp.wait_ge(s["v_sb"], START + g + 1)
                    sp.sem_inc(s["passed"], 1)
                    sp.wait_ge(s["pv_mm"], START + back_to(g, c, 1))
                    for x in range(2):
                        cols = slice(512 * x, 512 * x + 512)
                        for w in range(1, 4):
                            sp.dma_start(VW[par][64 * x:64 * x + 64, w, :], V[par][32 * w - 32:32 * w + 32, cols])\
                              .then_inc(s["vs_in"], 16)
                        sp.dma_start(VW[par][64 * x:64 * x + 32, 0, :], V[1 - par][96:128, cols])\
                          .then_inc(s["vs_in"], 16)
                        sp.dma_start(VW[par][64 * x + 32:64 * x + 64, 0, :], V[par][0:32, cols])\
                          .then_inc(s["vs_in"], 16)
                steps(sp, lam, window_values)

        VS = 160

        def pe_stack(pe, call):
            n0 = LN_S0 if call == 0 else LN_S1
            with pe.Fori(0, DEPTH) as L:
                lam = L + DEPTH * call
                pe.wait_ge(s["w_lo_done"], START + (lam + 1) * 3)

                def project_in(o, par, third):
                    for i in range(2):
                        cols = slice(third * INNER + i * 512, third * INNER + (i + 1) * 512)
                        out = o[:, i * 512:(i + 1) * 512]
                        pe.matmul(out, x_hi[par][:, :], w_hi[:, cols], start=True, stop=False)
                        pe.matmul(out, x_hi[par][:, :], w_lo[:, cols], start=False, stop=False)
                        mm = pe.matmul(out, x_lo[par][:, :], w_hi[:, cols], start=False, stop=True)
                    return mm

                def step(g, c, par, front, mid, late, back):
                    if front:
                        pe.wait_ge(s["xc_done"], START + g + 1)
                        pe.wait_ge(s["q_evac"], START + g)
                        pe.wait_ge(s["kT_sb"], START + back_to(g, c, 1))
                        project_in(slot[0], par, 0).then_inc(s["q_mm"], 1)
                    if mid:
                        pe.wait_ge(s["qn_done"], START + g)
                        pe.wait_ge(s["xb_done"], START + 2 * back_to(g, c, 3))
                        for j in range(8):
                            mm = pe.transpose(slot[1][:, j * 128:(j + 1) * 128],
                                              rot_out[0][:, j * 128:(j + 1) * 128], ident)
                        mm.then_inc(s["tq_mm"], 1)
                    if front:
                        pe.wait_ge(s["v_sb"], START + g)
                        project_in(slot[3], par, 1).then_inc(s["k_mm"], 1)
                    if mid:
                        pe.wait_ge(s["kn_done"], START + g)
                        if front:
                            pe.wait_ge(s["q_evac"], START + g + 1)
                        for j in range(8):
                            mm = pe.transpose(slot[0][:, j * 128:(j + 1) * 128],
                                              rot_out[1][:, j * 128:(j + 1) * 128], ident)
                        mm.then_inc(s["tk_mm"], 1)
                    if late:
                        pe.wait_ge(s["probs_exp"], START + g - 1)
                        for j in range(8):
                            mm = pe.transpose(slot[2][:, j * 128:(j + 1) * 128],
                                              probs[:, j * 128:(j + 1) * 128], ident)
                        mm.then_inc(s["pt_mm"], 1)
                    if back:
                        pe.wait_ge(s["on_done"], START + g - 2)
                        if mid:
                            pe.wait_ge(s["qT_sb"], START + g)
                        else:
                            pe.wait_ge(s["xb_done"], START + 2 * (g - 3))
                        for j in range(8):
                            mm = pe.transpose(slot[1][:, j * 128:(j + 1) * 128],
                                              Os[:, j * 128:(j + 1) * 128], ident)
                        mm.then_inc(s["ot_mm"], 1)
                    if late:
                        pe.wait_ge(s["pt_sb"], START + g - 1)
                        pe.wait_ge(s["vs_in"], START + VS * (g - 1))
                        pe.sem_inc(s["passed"], 1)
                        for h in range(H):
                            r = slice(64 * (h % 2), 64 * (h % 2) + 64)
                            at = (h % 2) * 512 + (h // 2) * 64
                            for w in range(4):
                                mm = pe.matmul(slot[2][32 * w:32 * w + 32, at:at + 64],
                                               probsT[r, h // 2, 32 * w:32 * w + 32],
                                               VW[par][r, w, (h // 2) * 64:(h // 2) * 64 + 64],
                                               start=True, stop=True)
                        mm.then_inc(s["pv_mm"], 1)
                    if front:
                        pe.wait_ge(s["k_evac"], START + g + 1)
                        project_in(slot[3], par, 2).then_inc(s["v_mm"], 1)
                    if back:
                        pe.wait_ge(s["wo_in"], START + (lam + 1) * 16)
                        pe.wait_ge(s["ot_sb"], START + g - 2)
                        for j in range(8):
                            mm = pe.matmul(slot[1][:, 0:128], Wo[:, j, :], OT[:, j, :], start=(j == 0), stop=(j == 7))
                        mm.then_inc(s["y_mm"], 1)
                    if mid:
                        pe.wait_ge(s["qT_sb"], START + g)
                        pe.wait_ge(s["kT_sb"], START + g)
                        if late:
                            pe.wait_ge(s["on_done"], START + g - 1)
                        first = 0 if isinstance(c, int) and c == 1 else 1
                        for i in range(2):
                            pe.matmul(slot[2][:, i * 512:(i + 1) * 512], ident_b[:, :],
                                      mask_win[:, first:first + 1, :].to_broadcast([128, 8, 2 * WIN]),
                                      start=True, stop=False, skip_group_check=True)
                        for h in range(H):
                            r = 64 * (h % 2)
                            at = (h % 2) * 512 + (h // 2) * 64
                            for w in range(4):
                                mm = pe.matmul(slot[2][32 * w:32 * w + 32, at:at + 64],
                                               qT[r:r + 64, h // 2, 32 * w:32 * w + 32],
                                               kT[r:r + 64, h // 2, 32 * w:32 * w + 64],
                                               start=False, stop=True, skip_group_check=True)
                        mm.then_inc(s["s_mm"], 1)

                n = (n0 + 1 + L) * NB

                def mean(b):
                    if b == 0:
                        pe.wait_ge(s["kT_sb"], START + (lam + 1) * NCH)
                    pe.wait_ge(s["xb_done"], START + 2 * (lam * NCH) + 8 * (b + 1))
                    if b:
                        pe.wait_ge(s["ln_centred"], START + n + b)
                    pe_mean(pe, slot[0], XB[:, b * 512:b * 512 + 512])

                def var(b):
                    if b:
                        pe.wait_ge(s["ln_half"], START + n + b)
                    pe_var(pe, slot[0], n + b, b)
                steps(pe, lam, step, 0, NCH)
                mean(0)
                steps(pe, lam, step, NCH + 1, NCH + 1)
                var(0)
                steps(pe, lam, step, NCH + 2, NCH + 2)
                pe_spread(pe, slot[0], n, 0)
                pe.wait_ge(s["ffn_in"], START + (lam + 1) * 16 * 13)
                for b in range(NB):
                    f = lam * NB + b
                    if b + 1 < NB:
                        mean(b + 1)
                    pe.wait_ge(s["ln_done"], START + n + b + 1)
                    for j, (a, m) in enumerate(FT):
                        if b == 0 and j == 0:
                            pe.wait_ge(s["xb_done"], START + 2 * (lam + 1) * NCH)
                            pe.wait_ge(s["on_done"], START + (lam + 1) * NCH)
                            pe.wait_ge(s["v_sb"], START + (lam + 1) * NCH)
                        if b >= 1:
                            pe.wait_ge(s["hid_done"], START + (f - 1) * 3 + j + 1)
                            if j == 0:
                                pe.wait_ge(s["f_done"], START + 2 * f)
                        for i in range(2):
                            mm = pe.matmul(slot[j + 1][0:m, i * 512:(i + 1) * 512],
                                           W1[:, i * DFF + a:i * DFF + a + m], normed[:, b * 512:b * 512 + 512],
                                           start=True, stop=True)
                        mm.then_inc(s["w1_mm"], 1)
                        if j == 1 and b + 1 < NB:
                            var(b + 1)
                    if b + 1 < NB:
                        pe_spread(pe, slot[0], n + b + 1, b + 1)
                    for j, (a, m) in enumerate(FT):
                        pe.wait_ge(s["hid_done"], START + f * 3 + j + 1)
                        mm = pe.matmul(slot[1][:, 0:512], W2[0:m, j, :], hidden[0:m, j, :],
                                       start=(j == 0), stop=(j == 2))
                    mm.then_inc(s["w2_mm"], 1)

        def act_stack(act, call):
            n0 = LN_S0 if call == 0 else LN_S1
            with act.Fori(0, DEPTH) as L:
                lam = L + DEPTH * call
                for i in range(3):
                    act.wait_ge(s["w_raw_in"], START + 16 * (3 * lam + i + 1))
                    act.wait_ge(s["v_mm"], START + lam * NCH)
                    act.activation(w_hi[:, i * INNER:(i + 1) * INNER], w_raw[:, :], ACT.Copy)\
                       .then_inc(s["w_hi_done"], 1)

                def step(g, c, par, front, mid, late, back):
                    if front:
                        act.wait_ge(s["q_mm"], START + g + 1)
                        act.wait_ge(s["aq_done"], START + g)
                        act.wait_ge(s["bq_done"], START + g)
                        act.activation(raw[0], slot[0][:, :], ACT.Copy).then_inc(s["q_copy"], 1)
                    if late:
                        act.wait_ge(s["sub_done"], START + g - 1)
                        act.activation(probs[:, :], probs[:, :], ACT.Exp).then_inc(s["probs_exp"], 1)
                    if front:
                        act.wait_ge(s["ck_done"], START + g)
                        act.activation(sq[:, :], slot[0][:, :], ACT.Square).then_inc(s["q_evac"], 1)
                    if mid:
                        act.wait_ge(s["tq_mm"], START + g)
                        act.wait_ge(s["s_mm"], START + g - 1)
                        act.activation(qT[:, :, :].rearrange("p j t -> p (j t)"), slot[1][:, :], ACT.Copy)\
                           .then_inc(s["qT_sb"], 1)
                    if front:
                        act.wait_ge(s["k_mm"], START + g + 1)
                        act.wait_ge(s["ak_done"], START + g)
                        act.wait_ge(s["bk_done"], START + g)
                        act.activation(raw[1], slot[3][:, :], ACT.Copy).then_inc(s["k_copy"], 1)
                    if late:
                        act.wait_ge(s["pt_mm"], START + g - 1)
                        act.wait_ge(s["pv_mm"], START + back_to(g, c, 2))
                        act.activation(probsT[:, :, :].rearrange("p j t -> p (j t)"), slot[2][:, :], ACT.Copy)\
                           .then_inc(s["pt_sb"], 1)
                    if front:
                        act.wait_ge(s["cq_done"], START + g + 1)
                        act.activation(sq[:, :], slot[3][:, :], ACT.Square).then_inc(s["k_evac"], 1)
                    if mid:
                        act.wait_ge(s["kT_sb"], START + g - 1)
                        act.activation(kT[:, :, 0:32], kT[:, :, 128:160], ACT.Copy, scale=const("cross"))\
                           .then_inc(s["kT_cross"], 1)
                        act.wait_ge(s["tk_mm"], START + g)
                        act.wait_ge(s["kT_cross"], START + g)
                        act.activation(kT[:, :, 32:160], slot[0][:, :].rearrange("p (j t) -> p j t", j=8), ACT.Copy)\
                           .then_inc(s["kT_sb"], 1)
                    if back:
                        act.wait_ge(s["ot_mm"], START + g - 2)
                        act.wait_ge(s["y_mm"], START + back_to(g, c, 3))
                        act.activation(OT[:, :, :].rearrange("p j t -> p (j t)"), slot[1][:, :], ACT.Copy)\
                           .then_inc(s["ot_sb"], 1)
                    if front:
                        act.wait_ge(s["v_mm"], START + g + 1)
                        act.wait_ge(s["vs_in"], START + VS * g)
                        act.activation(V[par][:, :].rearrange("p (x j d) -> p j x d", x=2, d=DH),
                                       slot[3][:, :].rearrange("p (j x d) -> p j x d", x=2, d=DH), ACT.Copy)\
                           .then_inc(s["v_sb"], 1)
                n = (n0 + 1 + L) * NB
                steps(act, lam, step, 0, NCH)
                act_square(act, n, 0)
                steps(act, lam, step, NCH + 1, LAST)
                act.wait_ge(s["ffn_in"], START + (lam + 1) * 16 * 13)
                for b in range(NB):
                    f = lam * NB + b
                    if b + 1 < NB:
                        act_square(act, n + b + 1, b + 1)
                    for j, (a, m) in enumerate(FT):
                        act.wait_ge(s["w1_mm"], START + f * 3 + j + 1)
                        if b >= 1:
                            act.wait_ge(s["hid_done"], START + (f - 1) * 3 + j + 1)
                        act.activation(gate[0:m, j, :], slot[j + 1][0:m, 512:1024], ACT.Gelu,
                                       bias=b1[0:m, 1, j:j + 1]).then_inc(s["gelu_done"], 1)

        def pool_stack(pool, call):
            n0 = LN_S0 if call == 0 else LN_S1
            with pool.Fori(0, DEPTH) as L:
                lam = L + DEPTH * call
                for i in range(3):
                    cols = slice(i * INNER, (i + 1) * INNER)
                    pool.wait_ge(s["w_hi_done"], START + 3 * lam + i + 1)
                    pool.tensor_tensor(w_lo[:, cols], w_raw[:, :], w_hi[:, cols].bitcast(F32), ALU.subtract)\
                        .then_inc(s["w_lo_done"], 1)
                pool.wait_ge(s["tables_done"], START + 4 * (lam + 1))

                def sin_half(i, c, copied, done):
                    pool.wait_ge(*copied)
                    src = raw[i].rearrange("p (h x d) -> p h x d", h=H, x=2)
                    dst = rot_sin[i].rearrange("p (h x d) -> p h x d", h=H, x=2)
                    for x in range(2):
                        tab = rot[2 * i + 1][:, bass.ds(c * DH + 32 * x, 32)].unsqueeze(1).to_broadcast([128, H, 32])
                        ins = pool.tensor_tensor(dst[:, :, x, :], src[:, :, 1 - x, :], tab, ALU.mult)
                    ins.then_inc(s[done], 1)

                def inverse(i, g, n_done, used, done):
                    pool.wait_ge(s[n_done], START + g + 1)
                    pool.wait_ge(s[used], START + g)
                    pool.tensor_tensor(inv_norm[i][:, :], norm2c[i][:, :], minus_half[:, 0:H], ALU.pow)\
                        .then_inc(s[done], 1)

                def step(g, c, par, front, mid, late, back):
                    if front:
                        sin_half(0, c, (s["q_copy"], START + g + 1), "bq_done")
                        inverse(0, g, "nq_done", "qn_done", "iq_done")
                        pool.wait_ge(s["rk_done"], START + g)
                        sin_half(1, c, (s["k_copy"], START + g + 1), "bk_done")
                        pool.wait_ge(s["aq_done"], START + g + 1)
                        pool.wait_ge(s["bq_done"], START + g + 1)
                        pool.tensor_tensor(rot_out[0][:, :], rot_out[0][:, :], rot_sin[0], ALU.add)\
                            .then_inc(s["rq_done"], 1)
                        inverse(1, g, "nk_done", "kn_done", "ik_done")
                steps(pool, lam, step)
                for b in range(NB):
                    pool_rstd(pool, (n0 + 1 + L) * NB + b, b)

        def dve_stack(dve, call):
            n0 = LN_S0 if call == 0 else LN_S1
            with dve.Fori(0, DEPTH) as L:
                lam = L + DEPTH * call

                def take_chunk(g, c, par, used):
                    dve.wait_ge(s["v_mm"], START + used)
                    x = XA[:, bass.ds(c * 128, 128)]
                    dve.tensor_copy(x_hi[par][:, :], x).then_inc(s["xh_done"], 1)
                    dve.wait_ge(s["xh_done"], START + g + 1)
                    dve.tensor_tensor(x_lo[par][:, :], x, x_hi[par][:, :].bitcast(F32), ALU.subtract)\
                       .then_inc(s["xc_done"], 1)
                dve.wait_ge(s["stack_in"], START + NB * (call + 1) * 2)
                dve.wait_ge(s["f_done"], START + 2 * NB * lam)
                take_chunk(lam * NCH, 0, 0, lam * NCH)
                dve.wait_ge(s["scales_in"], START + (lam + 1) * 96)
                dve.wait_ge(s["bk_done"], START + lam * NCH)
                for i, name in enumerate(("rot_q_cos", "rot_q_sin", "rot_k_cos", "rot_k_sin")):
                    dve.tensor_tensor(rot[i][:, :].rearrange("p (c d) -> p c d", d=DH),
                                      const(name).rearrange("p (c d) -> p c d", d=DH),
                                      qk_scales[:, i:i + 1, :].to_broadcast([128, NCH, DH]), ALU.mult)\
                       .then_inc(s["tables_done"], 1)
                dve.wait_ge(s["tables_done"], START + 4 * (lam + 1))

                def heads(a):
                    return a.rearrange("p (h d) -> p h d", h=H)

                def cos_half(i, g, c, copied, used, done):
                    dve.wait_ge(s[copied], START + g + 1)
                    dve.wait_ge(s[used], START + g)
                    tab = rot[2 * i][:, bass.ds(c * DH, DH)].unsqueeze(1).to_broadcast([128, H, DH])
                    dve.tensor_tensor(heads(rot_out[i][:, :]), heads(raw[i]), tab, ALU.mult).then_inc(s[done], 1)

                def norm_squared(i, g, squared, summed, used, done):
                    dve.wait_ge(s[squared], START + g + 1)
                    dve.tensor_reduce(norm2[i][:, :], heads(sq[:, :]), AX.X, ALU.add).then_inc(s[summed], 1)
                    dve.wait_ge(s[summed], START + g + 1)
                    dve.wait_ge(s[used], START + g)
                    dve.tensor_scalar(norm2c[i][:, :], norm2[i][:, :], 1e-24, None, ALU.max)\
                       .then_inc(s[done], 1)

                def normalise(i, g, summed, inverted, done):
                    dve.wait_ge(s[summed], START + g + 1)
                    dve.wait_ge(s[inverted], START + g + 1)
                    v = heads(rot_out[i][:, :])
                    dve.tensor_tensor(v, v, inv_norm[i][:, :].unsqueeze(2).to_broadcast([128, H, DH]), ALU.mult)\
                       .then_inc(s[done], 1)

                def step(g, c, par, front, mid, late, back):
                    by_bank = slot[2][:, :].rearrange("p (x j k) -> p j x k", x=2, k=64)
                    if late:
                        dve.wait_ge(s["s_mm"], START + g - 1)
                        dve.tensor_reduce(row_max[:, :], slot[2][:, :].rearrange("p (h k) -> p h k", h=H),
                                          AX.X, ALU.max).then_inc(s["max_done"], 1)
                        dve.wait_ge(s["max_done"], START + g - 1)
                        dve.wait_ge(s["pt_mm"], START + back_to(g, c, 2))
                        dve.tensor_tensor(probs[:, :].rearrange("p (j x k) -> p j x k", x=2, k=64), by_bank,
                                          row_max[:, :].rearrange("p (x j) -> p j x", x=2).unsqueeze(3)
                                          .to_broadcast([128, 8, 2, 64]), ALU.subtract).then_inc(s["sub_done"], 1)
                    if front:
                        cos_half(0, g, c, "q_copy", "tq_mm", "aq_done")
                        norm_squared(0, g, "q_evac", "cq_done", "iq_done", "nq_done")
                    if late:
                        dve.wait_ge(s["probs_exp"], START + g - 1)
                        dve.tensor_reduce(row_sum[:, :], heads(probs[:, :]), AX.X, ALU.add).then_inc(s["sum_done"], 1)
                        dve.wait_ge(s["sum_done"], START + g - 1)
                        dve.reciprocal(row_inv[:, :], row_sum[:, :]).then_inc(s["inv_done"], 1)
                    if front:
                        cos_half(1, g, c, "k_copy", "tk_mm", "ak_done")
                        norm_squared(1, g, "k_evac", "ck_done", "ik_done", "nk_done")
                    if late:
                        dve.wait_ge(s["pv_mm"], START + g - 1)
                        dve.wait_ge(s["inv_done"], START + g - 1)
                        dve.wait_ge(s["ot_mm"], START + back_to(g, c, 2))
                        dve.tensor_tensor(Os[:, :].rearrange("p (j x d) -> p j x d", x=2, d=DH), by_bank,
                                          row_inv[:, :].rearrange("p (j x) -> p j x", x=2).unsqueeze(3)
                                          .to_broadcast([128, 8, 2, DH]), ALU.mult).then_inc(s["on_done"], 1)
                    if front:
                        dve.wait_ge(s["ak_done"], START + g + 1)
                        dve.wait_ge(s["bk_done"], START + g + 1)
                        dve.tensor_tensor(rot_out[1][:, :], rot_out[1][:, :], rot_sin[1], ALU.add)\
                           .then_inc(s["rk_done"], 1)
                    if back:
                        dve.wait_ge(s["y_mm"], START + g - 2)
                        t0 = (c - 3) * 128
                        for p, o in ((slice(0, 64), 0), (slice(64, 128), 1)):
                            dve.tensor_tensor(XB[p, bass.ds(t0 + o, 128)], XA[p, bass.ds(t0 + o, 128)],
                                              slot[1][p, 0:128], ALU.add).then_inc(s["xb_done"], 1)
                    if front:
                        normalise(0, g, "rq_done", "iq_done", "qn_done")
                        if not isinstance(c, int) or c < NCH - 1:
                            take_chunk(g + 1, c + 1, 1 - par, back_to(g, c, 0))
                        normalise(1, g, "rk_done", "ik_done", "kn_done")

                idx = n0 + 1 + L
                n = idx * NB
                finish = dve_affine(dve, idx, normed, ffn_cols[:, 0:1], ffn_cols[:, 1:2])

                def centre(b):
                    dve.wait_ge(s["xb_done"], START + 2 * (lam * NCH) + 8 * (b + 1))
                    dve_centre(dve, slot[0], n + b, b, XB[:, b * 512:b * 512 + 512])
                steps(dve, lam, step, 0, NCH)
                centre(0)
                steps(dve, lam, step, NCH + 1, NCH + 1)
                dve_eps(dve, slot[0], n, 0, 1e-5)
                steps(dve, lam, step, NCH + 2, NCH + 2)
                dve_diag(dve, n, 0)
                dve.wait_ge(s["ffn_in"], START + (lam + 1) * 16 * 13)
                dve_finish(dve, slot[0], n, 0, finish)
                for b in range(NB):
                    f = lam * NB + b
                    if b + 1 < NB:
                        centre(b + 1)
                    for j, (a, m) in enumerate(FT):
                        dve.wait_ge(s["gelu_done"], START + f * 3 + j + 1)
                        dve.wait_ge(s["w2_mm"], START + f)
                        dve.scalar_tensor_tensor(out=hidden[0:m, j, :], in0=slot[j + 1][0:m, 0:512],
                                                 scalar=b1[0:m, 0, j:j + 1], in1=gate[0:m, j, :],
                                                 op0=ALU.add, op1=ALU.mult).then_inc(s["hid_done"], 1)
                        if j == 1 and b + 1 < NB:
                            dve_eps(dve, slot[0], n + b + 1, b + 1, 1e-5)
                            dve_diag(dve, n + b + 1, b + 1)
                    if b + 1 < NB:
                        dve_finish(dve, slot[0], n + b + 1, b + 1, finish)
                    dve.wait_ge(s["w2_mm"], START + f + 1)
                    for p, o in ((slice(0, 64), 0), (slice(64, 128), 1)):
                        cols = slice(b * 512 + o, b * 512 + o + 512)
                        dve.scalar_tensor_tensor(out=XA[p, cols], in0=slot[1][p, 0:512], scalar=ffn_cols[p, 2:3],
                                                 in1=XB[p, cols], op0=ALU.add, op1=ALU.add).then_inc(s["f_done"], 1)
            dve.wait_ge(s["f_done"], START + 2 * NB * DEPTH * (call + 1))
            for b in range(NB):
                for p, o in ((slice(0, 64), 0), (slice(64, 128), 1)):
                    dve.tensor_tensor(XM[p, b * 512:b * 512 + 512], XM[p, b * 512:b * 512 + 512],
                                      XA[p, b * 512 + o:b * 512 + o + 512], ALU.add).then_inc(s["xm_done"], 1)

        A_PE_ROWS = 24
        XM0 = 8 * ("S0" in stages)
        QB_UNITS = [4 * q + 4 for q in range(NB)]
        A_UNITS = sum(QB_UNITS)
        A_TILES = [(i, u) for i in range(NCH) for u in range(1 + (i >= 8))]
        PER_HEAD = len(A_TILES)

        def sp_setup(sp):
            sp.dma_start(consts[:, :], A["shape_constants"]).then_inc(s["consts_in"], 16)
            sp.dma_start(x_nat[:, :, :], A["x"][0].rearrange("(c p) d -> p c d", p=128)).then_inc(s["x_in"], 16)
            sp.dma_start(wqkv_nat[:, :, :], A["w_qkv"].rearrange("(c p) d -> p c d", p=128)).then_inc(s["wa_in"], 16)
            sp.dma_start(wout_nat[:, :], A["w_out"]).then_inc(s["wa_in"], 16)

        def pool_setup(pool):
            pool.memset(minus_half[:, :], -0.5).then_inc(s["setup_pool"], 1)
            pool.memset(ones[:, :], 1.0).then_inc(s["setup_pool"], 1)
            pool.memset(V4[:, :, :, :], 0.0).then_inc(s["setup_pool"], 1)
            pool.wait_ge(s["setup_pool"], START + 3)
            pool.memset(V4[:, :, :, 8:9], 1.0).then_inc(s["setup_pool"], 1)
            pool.wait_ge(s["setup_pool"], START + 4)

        def pe_setup(pe):
            pe.wait_ge(s["consts_in"], START + 16)
            pe.wait_ge(s["x_in"], START + 16)
            for c in range(NCH):
                mm = pe.transpose(slot[c // 8][:, (c % 8) * 128:(c % 8) * 128 + 128], x_nat[:, c, :], ident)
            mm.then_inc(s["tr_x"], 1)
            pe.wait_ge(s["wa_in"], START + 32)
            for c in range(3):
                mm = pe.transpose(slot[2][:, c * 128:(c + 1) * 128], wqkv_nat[:, c, :], ident)
            mm.then_inc(s["tr_x"], 1)
            pe.wait_ge(s["wa_rows"], START + 1)
            for g in range(4):
                mm = pe.transpose(slot[3][:, g * 128:(g + 1) * 128],
                                  wout_pad[:, 4 * g:4 * g + 4, :].rearrange("p h r -> p (h r)"), ident)
            mm.then_inc(s["tr_wo"], 1)

        def act_setup(act):
            act.wait_ge(s["tr_x"], START + 1)
            for i in range(2):
                act.activation(XM[:, i * 1024:(i + 1) * 1024], slot[i][:, :], ACT.Copy).then_inc(s["setup_act"], 1)
            act.wait_ge(s["tr_wo"], START + 1)
            act.activation(wout_rows[:, :, :].rearrange("p g n -> p (g n)"), slot[3][:, 0:512], ACT.Copy)\
               .then_inc(s["setup_act"], 1)

        def dve_setup(dve):
            dve.memset(wq_rows[:, :, :], 0.0)
            dve.memset(wk_rows[:, :, :], 0.0)
            dve.memset(wout_pad[:, :, :], 0.0)
            dve.memset(part_max[:, :, :], -3.0e38)
            dve.memset(neg_max[:, :], 0.0)
            dve.memset(XA[64:128, 0:1], 0.0)
            dve.memset(XB[64:128, 0:1], 0.0).then_inc(s["setup_dve"], 1)
            dve.wait_ge(s["setup_dve"], START + 1)
            dve.wait_ge(s["wa_in"], START + 32)
            dve.tensor_copy(wout_pad[:, :, 0:AH], wout_nat[:, :].rearrange("p (h d) -> p h d", d=AH))\
               .then_inc(s["wa_rows"], 1)
            dve.wait_ge(s["consts_in"], START + 16)
            dve.tensor_copy(ident_b[:, :], ident)
            dve.tensor_copy(mask_qk[:, :], const("mask_qk"))
            dve.tensor_copy(mask_kq[:, :], const("mask_kq"))
            dve.tensor_copy(mask_win[:, :, :], const("mask_win").rearrange("p (a k) -> p a k", a=2))\
               .then_inc(s["setup_dve"], 1)
            dve.wait_ge(s["tr_x"], START + 2)
            wt = slot[2][:, 0:384].rearrange("p (c h d) -> p c h d", c=3, d=AH)
            for rep in range(3):
                rows = slice(AH * rep, AH * rep + AH)
                dve.tensor_scalar(wq_rows[:, :, rows], wt[:, 0], AH ** -0.5, None, ALU.mult)
                dve.tensor_copy(wk_rows[:, :, rows], wt[:, 1])
            dve.tensor_copy(wv_cols[:, :], slot[2][:, 256:384]).then_inc(s["setup_dve"], 1)

        def sp_first(sp):
            with sp.Fori(0, 4) as g:
                sp.wait_ge(s["a_hi"], START + g + 1)
                sp.sem_inc(s["passed"], 1)
                sp.wait_ge(s["a_lo"], START + g + 1)
                for j, src in enumerate((neg_hi, neg_lo)):
                    sp.dma_start(rows_dram[j], src[:, :].bitcast(F32)).then_inc(s["a_rows"], 16)
                sp.wait_ge(s["a_rows"], START + 32 * (g + 1))
                for hh in range(4):
                    for j in range(2):
                        r = 32 * hh + A_PE_ROWS + j
                        sp.dma_start(QT[r:r + 1, :].bitcast(F32),
                                     rows_dram[j:j + 1, 16 * hh:16 * hh + 16, :].rearrange("a i t -> a (i t)"))\
                          .then_inc(s["a_dma"], 16)

        def pe_first(pe):
            pe_norm(pe, LN_A, lambda b: XM[:, b * 512:b * 512 + 512],
                    lambda b: (pe.wait_ge(s["setup_act"], START + 3), pe.wait_ge(s["setup_dve"], START + 3),
                               pe.wait_ge(s["setup_pool"], START + 4)))
            pe.wait_ge(s["ln_done"], START + NB)
            with pe.Fori(0, 4) as g:
                pe.wait_ge(s["a_w"], START + g + 1)
                for b in range(NB):
                    if b == 3:
                        pe.wait_ge(s["a_yadd"], START + 4 * g)
                    for i, w in enumerate((gq_w, gk_w)):
                        mm = pe.matmul(slot[b][:, i * 512:(i + 1) * 512], w[:, :], normed[:, b * 512:b * 512 + 512],
                                       start=True, stop=True)
                    mm.then_inc(s["a_qk"], 1)
                pe.wait_ge(s["a_split"], START + 4 * g + 1)
                for k in range(NCH):
                    mm = pe.matmul(slot[0][:, 32 * k:32 * k + 32], normed[:, k * 128:k * 128 + 128], gv_w[:, :],
                                   start=True, stop=True)
                mm.then_inc(s["a_v"], 1)
                pe.wait_ge(s["a_vsb"], START + g + 1)
                pe.wait_ge(s["a_split"], START + 4 * g + 4)
                n = 0
                for hh in range(4):
                    rows = slice(32 * hh, 32 * hh + A_PE_ROWS)
                    for i, u in A_TILES:
                        if n >= 4:
                            pe.wait_ge(s["a_max"], START + 4 * PER_HEAD * g + n - 3)
                        width = min(1024, 128 * (i + 1) - 1024 * u)
                        last = 128 * (i + 1) - 1024 * u <= 1024
                        for a in range(0, width, 512):
                            m = min(512, width - a)
                            diag = last and a + m == width
                            mm = pe.matmul(slot[n % 4][:, a:a + m], QT[rows, 128 * i:128 * i + 128],
                                           KT[rows, 1024 * u + a:1024 * u + a + m], start=True, stop=True)
                            if diag:
                                mm = pe.matmul(slot[n % 4][:, width - 128:width], ident_b[:, :], mask_qk[:, :],
                                               start=False, stop=True, skip_group_check=True)
                        mm.then_inc(s["a_s1"], 1)
                        n += 1
                pe.wait_ge(s["a_neg"], START + g + 1)
                pe.transpose(slot[0][:, 0:128], neg_max[:, :], ident).then_inc(s["a_nt"], 1)
                pe.wait_ge(s["a_dma"], START + 128 * (g + 1))
                units = [(qb, k) for qb in range(NB) for k in range(QB_UNITS[qb])]

                def scores(n):
                    qb, k = units[n]
                    c0 = max(0, 128 * (k - 4 * qb))
                    for half in range(2):
                        h2 = 2 * n + half
                        if h2 >= 3:
                            pe.wait_ge(s["a_exp"], START + 2 * A_UNITS * g + h2 - 2)
                        for e in range(2):
                            hh = 2 * half + e
                            rows = slice(32 * hh, 32 * hh + A_PE_ROWS + 2)
                            diag = k >= 4 * qb
                            o = slot[h2 % 3]
                            mm = pe.matmul(o[:, 512 * e + c0:512 * e + 512], KT[rows, 128 * k:128 * k + 128],
                                           QT[rows, 512 * qb + c0:512 * qb + 512], start=True, stop=True)
                            if diag:
                                mm = pe.matmul(o[:, 512 * e + c0:512 * e + c0 + 128], ident_b[:, :], mask_kq[:, :],
                                               start=False, stop=True, skip_group_check=True)
                        mm.then_inc(s["a_s"], 1)

                def values(n):
                    qb, k = units[n]
                    c0 = max(0, 128 * (k - 4 * qb))
                    pe.wait_ge(s["a_exp"], START + 2 * A_UNITS * g + 2 * n + 2)
                    if k == 0:
                        pe.wait_ge(s["a_osb"], START + 4 * g + qb)
                    for hh in range(4):
                        mm = pe.matmul(slot[3][32 * hh:32 * hh + 32, c0:512], V4[:, k, hh, :],
                                       Pa[:, (2 * n + hh // 2) % 4, 512 * (hh % 2) + c0:512 * (hh % 2) + 512],
                                       start=(k == 0), stop=(k >= 4 * qb), skip_group_check=True)
                    mm.then_inc(s["a_pv"], 1)

                def sums(qb):
                    pe.wait_ge(s["a_osb"], START + 4 * g + qb + 1)
                    pe.wait_ge(s["a_yadd"], START + 4 * g + qb)
                    pe.matmul(slot[3][:, 512:1024], const("sum_rows"), Oa[:, :], start=True, stop=True)\
                      .then_inc(s["a_bc"], 1)

                def project(qb):
                    pe.wait_ge(s["a_on"], START + 4 * g + qb + 1)
                    pe.matmul(slot[3][:, 512:1024], go_w[:, :], On[:, :], start=True, stop=True)\
                      .then_inc(s["a_y"], 1)

                scores(0)
                for n, (qb, k) in enumerate(units):
                    if n + 1 < len(units):
                        scores(n + 1)
                    values(n)
                    if qb >= 1 and k == 1:
                        sums(qb - 1)
                    if qb >= 1 and k == 5:
                        project(qb - 1)
                sums(NB - 1)
                project(NB - 1)

        def act_first(act):
            act.wait_ge(s["setup_pool"], START + 4)
            act_norm(act, LN_A)
            with act.Fori(0, 4) as g:
                for b in range(NB):
                    act.wait_ge(s["a_qk"], START + 4 * g + b + 1)
                    act.activation(rounded[:, b % 2, :], slot[b][:, :], ACT.Copy).then_inc(s["a_round"], 1)
                    act.wait_ge(s["a_round"], START + 4 * g + b + 1)
                    act.wait_ge(s["a_split"], START + 4 * g + (b - 1 if b >= 2 else 0))
                    act.activation(scaled[:, b % 2, 0:512], rounded[:, b % 2, 0:512].bitcast(F32), ACT.Copy,
                                   scale=const("rows")[:, 0:1])
                    act.activation(scaled[:, b % 2, 512:1024], rounded[:, b % 2, 512:1024].bitcast(F32),
                                   ACT.Identity, scale=const("rows")[:, 2:3], bias=const("rows")[:, 4:5])\
                       .then_inc(s["a_scaled"], 1)
                act.wait_ge(s["a_v"], START + g + 1)
                act.wait_ge(s["a_pv"], START + A_UNITS * g)
                act.activation(V4[:, :, :, 0:AH].rearrange("p k h d -> p (k h) d"),
                               slot[0][:, 0:512].rearrange("p (x d) -> p x d", d=AH), ACT.Copy)\
                   .then_inc(s["a_vsb"], 1)
                act.wait_ge(s["a_nt"], START + g + 1)
                act.wait_ge(s["a_dma"], START + 128 * g)
                act.activation(neg_hi[:, :], slot[0][0:64, 0:128], ACT.Copy).then_inc(s["a_hi"], 1)
                units = [(qb, k) for qb in range(NB) for k in range(QB_UNITS[qb])]

                def take_output(qb):
                    act.wait_ge(s["a_pv"], START + A_UNITS * g + sum(QB_UNITS[:qb + 1]))
                    act.wait_ge(s["a_on"], START + 4 * g + qb)
                    act.activation(Oa[:, :], slot[3][:, 0:512], ACT.Copy).then_inc(s["a_osb"], 1)
                for n, (qb, k) in enumerate(units):
                    c0 = max(0, 128 * (k - 4 * qb))
                    for half in range(2):
                        h2 = 2 * n + half
                        act.wait_ge(s["a_s"], START + 2 * A_UNITS * g + h2 + 1)
                        if n >= 2:
                            act.wait_ge(s["a_pv"], START + A_UNITS * g + n - 1)
                        act.activation(Pa[:, h2 % 4, :].rearrange("p (e q) -> p e q", e=2)[:, :, c0:512],
                                       slot[h2 % 3][:, :].rearrange("p (e q) -> p e q", e=2)[:, :, c0:512],
                                       ACT.Exp).then_inc(s["a_exp"], 1)
                    if qb >= 1 and k == 0:
                        take_output(qb - 1)
                take_output(NB - 1)

        def dve_first(dve):
            dve.wait_ge(s["setup_act"], START + 2)
            dve_norm(dve, LN_A, lambda b: XM[:, b * 512:b * 512 + 512], 1e-5, dve_plain(dve, LN_A, normed))
            dve.wait_ge(s["setup_act"], START + 3)
            dve.wait_ge(s["setup_dve"], START + 3)
            with dve.Fori(0, 4) as g:
                dve.wait_ge(s["a_y"], START + 4 * g)
                dve.tensor_copy(gq_w[:, :], wq_rows[:, :, :].rearrange("p h r -> p (h r)")[:, bass.ds(g * 128, 128)])
                dve.tensor_copy(gk_w[:, :], wk_rows[:, :, :].rearrange("p h r -> p (h r)")[:, bass.ds(g * 128, 128)])
                dve.tensor_copy(gv_w[:, :], wv_cols[:, bass.ds(g * 32, 32)])
                dve.tensor_copy(go_w[:, :], wout_rows[:, :, :].rearrange("p g n -> p (g n)")[:, bass.ds(g * 128, 128)])\
                   .then_inc(s["a_w"], 1)
                for b in range(NB):
                    dve.wait_ge(s["a_scaled"], START + 4 * g + b + 1)
                    cols = slice(b * 512, b * 512 + 512)
                    dve.scalar_tensor_tensor(out=QT[:, cols], in0=slot[b][:, 0:512], scalar=const("rows")[:, 1:2],
                                             in1=scaled[:, b % 2, 0:512], op0=ALU.mult, op1=ALU.add)
                    dve.scalar_tensor_tensor(out=KT[:, cols], in0=slot[b][:, 512:1024], scalar=const("rows")[:, 3:4],
                                             in1=scaled[:, b % 2, 512:1024], op0=ALU.mult, op1=ALU.add)\
                       .then_inc(s["a_split"], 1)
                n = 0
                for hh in range(4):
                    for i, u in A_TILES:
                        width = min(1024, 128 * (i + 1) - 1024 * u)
                        dve.wait_ge(s["a_s1"], START + 4 * PER_HEAD * g + n + 1)
                        dve.tensor_reduce(part_max[:, 16 * hh + i, u:u + 1], slot[n % 4][:, 0:width], AX.X, ALU.max)\
                           .then_inc(s["a_max"], 1)
                        n += 1
                dve.wait_ge(s["a_max"], START + 4 * PER_HEAD * (g + 1))
                dve.wait_ge(s["a_nt"], START + g)
                dve.tensor_tensor(neg_max[:, 0:64], part_max[:, :, 0], part_max[:, :, 1], ALU.max)\
                   .then_inc(s["a_comb"], 1)
                dve.wait_ge(s["a_comb"], START + g + 1)
                dve.tensor_scalar(neg_max[:, 0:64], neg_max[:, 0:64], -1.0, None, ALU.mult).then_inc(s["a_neg"], 1)
                dve.wait_ge(s["a_hi"], START + g + 1)
                dve.tensor_tensor(neg_lo[:, :], slot[0][0:64, 0:128], neg_hi[:, :].bitcast(F32), ALU.subtract)\
                   .then_inc(s["a_lo"], 1)
                for qb in range(NB):
                    dve.wait_ge(s["a_bc"], START + 4 * g + qb + 1)
                    dve.reciprocal(sum_inv[:, :], slot[3][:, 512:1024]).then_inc(s["a_inv"], 1)
                    dve.wait_ge(s["a_inv"], START + 4 * g + qb + 1)
                    dve.tensor_tensor(On[:, :], Oa[:, :], sum_inv[:, :], ALU.mult).then_inc(s["a_on"], 1)
                    dve.wait_ge(s["a_y"], START + 4 * g + qb + 1)
                    cols = slice(qb * 512, qb * 512 + 512)
                    dve.tensor_tensor(XM[:, cols], XM[:, cols], slot[3][:, 512:1024], ALU.add)\
                       .then_inc(s["a_yadd"], 1)

        def xm_ready(eng, call):
            if call == 0:
                eng.wait_ge(s["a_yadd"], START + (16 if "A" in stages else 0))
                eng.wait_ge(s["setup_act"], START + 3)
                eng.wait_ge(s["setup_dve"], START + 3)
            else:
                eng.wait_ge(s["b_yadd"], START + (32 if "B" in stages else 0))
                eng.wait_ge(s["xm_done"], START + XM0)

        def ln_into(call):
            return LN_S0 if call == 0 else LN_S1

        def pe_into(pe, call):
            pe_norm(pe, ln_into(call), lambda b: XM[:, b * 512:b * 512 + 512],
                    lambda b: xm_ready(pe, call))

        def dve_into(dve, call):
            n = ln_into(call)
            xm_ready(dve, call)

            def finish(b, c, r):
                dve.wait_ge(s["stack_in"], START + 8 * call)
                for p, o in ((slice(0, 64), 0), (slice(64, 128), 1)):
                    ins = dve.tensor_tensor(XA[p, b * 512 + o:b * 512 + o + 512], c[p], r[p], ALU.mult)
                    ins.then_inc(s["stack_in"], 1)
                dve.wait_ge(s["stack_in"], START + 8 * call + 2 * b + 2)
                dve.sem_inc(s["ln_half"], 1)
                dve.sem_inc(s["ln_done"], 1)
            dve_norm(dve, n, lambda b: XM[:, b * 512:b * 512 + 512], 1e-5, finish)
            dve.memset(kT[:, :, :], 0.0)
            dve.memset(V[1][:, :], 0.0).then_inc(s["stack_out"], 1)

        def sp_grouped(sp):
            sp.wait_ge(s["xm_done"], START + XM0)
            sp.dma_start(b_wq[:, :], A["Wq"]).then_inc(s["wb_in"], 16)
            sp.dma_start(b_wkv[:, :], A["Wkv"]).then_inc(s["wb_in"], 16)
            sp.dma_start(b_wout[:, :, :], A["Wout"].rearrange("(j p) n -> p j n", p=128)).then_inc(s["wb_in"], 16)
            for j, name in enumerate(("b_ln_scale", "b_ln_bias")):
                sp.dma_start(b_cols[:, j:j + 1], A[name].rearrange("(p a) -> p a", a=1)).then_inc(s["wb_in"], 16)
            for j, name in enumerate(("qn_scale", "qn_bias", "kn_scale", "kn_bias")):
                for r in range(2):
                    sp.dma_start(b_cols[64 * r:64 * r + 64, j + 2:j + 3], A[name].rearrange("(p a) -> p a", a=1))\
                      .then_inc(s["wb_in"], 16)
            with sp.Fori(0, 8) as p:
                sp.wait_ge(s["b_his"], START + p + 1)
                sp.sem_inc(s["passed"], 1)
                sp.wait_ge(s["b_los"], START + p + 1)
                for j, src in enumerate((b_hi, b_lo)):
                    sp.dma_start(rows_dram[j, 0:32, :], src[:, :].bitcast(F32)).then_inc(s["b_rows"], 16)
                sp.wait_ge(s["b_rows"], START + 32 * (p + 1))
                for hh in range(2):
                    for j in range(2):
                        sp.dma_start(QB[hh][64 + j:65 + j, :].bitcast(F32),
                                     rows_dram[j:j + 1, 16 * hh:16 * hh + 16, :].rearrange("a i t -> a (i t)"))\
                          .then_inc(s["b_dma"], 16)

        WB_IN = 16 * 13
        def ln_k(kv):
            return LN_B + 2 + 5 * kv

        def ln_q(kv, pr, hh):
            return LN_B + 2 + 5 * kv + 1 + 2 * pr + hh

        def b_ring():
            entries = []
            for n in range(64):
                entries.append(("s", n))
                if n % 16 == 6 and n >= 16:
                    entries.append(("y", n // 16 - 1))
            entries.append(("y", NB - 1))
            place_of, before = {}, {}
            for m, e in enumerate(entries):
                place_of[e] = m % 3
                before[e] = entries[m - 3] if m >= 3 else None
            return entries, place_of, before

        B_ENTRIES, B_PLACE, B_BEFORE = b_ring()

        def ring_free(pe, e, p):
            b = B_BEFORE[e]
            if b is not None:
                pe.wait_ge(s["b_exp"] if b[0] == "s" else s["b_yadd"],
                           START + (64 if b[0] == "s" else NB) * p + b[1] + 1)

        def pe_head(pe, n, mm_before, which):
            for b in range(NB):
                mm = pe.matmul(slot[b][:, 0:512], b_w[:, which, :], z2[:, b * 512:b * 512 + 512],
                               start=True, stop=True)
                mm.then_inc(s["b_mm"], 1)
            pe_norm(pe, n, lambda b: b_part[:, b * 512:b * 512 + 512],
                    lambda b: pe.wait_ge(s["b_qb"], START + mm_before + b + 1))

        def pe_grouped(pe):
            pe_norm(pe, LN_B, lambda b: XM[:, b * 512:b * 512 + 512],
                    lambda b: pe.wait_ge(s["xm_done"], START + XM0))
            pe_norm(pe, LN_B + 1, lambda b: normed[:, b * 512:b * 512 + 512],
                    lambda b: pe.wait_ge(s["ln_done"], START + (LN_B + 1) * NB))
            pe.wait_ge(s["ln_done"], START + (LN_B + 2) * NB)
            with pe.Fori(0, 4) as kv:
                pe.wait_ge(s["b_w_done"], START + kv * 3 + 1)
                pe.wait_ge(s["b_yadd"], START + 8 * NB * 0 + 2 * NB * kv)
                pe_head(pe, ln_k(kv), (5 * kv) * NB, 0)
                pe.wait_ge(s["ln_done"], START + (ln_k(kv) + 1) * NB)
                for k in range(NCH):
                    mm = pe.matmul(slot[0][:, 64 * k:64 * k + 64], z2[:, k * 128:k * 128 + 128], b_w[:, 2, 0:64],
                                   start=True, stop=True)
                mm.then_inc(s["b_v"], 1)
                with pe.Fori(0, 2) as pr:
                    p = pe.snap(kv * 2 + pr)
                    pe.wait_ge(s["b_w_done"], START + kv * 3 + pr + 2)
                    pe.wait_ge(s["b_vsb"], START + kv + 1)
                    pe.wait_ge(s["b_yadd"], START + NB * p)
                    for hh in range(2):
                        pe_head(pe, ln_q(kv, pr, hh), (5 * kv + 1 + 2 * pr + hh) * NB, hh)
                        pe.wait_ge(s["ln_done"], START + (ln_q(kv, pr, hh) + 1) * NB)
                    pe.wait_ge(s["b_split"], START + 5 * kv + 2 * pr + 3)
                    n = 0
                    for hh in range(2):
                        for i in range(NCH):
                            for u in range(2):
                                if n >= 4:
                                    pe.wait_ge(s["b_max"], START + 64 * p + n - 3)
                                for a in (0, 512):
                                    keys = slice(1024 * u + a, 1024 * u + a + 512)
                                    pe.matmul(slot[n % 4][:, a:a + 512], QA[hh][:, 128 * i:128 * i + 128],
                                              KA[:, keys], start=True, stop=False)
                                    mm = pe.matmul(slot[n % 4][:, a:a + 512], QB[hh][0:64, 128 * i:128 * i + 128],
                                                   KB[0:64, keys], start=False, stop=True)
                                mm.then_inc(s["b_s1"], 1)
                                n += 1
                    pe.wait_ge(s["b_neg"], START + p + 1)
                    pe.transpose(slot[0][:, 0:128], b_nmax[:, :], ident).then_inc(s["b_nt"], 1)
                    pe.wait_ge(s["b_dma"], START + 64 * (p + 1))

                    def scores(n):
                        ring_free(pe, ("s", n), p)
                        qb, k = n // 16, n % 16
                        o = slot[B_PLACE[("s", n)]]
                        for hh in range(2):
                            pe.matmul(o[:, 512 * hh:512 * hh + 512], KA[:, 128 * k:128 * k + 128],
                                      QA[hh][:, 512 * qb:512 * qb + 512], start=True, stop=False)
                            mm = pe.matmul(o[:, 512 * hh:512 * hh + 512], KB[:, 128 * k:128 * k + 128],
                                           QB[hh][:, 512 * qb:512 * qb + 512], start=False, stop=True)
                        mm.then_inc(s["b_s"], 1)

                    def values(n):
                        qb, k = n // 16, n % 16
                        pe.wait_ge(s["b_exp"], START + 64 * p + n + 1)
                        if k == 0:
                            pe.wait_ge(s["b_rnd"], START + NB * p + qb)
                        for hh in range(2):
                            pe.matmul(slot[3][64 * hh:64 * hh + 64, 0:512], Vb[:, k, :],
                                      Pb[:, n % 3, 512 * hh:512 * hh + 512], start=(k == 0), stop=(k == 15),
                                      skip_group_check=True)
                        for hh in range(2):
                            mm = pe.matmul(slot[3][64 * hh:64 * hh + 32, 512:1024], ones32[:, :],
                                           Pb[:, n % 3, 512 * hh:512 * hh + 512], start=(k == 0), stop=(k == 15),
                                           skip_group_check=True)
                        mm.then_inc(s["b_pv"], 1)

                    def project(qb):
                        ring_free(pe, ("y", qb), p)
                        pe.wait_ge(s["b_on"], START + NB * p + qb + 1)
                        pe.matmul(slot[B_PLACE[("y", qb)]][:, 0:512], b_wo[:, :], Ob[:, :], start=True, stop=True)\
                          .then_inc(s["b_y"], 1)

                    scores(0)
                    done = 0
                    for kind, n in B_ENTRIES[1:]:
                        if kind == "s":
                            scores(n)
                            values(n - 1)
                            done = n
                        else:
                            if n == NB - 1:
                                values(done)
                            project(n)

        def act_head(act, mm_before, n):
            for b in range(NB):
                act.wait_ge(s["b_mm"], START + mm_before + b + 1)
                act.activation(b_part[:, b * 512:b * 512 + 512], slot[b][:, 0:512], ACT.Copy).then_inc(s["b_qb"], 1)
            act_norm(act, n)

        def act_grouped(act):
            act_norm(act, LN_B)
            act_norm(act, LN_B + 1)
            with act.Fori(0, 4) as kv:
                act.wait_ge(s["b_split"], START + 5 * kv)
                act_head(act, (5 * kv) * NB, ln_k(kv))
                act.wait_ge(s["ln_done"], START + (ln_k(kv) + 1) * NB)
                act.activation(KA[:, :], normed[:, :], ACT.Copy).then_inc(s["b_prt"], 1)
                act.wait_ge(s["b_v"], START + kv + 1)
                act.activation(Vb[:, :, :].rearrange("p k d -> p (k d)"), slot[0][:, :], ACT.Copy)\
                   .then_inc(s["b_vsb"], 1)
                with act.Fori(0, 2) as pr:
                    p = act.snap(kv * 2 + pr)
                    for hh in range(2):
                        act.wait_ge(s["b_split"], START + 5 * kv + 2 * pr + hh + 1)
                        act_head(act, (5 * kv + 1 + 2 * pr + hh) * NB, ln_q(kv, pr, hh))
                        act.wait_ge(s["ln_done"], START + (ln_q(kv, pr, hh) + 1) * NB)
                        act.activation(b_round[:, :], normed[:, :], ACT.Copy).then_inc(s["b_ln"], 1)
                        act.wait_ge(s["b_ln"], START + 4 * kv + 2 * pr + hh + 1)
                        act.activation(b_part[:, :], b_round[:, :].bitcast(F32), ACT.Copy,
                                       scale=const("rows")[:, 5:6])
                        act.activation(QB[hh][0:64, :], b_round[0:64, :].bitcast(F32), ACT.Copy)\
                           .then_inc(s["b_prt"], 1)
                    act.wait_ge(s["b_nt"], START + p + 1)
                    act.wait_ge(s["b_dma"], START + 64 * p)
                    act.activation(b_hi[:, :], slot[0][0:32, 0:128], ACT.Copy).then_inc(s["b_his"], 1)

                    def take_output(qb):
                        act.wait_ge(s["b_pv"], START + 64 * p + 16 * (qb + 1))
                        act.wait_ge(s["b_on"], START + NB * p + qb)
                        act.activation(Oc[:, :], slot[3][:, :], ACT.Copy).then_inc(s["b_rnd"], 1)
                    for n in range(64):
                        act.wait_ge(s["b_s"], START + 64 * p + n + 1)
                        act.wait_ge(s["b_pv"], START + 64 * p + (n - 2 if n >= 3 else 0))
                        act.activation(Pb[:, n % 3, :], slot[B_PLACE[("s", n)]][:, :], ACT.Exp)\
                           .then_inc(s["b_exp"], 1)
                        if n % 16 == 0 and n:
                            take_output(n // 16 - 1)
                    take_output(NB - 1)

        def pool_grouped(pool):
            for n in (LN_B, LN_B + 1):
                pool_norm(pool, n)
            with pool.Fori(0, 4) as kv:
                pool_norm(pool, ln_k(kv))
                with pool.Fori(0, 2) as pr:
                    for hh in range(2):
                        pool_norm(pool, ln_q(kv, pr, hh))

        def dve_grouped(dve):
            dve.wait_ge(s["xm_done"], START + XM0)
            dve.memset(ones32[:, :], 1.0)
            dve.memset(b_nmax[:, :], 0.0)
            dve.memset(KB[64:66, :].bitcast(F32), 1.0).then_inc(s["b_ones"], 1)
            dve_norm(dve, LN_B, lambda b: XM[:, b * 512:b * 512 + 512], 1e-5, dve_plain(dve, LN_B, normed))
            dve.wait_ge(s["wb_in"], START + WB_IN)
            dve_norm(dve, LN_B + 1, lambda b: normed[:, b * 512:b * 512 + 512], 1e-6,
                     dve_affine(dve, LN_B + 1, z2, b_cols[:, 0:1], b_cols[:, 1:2]))
            dve.tensor_scalar(b_cols[:, 2:4], b_cols[:, 2:4], DH ** -0.5, None, ALU.mult).then_inc(s["b_ones"], 1)
            dve.wait_ge(s["b_ones"], START + 2)

            def head(n, g, bias):
                dve_norm(dve, n, lambda b: b_part[:, b * 512:b * 512 + 512], 1e-6, dve_affine(dve, n, normed, g, bias))

            with dve.Fori(0, 4) as kv:
                dve.wait_ge(s["b_y"], START + 2 * NB * kv)
                for i in range(2):
                    dve.tensor_copy(b_w[:, 0, 64 * i:64 * i + 64], b_wkv[:, bass.ds(kv * 64, 64)])
                dve.tensor_copy(b_w[:, 2, 0:64], b_wkv[:, bass.ds(kv * 64 + 256, 64)]).then_inc(s["b_w_done"], 1)
                dve.wait_ge(s["b_prt"], START + 5 * kv)
                head(ln_k(kv), b_cols[:, 4:5], b_cols[:, 5:6])
                dve.wait_ge(s["b_prt"], START + 5 * kv + 1)
                dve.tensor_tensor(KB[0:64, :], normed[0:64, :], KA[0:64, :].bitcast(F32), ALU.subtract)\
                   .then_inc(s["b_split"], 1)
                with dve.Fori(0, 2) as pr:
                    p = dve.snap(kv * 2 + pr)
                    dve.wait_ge(s["b_mm"], START + 5 * NB * kv + NB + 2 * NB * pr)
                    dve.wait_ge(s["b_y"], START + NB * p)
                    dve.wait_ge(s["b_v"], START + kv + 1)
                    for hh in range(2):
                        for i in range(2):
                            dve.tensor_copy(b_w[:, hh, 64 * i:64 * i + 64],
                                            b_wq[:, bass.ds(kv * 256 + pr * 128 + hh * 64, 64)])
                    dve.tensor_copy(b_wo[:, :], b_wout[:, :, :].rearrange("p j n -> p (j n)")[:, bass.ds(p * 128, 128)])\
                       .then_inc(s["b_w_done"], 1)
                    for hh in range(2):
                        head(ln_q(kv, pr, hh), b_cols[:, 2:3], b_cols[:, 3:4])
                        dve.wait_ge(s["b_prt"], START + 5 * kv + 1 + 2 * pr + hh + 1)
                        dve.scalar_tensor_tensor(out=QA[hh][:, :], in0=normed[:, :], scalar=const("rows")[:, 6:7],
                                                 in1=b_part[:, :], op0=ALU.mult, op1=ALU.add)\
                           .then_inc(s["b_split"], 1)
                    n = 0
                    for hh in range(2):
                        for i in range(NCH):
                            for u in range(2):
                                dve.wait_ge(s["b_s1"], START + 64 * p + n + 1)
                                dve.tensor_reduce(b_pmax[:, 16 * hh + i, u:u + 1], slot[n % 4][:, :], AX.X, ALU.max)\
                                   .then_inc(s["b_max"], 1)
                                n += 1
                    dve.wait_ge(s["b_max"], START + 64 * (p + 1))
                    dve.wait_ge(s["b_nt"], START + p)
                    dve.tensor_tensor(b_nmax[:, 0:32], b_pmax[:, :, 0], b_pmax[:, :, 1], ALU.max)\
                       .then_inc(s["b_comb"], 1)
                    dve.wait_ge(s["b_comb"], START + p + 1)
                    dve.tensor_scalar(b_nmax[:, 0:32], b_nmax[:, 0:32], -1.0, None, ALU.mult).then_inc(s["b_neg"], 1)
                    dve.wait_ge(s["b_his"], START + p + 1)
                    dve.tensor_tensor(b_lo[:, :], slot[0][0:32, 0:128], b_hi[:, :].bitcast(F32), ALU.subtract)\
                       .then_inc(s["b_los"], 1)
                    for qb in range(NB):
                        dve.wait_ge(s["b_rnd"], START + NB * p + qb + 1)
                        for hh in range(2):
                            r = slice(64 * hh, 64 * hh + 32)
                            ins = dve.reciprocal(b_inv[r, :], Oc[r, 512:1024])
                        ins.then_inc(s["b_invd"], 1)
                        dve.wait_ge(s["b_invd"], START + NB * p + qb + 1)
                        for hh in range(2):
                            r = slice(64 * hh, 64 * hh + 32)
                            q = slice(64 * hh + 32, 64 * hh + 64)
                            dve.tensor_tensor(Ob[r, :], Oc[r, 0:512], b_inv[r, :], ALU.mult)
                            ins = dve.tensor_tensor(Ob[q, :], Oc[q, 0:512], b_inv[r, :], ALU.mult)
                        ins.then_inc(s["b_on"], 1)
                        dve.wait_ge(s["b_y"], START + NB * p + qb + 1)
                        cols = slice(qb * 512, qb * 512 + 512)
                        dve.tensor_tensor(XM[:, cols], XM[:, cols], slot[B_PLACE[("y", qb)]][:, 0:512], ALU.add)\
                           .then_inc(s["b_yadd"], 1)

        def final_ready(eng):
            if "S1" in stages:
                eng.wait_ge(s["xm_done"], START + 16)
            elif "B" in stages:
                eng.wait_ge(s["b_yadd"], START + 32)
            elif "S0" in stages:
                eng.wait_ge(s["xm_done"], START + XM0)
            else:
                eng.wait_ge(s["a_yadd"], START + 16)

        def pe_out(pe):
            final_ready(pe)
            for c in range(NCH):
                mm = pe.transpose(slot[c // 8][:, (c % 8) * 128:(c % 8) * 128 + 128], XM[:, c * 128:c * 128 + 128],
                                  ident)
                if c % 8 == 7:
                    mm.then_inc(s["tr_out"], 1)

        def act_out(act):
            final_ready(act)
            for i in range(2):
                act.wait_ge(s["tr_out"], START + i + 1)
                act.activation(out_nat[:, 8 * i:8 * i + 8, :].rearrange("p c d -> p (c d)"), slot[i][:, :], ACT.Copy)\
                   .then_inc(s["out_sb"], 1)

        def sp_out(sp):
            for i in range(2):
                sp.wait_ge(s["out_sb"], START + i + 1)
                sp.dma_start(out[0, 1024 * i:1024 * i + 1024, :].rearrange("(c p) d -> p c d", p=128),
                             out_nat[:, 8 * i:8 * i + 8, :]).then_inc(s["out_done"], 16)
            sp.wait_ge(s["out_done"], START + 32)

        def start_counts(eng, which):
            for name in names[which::5]:
                eng.sem_inc(s[name], START)

        @block.sync
        def _(sp):
            start_counts(sp, 0)
            sp_setup(sp)
            if "A" in stages:
                sp_first(sp)
            if "S0" in stages:
                sp.wait_ge(s["stack_in"], START + 8)
                sp_stack(sp, 0)
            if "B" in stages:
                sp_grouped(sp)
            if "S1" in stages:
                sp.wait_ge(s["stack_in"], START + 16)
                sp_stack(sp, 1)
            sp_out(sp)

        @block.gpsimd
        def _(pool):
            start_counts(pool, 1)
            pool_setup(pool)
            if "A" in stages:
                pool_norm(pool, LN_A)
            if "S0" in stages:
                pool_norm(pool, LN_S0)
                pool_stack(pool, 0)
            if "B" in stages:
                pool_grouped(pool)
            if "S1" in stages:
                pool_norm(pool, LN_S1)
                pool_stack(pool, 1)

        @block.scalar
        def _(act):
            start_counts(act, 2)
            act_setup(act)
            if "A" in stages:
                act_first(act)
            if "S0" in stages:
                act.wait_ge(s["setup_pool"], START + 4)
                act_norm(act, LN_S0)
                act.wait_ge(s["stack_out"], START + 1)
                act_stack(act, 0)
            if "B" in stages:
                act_grouped(act)
            if "S1" in stages:
                act_norm(act, LN_S1)
                act.wait_ge(s["stack_out"], START + 2)
                act_stack(act, 1)
            act_out(act)

        @block.vector
        def _(dve):
            start_counts(dve, 3)
            dve_setup(dve)
            if "A" in stages:
                dve_first(dve)
            if "S0" in stages:
                dve_into(dve, 0)
                dve_stack(dve, 0)
            if "B" in stages:
                dve_grouped(dve)
            if "S1" in stages:
                dve_into(dve, 1)
                dve_stack(dve, 1)

        @block.tensor
        def _(pe):
            start_counts(pe, 4)
            pe_setup(pe)
            if "A" in stages:
                pe_first(pe)
            if "S0" in stages:
                pe_into(pe, 0)
                pe_stack(pe, 0)
            if "B" in stages:
                pe_grouped(pe)
            if "S1" in stages:
                pe_into(pe, 1)
                pe_stack(pe, 1)
            pe_out(pe)


_INS = {"x": "L0_attn_a_x", "w_qkv": "L0_attn_a_w_qkv", "w_out": "L0_attn_a_w_out",
        "b_ln_scale": "L0_attn_b_ln_scale", "b_ln_bias": "L0_attn_b_ln_bias", "Wq": "L0_attn_b_Wq",
        "Wkv": "L0_attn_b_Wkv", "qn_scale": "L0_attn_b_qn_scale", "qn_bias": "L0_attn_b_qn_bias",
        "kn_scale": "L0_attn_b_kn_scale", "kn_bias": "L0_attn_b_kn_bias", "Wout": "L0_attn_b_Wout",
        "Wqkv": "L0_ffn_Wqkv", "q_scale": "L0_ffn_q_scale", "k_scale": "L0_ffn_k_scale", "Wo": "L0_ffn_Wo",
        "ln_g": "L0_ffn_ln_g", "ln_b": "L0_ffn_ln_b", "W1": "L0_ffn_W1", "b1": "L0_ffn_b1",
        "W2": "L0_ffn_W2", "b2": "L0_ffn_b2"}


def kernel(**inputs):
    import concourse.bacc as bacc
    from concourse.bass_utils import run_bass_kernel_spmd

    nc = bacc.Bacc("TRN2", target_bir_lowering=False, num_devices=1)
    nc.disable_value_cache = True
    table, place = shape_constants()
    arrays = {"in_shape_constants": np.ascontiguousarray(table)}
    for short, name in _INS.items():
        arrays[f"in_{short}"] = np.ascontiguousarray(inputs[name])
    A = {k[3:]: nc.dram_tensor(k, a.shape, mybir.dt.from_np(a.dtype), kind="ExternalInput").ap()
         for k, a in arrays.items()}
    out = nc.dram_tensor("out", (1, S, D), F32, kind="ExternalOutput").ap()
    build(nc, A, out, place)
    r = run_bass_kernel_spmd(nc, [arrays], core_ids=[0])
    return r.results[0]["out"]
```

```python
from contextlib import ExitStack

import numpy as np

import concourse.bass as bass
from concourse import mybir

F32 = mybir.dt.float32
F32R = mybir.dt.float32r
BF16 = mybir.dt.bfloat16
ALU = mybir.AluOpType
ACT = mybir.ActivationFunctionType
AX = mybir.AxisListType

S = 2048
D = 128
NCH = S // 128
NB = S // 512
DEPTH = 6
H, DH = 16, 64
WIN = 32
INNER = H * DH
DFF = 341
FT = [(0, 128), (128, 128), (256, DFF - 256)]
AH = 8
START = 1
NEG = -1.0e30


def shape_constants():
    f = np.float32
    parts = {}
    parts["ident"] = np.eye(128, dtype=f)
    parts["mean128"] = np.full((128, 128), 1.0 / 128, f)
    i = np.arange(128)
    parts["mask_qk"] = np.where(i[None, :] <= i[:, None], 0, NEG).astype(f)
    parts["mask_kq"] = np.where(i[:, None] <= i[None, :], 0, NEG).astype(f)
    q = (i % WIN)[:, None]
    m = np.arange(2 * WIN)[None, :]
    ok = np.where(m < WIN, q <= m, m - WIN <= q)
    win = np.repeat(np.where(ok, 0, NEG)[:, None, :], 2, 1)
    win[:WIN, 0, :WIN] = NEG
    parts["mask_win"] = win.reshape(128, 2 * 2 * WIN).astype(f)
    half = np.arange(0, DH, 2, dtype=f)
    inv_freq = (f(1.0) / np.power(f(10000.0), half / f(DH))).astype(f)
    t = np.arange(S, dtype=f)
    ang = (t[:, None] * inv_freq[None, :]).astype(f)
    ang = np.concatenate([ang, ang], -1).astype(np.float64)
    base = (half.astype(np.float64) + 0.4 * DH) / (1.4 * DH)
    base = np.concatenate([base, base])
    power = (np.arange(S) % 128) / (WIN // 2)
    scale = base[None, :] ** power[:, None]
    sign = np.where(np.arange(DH) < DH // 2, -1.0, 1.0)

    def chunked(a):
        return a.reshape(NCH, 128, DH).transpose(1, 0, 2).reshape(128, NCH * DH).astype(f)

    parts["rot_q_cos"] = chunked(np.cos(ang) * scale * 8.0)
    parts["rot_q_sin"] = chunked(np.sin(ang) * scale * 8.0 * sign)
    parts["rot_k_cos"] = chunked(np.cos(ang) / scale)
    parts["rot_k_sin"] = chunked(np.sin(ang) / scale * sign)
    parts["cross"] = np.tile(base ** 8.0, 2).reshape(128, 1).astype(f)
    r = i % 32
    hi_q, lo_q = (r < 8) | ((r >= 16) & (r < 24)), (r >= 8) & (r < 16)
    hi_k, lo_k = r < 16, (r >= 16) & (r < 24)
    cols = [hi_q * 1.0 - lo_q, lo_q * 1.0, hi_k * 1.0 - lo_k, lo_k * 1.0,
            ((r == 24) | (r == 25)) * 1.0,
            np.where(i < 64, 1.0, -1.0), np.where(i < 64, 0.0, 1.0)]
    parts["rows"] = np.stack(cols, 1).astype(f)
    parts["sum_rows"] = ((i[:, None] // 32 == i[None, :] // 32) & (i[:, None] % 32 == 8)).astype(f)
    at, place = 0, {}
    for name, a in parts.items():
        place[name] = (at, a.shape[1])
        at += a.shape[1]
    return np.concatenate(list(parts.values()), 1), place


def build(nc, A, out, place, stages=("A", "S0", "B", "S1")):
    n_const = A["shape_constants"].shape[1]
    ctx = ExitStack()
    with ctx:
        def sem(name):
            return ctx.enter_context(nc.semaphore(name))

        def sb(name, shape, dt=F32, at=ctx):
            return at.enter_context(nc.sbuf_tensor(name, shape, dt))

        consts = sb("consts", [128, n_const])

        def const(name):
            a, n = place[name]
            return consts[:, a:a + n]

        ident = const("ident")
        ident_b = sb("ident_b", [128, 128], BF16)
        mask_qk = sb("mask_qk", [128, 128], BF16)
        mask_kq = sb("mask_kq", [128, 128], BF16)
        mask_win = sb("mask_win", [128, 2, 2 * WIN], BF16)
        minus_half = sb("minus_half", [128, H])
        ones = sb("ones", [128, 128])
        XM = sb("XM", [128, S])
        XA = sb("XA", [128, S + 1])
        XB = sb("XB", [128, S + 1])
        centred = sb("centred", [128, S])
        normed = sb("normed", [128, S])
        squares = sb("squares", [128, 2, 512])
        variance = sb("variance", [128, NCH])
        rstd = sb("rstd", [128, NCH])
        diag = sb("diag", [128, 2, 512])
        slot = [ctx.enter_context(nc.psum_tensor(f"slot{i}", [128, 1024], F32)) for i in range(4)]

        rows_dram = nc.dram_tensor("rows_dram", (2, 64, 128), F32).ap()

        B_RING = 3

        mem = ExitStack()
        x_nat = sb("x_nat", [128, NCH, D], F32, mem)
        wqkv_nat = sb("wqkv_nat", [128, 3, D], F32, mem)
        wout_nat = sb("wout_nat", [128, D], F32, mem)
        wq_rows = sb("wq_rows", [128, 16, 32], F32, mem)
        wk_rows = sb("wk_rows", [128, 16, 32], F32, mem)
        wv_cols = sb("wv_cols", [128, D], F32, mem)
        wout_pad = sb("wout_pad", [128, 16, 32], F32, mem)
        wout_rows = sb("wout_rows", [128, 4, D], F32, mem)
        gq_w = sb("gq_w", [128, D], F32, mem)
        gk_w = sb("gk_w", [128, D], F32, mem)
        gv_w = sb("gv_w", [128, 32], F32, mem)
        go_w = sb("go_w", [128, D], F32, mem)
        rounded = sb("rounded", [128, 2, 1024], F32R, mem)
        scaled = sb("scaled", [128, 2, 1024], F32, mem)
        QT = sb("QT", [128, S], F32R, mem)
        KT = sb("KT", [128, S], F32R, mem)
        V4 = sb("V4", [128, NCH, 4, 32], F32, mem)
        part_max = sb("part_max", [128, 64, 2], F32, mem)
        neg_max = sb("neg_max", [128, 128], F32, mem)
        neg_hi = sb("neg_hi", [64, 128], F32R, mem)
        neg_lo = sb("neg_lo", [64, 128], F32R, mem)
        Pa = sb("Pa", [128, 4, 1024], F32, mem)
        Oa = sb("Oa", [128, 512], F32, mem)
        sum_inv = sb("sum_inv", [128, 512], F32, mem)
        On = sb("On", [128, 512], F32, mem)
        out_nat = sb("out_nat", [128, NCH, D], F32, mem)
        mem.close()

        mem = ExitStack()
        b_wq = sb("b_wq", [128, INNER], F32, mem)
        b_wkv = sb("b_wkv", [128, 512], F32, mem)
        b_wout = sb("b_wout", [128, 8, D], F32, mem)
        b_wmean = sb("b_wmean", [128, 20], F32, mem)
        b_cols = sb("b_cols", [128, 6], F32, mem)
        b_w = sb("b_w", [128, 3, 128], F32, mem)
        b_wo = sb("b_wo", [128, D], F32, mem)
        z2 = XA[:, 1:S + 1]
        b_sum = XB[:, 1:S + 1].rearrange("p (i c) -> p i c", i=2)
        mean2 = sb("mean2", [128, 2], F32, mem)
        b_variance = sb("b_variance", [128, 8 * NB], F32, mem)
        b_rstd = sb("b_rstd", [128, 8 * NB], F32, mem)
        QA = [[sb(f"QA{i}{h}", [128, S], F32R, mem) for h in range(2)] for i in range(2)]
        QB = [[sb(f"QB{i}{h}", [66, S], F32R, mem) for h in range(2)] for i in range(2)]
        KA = sb("KA", [128, S], F32R, mem)
        KB = sb("KB", [66, S], F32R, mem)
        KA_next = sb("KA_next", [128, S], F32R, mem)
        KB_next = sb("KB_next", [64, S], F32R, mem)
        Vb = sb("Vb", [128, NCH, 64], F32, mem)
        b_pmax = sb("b_pmax", [128, 32, 2], F32, mem)
        b_nmax = sb("b_nmax", [128, 128], F32, mem)
        b_hi = sb("b_hi", [32, 128], F32R, mem)
        b_lo = sb("b_lo", [32, 128], F32R, mem)
        Pb = sb("Pb", [128, B_RING, 1024], F32, mem)
        Oc = sb("Oc", [128, 512], F32, mem)
        b_inv = sb("b_inv", [128, 512], F32, mem)
        Ob = sb("Ob", [128, 512], F32, mem)
        mem.close()

        mem = ExitStack()
        w_raw = sb("w_raw", [128, INNER], F32, mem)
        w_hi = sb("w_hi", [128, 3 * INNER], F32R, mem)
        w_lo = sb("w_lo", [128, 3 * INNER], F32R, mem)
        Wo = sb("Wo", [128, 8, D], F32, mem)
        W1 = sb("W1", [128, 2 * DFF], F32, mem)
        W2 = sb("W2", [128, 3, D], F32, mem)
        b1 = sb("b1", [128, 2, 3], F32, mem)
        ffn_cols = sb("ffn_cols", [128, 3], F32, mem)
        qk_scales = sb("qk_scales", [128, 4, DH], F32, mem)
        rot = [sb(f"rot{i}", [128, NCH * DH], F32, mem) for i in range(4)]
        x_hi = [sb(f"x_hi{i}", [128, 128], F32R, mem) for i in range(2)]
        x_lo = [sb(f"x_lo{i}", [128, 128], F32R, mem) for i in range(2)]
        raw_qk = sb("raw_qk", [128, 2 * INNER], F32, mem)
        raw = [raw_qk[:, 0:INNER], raw_qk[:, INNER:2 * INNER]]
        sq = sb("sq", [128, INNER], F32, mem)
        rot_out = [sb(f"rot_out{i}", [128, INNER], F32, mem) for i in range(2)]
        sin_qk = sb("sin_qk", [128, 2 * INNER], F32, mem)
        rot_sin = [sin_qk[:, 0:INNER], sin_qk[:, INNER:2 * INNER]]
        norm2 = [sb(f"norm2_{i}", [128, H], F32, mem) for i in range(2)]
        norm2c = [sb(f"norm2c_{i}", [128, H], F32, mem) for i in range(2)]
        inv_norm = [sb(f"inv_norm{i}", [128, H], F32, mem) for i in range(2)]
        qT = sb("qT", [128, 8, 128], F32, mem)
        kT = sb("kT", [128, 8, 160], F32, mem)
        V = [sb(f"V{i}", [128, INNER], F32, mem) for i in range(2)]
        VW = [sb(f"VW{i}", [128, 4, 512], F32, mem) for i in range(2)]
        row_max = sb("row_max", [128, H], F32, mem)
        row_sum = sb("row_sum", [128, H], F32, mem)
        row_inv = sb("row_inv", [128, H], F32, mem)
        probs = sb("probs", [128, INNER], F32, mem)
        probsT = sb("probsT", [128, 8, 128], F32, mem)
        Os = sb("Os", [128, INNER], F32, mem)
        OT = sb("OT", [128, 8, 128], F32, mem)
        gate = raw_qk[:, 0:1536].rearrange("p (j t) -> p j t", j=3)
        hidden = sin_qk[:, 0:1536].rearrange("p (j t) -> p j t", j=3)
        mem.close()

        names = ("consts_in x_in wa_in setup_pool setup_dve setup_act xm_done "
                 "ln_mean ln_centred ln_square ln_var ln_eps ln_pow ln_diag ln_bc ln_half ln_done "
                 "w_raw_in w_hi_done w_lo_done xh_done scales_in wo_in ffn_in tables_done xc_done "
                 "q_mm k_mm v_mm tq_mm tk_mm s_mm ot_mm y_mm pv_mm "
                 "q_copy k_copy q_evac k_evac qT_sb kT_cross kT_sb v_sb probs_exp ot_sb vs_in "
                 "nq_done nk_done aq_done ak_done bq_done bk_done cq_done ck_done iq_done ik_done "
                 "rq_done rk_done qn_done kn_done max_done sub_done pt_mm pt_sb sum_done inv_done on_done xb_done "
                 "w1_mm gelu_done hid_done w2_mm f_done stack_in stack_out "
                 "tr_x tr_wo wa_rows a_w a_qk a_round a_scaled a_split a_v a_vsb a_s1 a_max a_comb a_neg a_nt "
                 "a_hi a_lo a_dma a_s a_exp a_pv a_osb a_bc a_inv a_on a_y a_yadd "
                 "wb_in wsum_done wmean_done wcen_done wk_done wq_done wv_done wo_done b_rnd b_qhi b_qlo b_khi b_klo b_kcur b_v b_vsb "
                 "b_s1 b_max b_comb b_neg b_nt b_his b_los b_dma b_s a_rows b_rows passed b_psum b_lsum "
                 "b_exp b_pv b_invd b_on b_y b_yadd b_ones tr_out out_sb out_done ").split()
        s = {n: sem(n) for n in names}

        LN_A, LN_S0 = 0, int("A" in stages)
        LN_B = LN_S0 + (1 + DEPTH) * ("S0" in stages)
        LN_S1 = LN_B + 2 + 4 * 3
        block = ctx.enter_context(nc.Block())

        def pe_mean(pe, o, src):
            pe.matmul(o[:, 0:512], const("mean128"), src, start=True, stop=True).then_inc(s["ln_mean"], 1)

        def pe_var(pe, o, m, b):
            pe.wait_ge(s["ln_square"], START + m + 1)
            for c in range(4):
                mm = pe.matmul(o[:, 512 + c:513 + c], squares[:, b % 2, c * 128:c * 128 + 128],
                               const("mean128")[:, 0:1], start=True, stop=True)
            mm.then_inc(s["ln_var"], 1)

        def pe_spread(pe, o, m, b):
            pe.wait_ge(s["ln_diag"], START + m + 1)
            pe.matmul(o[:, 512:1024], ones[:, :], diag[:, b % 2, :], start=True, stop=True).then_inc(s["ln_bc"], 1)

        def act_square(act, m, b):
            act.wait_ge(s["ln_centred"], START + m + 1)
            act.wait_ge(s["ln_var"], START + (m - 1 if b >= 2 else m - b))
            act.activation(squares[:, b % 2, :], centred[:, b * 512:b * 512 + 512], ACT.Square)\
               .then_inc(s["ln_square"], 1)

        def pool_rstd(pool, m, b):
            pool.wait_ge(s["ln_eps"], START + m + 1)
            pool.tensor_tensor(rstd[:, 4 * b:4 * b + 4], variance[:, 4 * b:4 * b + 4], minus_half[:, 0:4], ALU.pow)\
                .then_inc(s["ln_pow"], 1)

        def dve_centre(dve, o, m, b, src):
            dve.wait_ge(s["ln_mean"], START + m + 1)
            dve.tensor_tensor(centred[:, b * 512:b * 512 + 512], src, o[:, 0:512], ALU.subtract)\
               .then_inc(s["ln_centred"], 1)

        def dve_eps(dve, o, m, b, eps):
            dve.wait_ge(s["ln_var"], START + m + 1)
            dve.tensor_scalar(variance[:, 4 * b:4 * b + 4], o[:, 512:516], eps, None, ALU.add)\
               .then_inc(s["ln_eps"], 1)

        def dve_diag(dve, m, b):
            dve.wait_ge(s["ln_pow"], START + m + 1)
            dve.wait_ge(s["ln_bc"], START + (m - 1 if b >= 2 else m - b))
            dve.tensor_tensor(diag[:, b % 2, :].rearrange("p (c t) -> p c t", c=4),
                              ident.unsqueeze(1).to_broadcast([128, 4, 128]),
                              rstd[:, 4 * b:4 * b + 4].unsqueeze(2).to_broadcast([128, 4, 128]), ALU.mult)\
               .then_inc(s["ln_diag"], 1)

        def dve_finish(dve, o, m, b, finish):
            dve.wait_ge(s["ln_bc"], START + m + 1)
            finish(b, centred[:, b * 512:b * 512 + 512], o[:, 512:1024])

        def pe_norm(pe, idx, src, ready):
            for b in range(NB):
                ready(b)
                pe_mean(pe, slot[b], src(b))
            for b in range(NB):
                pe_var(pe, slot[b], idx * NB + b, b)
            for b in range(NB):
                pe_spread(pe, slot[b], idx * NB + b, b)

        def act_norm(act, idx):
            for b in range(NB):
                act_square(act, idx * NB + b, b)

        def pool_norm(pool, idx):
            for b in range(NB):
                pool_rstd(pool, idx * NB + b, b)

        def dve_norm(dve, idx, src, eps, finish):
            n = idx * NB
            for b in range(NB):
                dve_centre(dve, slot[b], n + b, b, src(b))
            dve_eps(dve, slot[0], n, 0, eps)
            dve_eps(dve, slot[1], n + 1, 1, eps)
            dve_diag(dve, n, 0)
            dve_eps(dve, slot[2], n + 2, 2, eps)
            dve_diag(dve, n + 1, 1)
            dve_eps(dve, slot[3], n + 3, 3, eps)
            for b in range(NB):
                dve_finish(dve, slot[b], n + b, b, finish)
                if b + 2 < NB:
                    dve_diag(dve, n + b + 2, b + 2)

        def dve_affine(dve, idx, dst, g, bias):
            def finish(b, c, r):
                cols = slice(b * 512, b * 512 + 512)
                dve.tensor_tensor(dst[:, cols], c, r, ALU.mult).then_inc(s["ln_half"], 1)
                dve.wait_ge(s["ln_half"], START + idx * NB + b + 1)
                dve.tensor_scalar(dst[:, cols], dst[:, cols], g, bias, ALU.mult, ALU.add)\
                   .then_inc(s["ln_done"], 1)
            return finish

        def dve_plain(dve, idx, dst):
            def finish(b, c, r):
                dve.tensor_tensor(dst[:, b * 512:b * 512 + 512], c, r, ALU.mult).then_inc(s["ln_half"], 1)
                dve.wait_ge(s["ln_half"], START + idx * NB + b + 1)
                dve.sem_inc(s["ln_done"], 1)
            return finish

        LAST = NCH + 2

        def steps(eng, lam, step, start=0, end=LAST):
            def one(c, at=None):
                static = isinstance(c, int)
                at = c if static else at
                step(lam * NCH + c, c, at % 2, at < NCH, 1 <= at <= NCH, 2 <= at <= NCH + 1, at >= 3)
            if start < 3:
                for c in range(start, 3):
                    one(c)
                with eng.Fori(0, 6) as half:
                    one(half * 2 + 3, 3)
                    one(half * 2 + 4, 4)
                for c in range(15, end + 1):
                    one(c)
            else:
                for c in range(start, end + 1):
                    one(c)

        def back_to(g, c, k):
            return g - min(c, k) if isinstance(c, int) else g - k

        def tiles_of(b):
            return [((b + t) % 3,) + FT[(b + t) % 3] for t in range(3)]

        def read_before(f, t):
            return (f - 1) * 3 + (t + 1) % 3 + 1

        def first_third(call):
            return 3 * (DEPTH + 1) * call

        def sp_stack(sp, call):
            def load_third(count, layer, i):
                sp.wait_ge(s["w_lo_done"], START + count)
                sp.dma_start(w_raw[:, :], A["Wqkv"][bass.ds(layer, 1), :, i * INNER:(i + 1) * INNER]
                             .rearrange("a p n -> p (a n)")).then_inc(s["w_raw_in"], 16)

            for i in range(3):
                load_third(first_third(call) + i, 0, i)

            def layer(L, following):
                lam = L + DEPTH * call
                third = first_third(call) + 3 * (L + 1)
                sp.wait_ge(s["tables_done"], START + lam * 4)
                for j, name in enumerate(("q_scale", "k_scale")):
                    row = A[name][bass.ds(L, 1), :].rearrange("a n -> (a n)")
                    sp.dma_start(qk_scales[:, 2 * j, :], row.partition_broadcast(128))\
                      .then_inc(s["scales_in"], 16)
                    for x in range(2):
                        sp.dma_start(qk_scales[:, 2 * j + 1, 32 * x:32 * x + 32],
                                     row[32 - 32 * x:64 - 32 * x].partition_broadcast(128))\
                          .then_inc(s["scales_in"], 16)
                load_third(third, following, 0)
                sp.wait_ge(s["y_mm"], START + lam * NCH)
                sp.dma_start(Wo[:, :, :], A["Wo"][bass.ds(L, 1), :, :].rearrange("a (j p) n -> p (a j) n", p=128))\
                  .then_inc(s["wo_in"], 16)
                sp.wait_ge(s["f_done"], START + lam * NB * 2)
                sp.dma_start(W1[:, :], A["W1"][bass.ds(L, 1), :, :].rearrange("a p n -> p (a n)"))\
                  .then_inc(s["ffn_in"], 16)
                for j, (a, n) in enumerate(FT):
                    sp.dma_start(W2[0:n, j, :], A["W2"][bass.ds(L, 1), a:a + n, :].rearrange("a p n -> p (a n)"))\
                      .then_inc(s["ffn_in"], 16)
                    for i in range(2):
                        sp.dma_start(b1[0:n, i, j:j + 1], A["b1"][bass.ds(L, 1), i * DFF + a:i * DFF + a + n]
                                     .rearrange("a p -> p a")).then_inc(s["ffn_in"], 16)
                for j, name in enumerate(("ln_g", "ln_b", "b2")):
                    sp.dma_start(ffn_cols[:, j:j + 1], A[name][bass.ds(L, 1), :].rearrange("a p -> p a"))\
                      .then_inc(s["ffn_in"], 16)

                def window_values(g, c, par, front, mid, late, back):
                    if not front:
                        return
                    sp.wait_ge(s["v_sb"], START + g + 1)
                    sp.sem_inc(s["passed"], 1)
                    sp.wait_ge(s["pv_mm"], START + back_to(g, c, 1))
                    for x in range(2):
                        cols = slice(512 * x, 512 * x + 512)
                        for w in range(1, 4):
                            sp.dma_start(VW[par][64 * x:64 * x + 64, w, :], V[par][32 * w - 32:32 * w + 32, cols])\
                              .then_inc(s["vs_in"], 16)
                        sp.dma_start(VW[par][64 * x:64 * x + 32, 0, :], V[1 - par][96:128, cols])\
                          .then_inc(s["vs_in"], 16)
                        sp.dma_start(VW[par][64 * x + 32:64 * x + 64, 0, :], V[par][0:32, cols])\
                          .then_inc(s["vs_in"], 16)
                steps(sp, lam, window_values)
                for i in range(1, 3):
                    load_third(third + i, following, i)

            with sp.Fori(0, DEPTH - 1) as L:
                layer(L, L + 1)
            layer(DEPTH - 1, 0)

        VS = 160

        def pe_stack(pe, call):
            n0 = LN_S0 if call == 0 else LN_S1
            with pe.Fori(0, DEPTH) as L:
                lam = L + DEPTH * call
                pe.wait_ge(s["w_lo_done"], START + first_third(call) + 3 * (L + 1))

                def project_in(o, par, third):
                    for i in range(2):
                        cols = slice(third * INNER + i * 512, third * INNER + (i + 1) * 512)
                        out = o[:, i * 512:(i + 1) * 512]
                        pe.matmul(out, x_hi[par][:, :], w_hi[:, cols], start=True, stop=False)
                        pe.matmul(out, x_hi[par][:, :], w_lo[:, cols], start=False, stop=False)
                        mm = pe.matmul(out, x_lo[par][:, :], w_hi[:, cols], start=False, stop=True)
                    return mm

                def step(g, c, par, front, mid, late, back):
                    if front:
                        pe.wait_ge(s["xc_done"], START + g + 1)
                        pe.wait_ge(s["q_evac"], START + g)
                        pe.wait_ge(s["kT_sb"], START + back_to(g, c, 1))
                        project_in(slot[0], par, 0).then_inc(s["q_mm"], 1)
                    if mid:
                        pe.wait_ge(s["qn_done"], START + g)
                        pe.wait_ge(s["xb_done"], START + 2 * back_to(g, c, 3))
                        for j in range(8):
                            mm = pe.transpose(slot[1][:, j * 128:(j + 1) * 128],
                                              rot_out[0][:, j * 128:(j + 1) * 128], ident)
                        mm.then_inc(s["tq_mm"], 1)
                    if front:
                        pe.wait_ge(s["v_sb"], START + g)
                        project_in(slot[3], par, 1).then_inc(s["k_mm"], 1)
                    if mid:
                        pe.wait_ge(s["kn_done"], START + g)
                        if front:
                            pe.wait_ge(s["q_evac"], START + g + 1)
                        for j in range(8):
                            mm = pe.transpose(slot[0][:, j * 128:(j + 1) * 128],
                                              rot_out[1][:, j * 128:(j + 1) * 128], ident)
                        mm.then_inc(s["tk_mm"], 1)
                    if late:
                        pe.wait_ge(s["probs_exp"], START + g - 1)
                        for j in range(8):
                            mm = pe.transpose(slot[2][:, j * 128:(j + 1) * 128],
                                              probs[:, j * 128:(j + 1) * 128], ident)
                        mm.then_inc(s["pt_mm"], 1)
                    if back:
                        pe.wait_ge(s["on_done"], START + g - 2)
                        if mid:
                            pe.wait_ge(s["qT_sb"], START + g)
                        else:
                            pe.wait_ge(s["xb_done"], START + 2 * (g - 3))
                        for j in range(8):
                            mm = pe.transpose(slot[1][:, j * 128:(j + 1) * 128],
                                              Os[:, j * 128:(j + 1) * 128], ident)
                        mm.then_inc(s["ot_mm"], 1)
                    if late:
                        pe.wait_ge(s["pt_sb"], START + g - 1)
                        pe.wait_ge(s["vs_in"], START + VS * (g - 1))
                        pe.sem_inc(s["passed"], 1)
                        for h in range(H):
                            r = slice(64 * (h % 2), 64 * (h % 2) + 64)
                            at = (h % 2) * 512 + (h // 2) * 64
                            for w in range(4):
                                mm = pe.matmul(slot[2][32 * w:32 * w + 32, at:at + 64],
                                               probsT[r, h // 2, 32 * w:32 * w + 32],
                                               VW[par][r, w, (h // 2) * 64:(h // 2) * 64 + 64],
                                               start=True, stop=True)
                        mm.then_inc(s["pv_mm"], 1)
                    if front:
                        pe.wait_ge(s["k_evac"], START + g + 1)
                        project_in(slot[3], par, 2).then_inc(s["v_mm"], 1)
                    if back:
                        pe.wait_ge(s["wo_in"], START + (lam + 1) * 16)
                        pe.wait_ge(s["ot_sb"], START + g - 2)
                        for j in range(8):
                            mm = pe.matmul(slot[1][:, 0:128], Wo[:, j, :], OT[:, j, :], start=(j == 0), stop=(j == 7))
                        mm.then_inc(s["y_mm"], 1)
                    if mid:
                        pe.wait_ge(s["qT_sb"], START + g)
                        pe.wait_ge(s["kT_sb"], START + g)
                        if late:
                            pe.wait_ge(s["on_done"], START + g - 1)
                        first = 0 if isinstance(c, int) and c == 1 else 1
                        for i in range(2):
                            pe.matmul(slot[2][:, i * 512:(i + 1) * 512], ident_b[:, :],
                                      mask_win[:, first:first + 1, :].to_broadcast([128, 8, 2 * WIN]),
                                      start=True, stop=False, skip_group_check=True)
                        for h in range(H):
                            r = 64 * (h % 2)
                            at = (h % 2) * 512 + (h // 2) * 64
                            for w in range(4):
                                mm = pe.matmul(slot[2][32 * w:32 * w + 32, at:at + 64],
                                               qT[r:r + 64, h // 2, 32 * w:32 * w + 32],
                                               kT[r:r + 64, h // 2, 32 * w:32 * w + 64],
                                               start=False, stop=True, skip_group_check=True)
                        mm.then_inc(s["s_mm"], 1)

                n = (n0 + 1 + L) * NB

                def mean(b):
                    if b == 0:
                        pe.wait_ge(s["kT_sb"], START + (lam + 1) * NCH)
                    pe.wait_ge(s["xb_done"], START + 2 * (lam * NCH) + 8 * (b + 1))
                    if b:
                        pe.wait_ge(s["ln_centred"], START + n + b)
                    pe_mean(pe, slot[0], XB[:, b * 512:b * 512 + 512])

                def var(b):
                    if b:
                        pe.wait_ge(s["ln_half"], START + n + b)
                    pe_var(pe, slot[0], n + b, b)
                steps(pe, lam, step, 0, NCH)
                mean(0)
                steps(pe, lam, step, NCH + 1, NCH + 1)
                var(0)
                steps(pe, lam, step, NCH + 2, NCH + 2)
                pe_spread(pe, slot[0], n, 0)
                pe.wait_ge(s["ffn_in"], START + (lam + 1) * 16 * 13)
                for b in range(NB):
                    f = lam * NB + b
                    if b + 1 < NB:
                        mean(b + 1)
                    pe.wait_ge(s["ln_done"], START + n + b + 1)
                    for t, (j, a, m) in enumerate(tiles_of(b)):
                        if b == 0 and t == 0:
                            pe.wait_ge(s["xb_done"], START + 2 * (lam + 1) * NCH)
                            pe.wait_ge(s["on_done"], START + (lam + 1) * NCH)
                            pe.wait_ge(s["v_sb"], START + (lam + 1) * NCH)
                        if b >= 1:
                            pe.wait_ge(s["hid_done"], START + read_before(f, t))
                            if t == 2:
                                pe.wait_ge(s["f_done"], START + 2 * f)
                        for i in range(2):
                            mm = pe.matmul(slot[j + 1][0:m, i * 512:(i + 1) * 512],
                                           W1[:, i * DFF + a:i * DFF + a + m], normed[:, b * 512:b * 512 + 512],
                                           start=True, stop=True)
                        mm.then_inc(s["w1_mm"], 1)
                        if t == 0 and b + 1 < NB:
                            var(b + 1)
                    if b + 1 < NB:
                        pe_spread(pe, slot[0], n + b + 1, b + 1)
                    for t, (j, a, m) in enumerate(tiles_of(b)):
                        pe.wait_ge(s["hid_done"], START + f * 3 + t + 1)
                        mm = pe.matmul(slot[b % 3 + 1][:, 0:512], W2[0:m, j, :], hidden[0:m, j, :],
                                       start=(t == 0), stop=(t == 2))
                    mm.then_inc(s["w2_mm"], 1)

        def act_stack(act, call):
            n0 = LN_S0 if call == 0 else LN_S1
            def round_third(count, i):
                act.wait_ge(s["w_raw_in"], START + 16 * (count + 1))
                act.activation(w_hi[:, i * INNER:(i + 1) * INNER], w_raw[:, :], ACT.Copy).then_inc(s["w_hi_done"], 1)

            for i in range(3):
                round_third(first_third(call) + i, i)
            with act.Fori(0, DEPTH) as L:
                lam = L + DEPTH * call
                third = first_third(call) + 3 * (L + 1)

                def step(g, c, par, front, mid, late, back):
                    if front:
                        act.wait_ge(s["q_mm"], START + g + 1)
                        act.wait_ge(s["aq_done"], START + g)
                        act.wait_ge(s["bq_done"], START + g)
                        act.activation(raw[0], slot[0][:, :], ACT.Copy).then_inc(s["q_copy"], 1)
                    if late:
                        act.wait_ge(s["sub_done"], START + g - 1)
                        act.activation(probs[:, :], probs[:, :], ACT.Exp).then_inc(s["probs_exp"], 1)
                    if front:
                        act.wait_ge(s["ck_done"], START + g)
                        act.activation(sq[:, :], slot[0][:, :], ACT.Square).then_inc(s["q_evac"], 1)
                    if mid:
                        act.wait_ge(s["tq_mm"], START + g)
                        act.wait_ge(s["s_mm"], START + g - 1)
                        act.activation(qT[:, :, :].rearrange("p j t -> p (j t)"), slot[1][:, :], ACT.Copy)\
                           .then_inc(s["qT_sb"], 1)
                    if front:
                        act.wait_ge(s["k_mm"], START + g + 1)
                        act.wait_ge(s["ak_done"], START + g)
                        act.wait_ge(s["bk_done"], START + g)
                        act.activation(raw[1], slot[3][:, :], ACT.Copy).then_inc(s["k_copy"], 1)
                    if late:
                        act.wait_ge(s["pt_mm"], START + g - 1)
                        act.wait_ge(s["pv_mm"], START + back_to(g, c, 2))
                        act.activation(probsT[:, :, :].rearrange("p j t -> p (j t)"), slot[2][:, :], ACT.Copy)\
                           .then_inc(s["pt_sb"], 1)
                    if front:
                        act.wait_ge(s["cq_done"], START + g + 1)
                        act.activation(sq[:, :], slot[3][:, :], ACT.Square).then_inc(s["k_evac"], 1)
                    if mid:
                        act.wait_ge(s["kT_sb"], START + g - 1)
                        act.activation(kT[:, :, 0:32], kT[:, :, 128:160], ACT.Copy, scale=const("cross"))\
                           .then_inc(s["kT_cross"], 1)
                        act.wait_ge(s["tk_mm"], START + g)
                        act.wait_ge(s["kT_cross"], START + g)
                        act.activation(kT[:, :, 32:160], slot[0][:, :].rearrange("p (j t) -> p j t", j=8), ACT.Copy)\
                           .then_inc(s["kT_sb"], 1)
                    if back:
                        act.wait_ge(s["ot_mm"], START + g - 2)
                        act.wait_ge(s["y_mm"], START + back_to(g, c, 3))
                        act.activation(OT[:, :, :].rearrange("p j t -> p (j t)"), slot[1][:, :], ACT.Copy)\
                           .then_inc(s["ot_sb"], 1)
                    if front:
                        act.wait_ge(s["v_mm"], START + g + 1)
                        act.wait_ge(s["vs_in"], START + VS * g)
                        act.activation(V[par][:, :].rearrange("p (x j d) -> p j x d", x=2, d=DH),
                                       slot[3][:, :].rearrange("p (j x d) -> p j x d", x=2, d=DH), ACT.Copy)\
                           .then_inc(s["v_sb"], 1)
                n = (n0 + 1 + L) * NB
                steps(act, lam, step, 0, NCH)
                act_square(act, n, 0)
                act.wait_ge(s["v_mm"], START + (lam + 1) * NCH)
                round_third(third, 0)
                steps(act, lam, step, NCH + 1, NCH + 1)
                round_third(third + 1, 1)
                steps(act, lam, step, NCH + 2, LAST)
                round_third(third + 2, 2)
                act.wait_ge(s["ffn_in"], START + (lam + 1) * 16 * 13)
                for b in range(NB):
                    f = lam * NB + b
                    if b + 1 < NB:
                        act_square(act, n + b + 1, b + 1)
                    for t, (j, a, m) in enumerate(tiles_of(b)):
                        act.wait_ge(s["w1_mm"], START + f * 3 + t + 1)
                        if b >= 1:
                            act.wait_ge(s["hid_done"], START + read_before(f, t))
                        act.activation(gate[0:m, j, :], slot[j + 1][0:m, 512:1024], ACT.Gelu,
                                       bias=b1[0:m, 1, j:j + 1]).then_inc(s["gelu_done"], 1)

        def pool_stack(pool, call):
            n0 = LN_S0 if call == 0 else LN_S1
            def rest_of_third(count, i):
                cols = slice(i * INNER, (i + 1) * INNER)
                pool.wait_ge(s["w_hi_done"], START + count + 1)
                pool.tensor_tensor(w_lo[:, cols], w_raw[:, :], w_hi[:, cols].bitcast(F32), ALU.subtract)\
                    .then_inc(s["w_lo_done"], 1)

            for i in range(3):
                rest_of_third(first_third(call) + i, i)
            with pool.Fori(0, DEPTH) as L:
                lam = L + DEPTH * call
                third = first_third(call) + 3 * (L + 1)
                pool.wait_ge(s["tables_done"], START + 4 * (lam + 1))

                def sin_half(i, c, copied, done):
                    pool.wait_ge(*copied)
                    src = raw[i].rearrange("p (h x d) -> p h x d", h=H, x=2)
                    dst = rot_sin[i].rearrange("p (h x d) -> p h x d", h=H, x=2)
                    for x in range(2):
                        tab = rot[2 * i + 1][:, bass.ds(c * DH + 32 * x, 32)].unsqueeze(1).to_broadcast([128, H, 32])
                        ins = pool.tensor_tensor(dst[:, :, x, :], src[:, :, 1 - x, :], tab, ALU.mult)
                    ins.then_inc(s[done], 1)

                def inverse(i, g, n_done, used, done):
                    pool.wait_ge(s[n_done], START + g + 1)
                    pool.wait_ge(s[used], START + g)
                    pool.tensor_tensor(inv_norm[i][:, :], norm2c[i][:, :], minus_half[:, 0:H], ALU.pow)\
                        .then_inc(s[done], 1)

                def step(g, c, par, front, mid, late, back):
                    if front:
                        pool.wait_ge(s["rq_done"], START + g)
                        sin_half(0, c, (s["q_copy"], START + g + 1), "bq_done")
                        inverse(0, g, "nq_done", "qn_done", "iq_done")
                        pool.wait_ge(s["rk_done"], START + g)
                        sin_half(1, c, (s["k_copy"], START + g + 1), "bk_done")
                        pool.wait_ge(s["aq_done"], START + g + 1)
                        pool.wait_ge(s["bq_done"], START + g + 1)
                        pool.tensor_tensor(rot_out[0][:, :], rot_out[0][:, :], rot_sin[0], ALU.add)\
                            .then_inc(s["rq_done"], 1)
                        inverse(1, g, "nk_done", "kn_done", "ik_done")
                steps(pool, lam, step)
                rest_of_third(third, 0)
                pool_rstd(pool, (n0 + 1 + L) * NB, 0)
                rest_of_third(third + 1, 1)
                rest_of_third(third + 2, 2)
                for b in range(1, NB):
                    pool_rstd(pool, (n0 + 1 + L) * NB + b, b)

        def dve_stack(dve, call):
            n0 = LN_S0 if call == 0 else LN_S1
            with dve.Fori(0, DEPTH) as L:
                lam = L + DEPTH * call

                def take_chunk(g, c, par, used):
                    dve.wait_ge(s["v_mm"], START + used)
                    x = XA[:, bass.ds(c * 128, 128)]
                    dve.tensor_copy(x_hi[par][:, :], x).then_inc(s["xh_done"], 1)
                    dve.wait_ge(s["xh_done"], START + g + 1)
                    dve.tensor_tensor(x_lo[par][:, :], x, x_hi[par][:, :].bitcast(F32), ALU.subtract)\
                       .then_inc(s["xc_done"], 1)
                dve.wait_ge(s["stack_in"], START + NB * (call + 1) * 2)
                dve.wait_ge(s["f_done"], START + 2 * NB * lam)
                take_chunk(lam * NCH, 0, 0, lam * NCH)
                take_chunk(lam * NCH + 1, 1, 1, lam * NCH)
                dve.wait_ge(s["scales_in"], START + (lam + 1) * 96)
                dve.wait_ge(s["bk_done"], START + lam * NCH)
                for i, name in enumerate(("rot_q_cos", "rot_q_sin", "rot_k_cos", "rot_k_sin")):
                    dve.tensor_tensor(rot[i][:, :].rearrange("p (c d) -> p c d", d=DH),
                                      const(name).rearrange("p (c d) -> p c d", d=DH),
                                      qk_scales[:, i:i + 1, :].to_broadcast([128, NCH, DH]), ALU.mult)\
                       .then_inc(s["tables_done"], 1)
                dve.wait_ge(s["tables_done"], START + 4 * (lam + 1))

                def heads(a):
                    return a.rearrange("p (h d) -> p h d", h=H)

                def cos_half(i, g, c, copied, used, done):
                    dve.wait_ge(s[copied], START + g + 1)
                    dve.wait_ge(s[used], START + g)
                    tab = rot[2 * i][:, bass.ds(c * DH, DH)].unsqueeze(1).to_broadcast([128, H, DH])
                    dve.tensor_tensor(heads(rot_out[i][:, :]), heads(raw[i]), tab, ALU.mult).then_inc(s[done], 1)

                def norm_squared(i, g, squared, summed, used, done):
                    dve.wait_ge(s[squared], START + g + 1)
                    dve.tensor_reduce(norm2[i][:, :], heads(sq[:, :]), AX.X, ALU.add).then_inc(s[summed], 1)
                    dve.wait_ge(s[summed], START + g + 1)
                    dve.wait_ge(s[used], START + g)
                    dve.tensor_scalar(norm2c[i][:, :], norm2[i][:, :], 1e-24, None, ALU.max)\
                       .then_inc(s[done], 1)

                def normalise(i, g, summed, inverted, done):
                    dve.wait_ge(s[summed], START + g + 1)
                    dve.wait_ge(s[inverted], START + g + 1)
                    v = heads(rot_out[i][:, :])
                    dve.tensor_tensor(v, v, inv_norm[i][:, :].unsqueeze(2).to_broadcast([128, H, DH]), ALU.mult)\
                       .then_inc(s[done], 1)

                def step(g, c, par, front, mid, late, back):
                    by_bank = slot[2][:, :].rearrange("p (x j k) -> p j x k", x=2, k=64)
                    if late:
                        dve.wait_ge(s["s_mm"], START + g - 1)
                        dve.tensor_reduce(row_max[:, :], slot[2][:, :].rearrange("p (h k) -> p h k", h=H),
                                          AX.X, ALU.max).then_inc(s["max_done"], 1)
                        dve.wait_ge(s["max_done"], START + g - 1)
                        dve.wait_ge(s["pt_mm"], START + back_to(g, c, 2))
                        dve.tensor_tensor(probs[:, :].rearrange("p (j x k) -> p j x k", x=2, k=64), by_bank,
                                          row_max[:, :].rearrange("p (x j) -> p j x", x=2).unsqueeze(3)
                                          .to_broadcast([128, 8, 2, 64]), ALU.subtract).then_inc(s["sub_done"], 1)
                    if front:
                        cos_half(0, g, c, "q_copy", "tq_mm", "aq_done")
                        norm_squared(0, g, "q_evac", "cq_done", "iq_done", "nq_done")
                    if late:
                        dve.wait_ge(s["probs_exp"], START + g - 1)
                        dve.tensor_reduce(row_sum[:, :], heads(probs[:, :]), AX.X, ALU.add).then_inc(s["sum_done"], 1)
                        dve.wait_ge(s["sum_done"], START + g - 1)
                        dve.reciprocal(row_inv[:, :], row_sum[:, :]).then_inc(s["inv_done"], 1)
                    if front:
                        cos_half(1, g, c, "k_copy", "tk_mm", "ak_done")
                        norm_squared(1, g, "k_evac", "ck_done", "ik_done", "nk_done")
                    if late:
                        dve.wait_ge(s["pv_mm"], START + g - 1)
                        dve.wait_ge(s["inv_done"], START + g - 1)
                        dve.wait_ge(s["ot_mm"], START + back_to(g, c, 2))
                        dve.tensor_tensor(Os[:, :].rearrange("p (j x d) -> p j x d", x=2, d=DH), by_bank,
                                          row_inv[:, :].rearrange("p (j x) -> p j x", x=2).unsqueeze(3)
                                          .to_broadcast([128, 8, 2, DH]), ALU.mult).then_inc(s["on_done"], 1)
                    if front:
                        dve.wait_ge(s["ak_done"], START + g + 1)
                        dve.wait_ge(s["bk_done"], START + g + 1)
                        dve.tensor_tensor(rot_out[1][:, :], rot_out[1][:, :], rot_sin[1], ALU.add)\
                           .then_inc(s["rk_done"], 1)
                    if front:
                        normalise(0, g, "rq_done", "iq_done", "qn_done")
                    if front and (not isinstance(c, int) or 0 < c < NCH - 1):
                        take_chunk(g + 1, c + 1, 1 - par, back_to(g, c, 0))
                    if front:
                        normalise(1, g, "rk_done", "ik_done", "kn_done")
                    if back:
                        dve.wait_ge(s["y_mm"], START + g - 2)
                        t0 = (c - 3) * 128
                        for p, o in ((slice(0, 64), 0), (slice(64, 128), 1)):
                            dve.tensor_tensor(XB[p, bass.ds(t0 + o, 128)], XA[p, bass.ds(t0 + o, 128)],
                                              slot[1][p, 0:128], ALU.add).then_inc(s["xb_done"], 1)

                idx = n0 + 1 + L
                n = idx * NB
                finish = dve_affine(dve, idx, normed, ffn_cols[:, 0:1], ffn_cols[:, 1:2])

                def centre(b):
                    dve.wait_ge(s["xb_done"], START + 2 * (lam * NCH) + 8 * (b + 1))
                    dve_centre(dve, slot[0], n + b, b, XB[:, b * 512:b * 512 + 512])
                steps(dve, lam, step, 0, NCH)
                centre(0)
                steps(dve, lam, step, NCH + 1, NCH + 1)
                dve_eps(dve, slot[0], n, 0, 1e-5)
                steps(dve, lam, step, NCH + 2, NCH + 2)
                dve_diag(dve, n, 0)
                dve.wait_ge(s["ffn_in"], START + (lam + 1) * 16 * 13)
                dve_finish(dve, slot[0], n, 0, finish)
                for b in range(NB):
                    f = lam * NB + b
                    if b + 1 < NB:
                        centre(b + 1)
                    for t, (j, a, m) in enumerate(tiles_of(b)):
                        if t == 1 and b + 1 < NB:
                            dve_diag(dve, n + b + 1, b + 1)
                        dve.wait_ge(s["gelu_done"], START + f * 3 + t + 1)
                        dve.wait_ge(s["w2_mm"], START + f)
                        dve.scalar_tensor_tensor(out=hidden[0:m, j, :], in0=slot[j + 1][0:m, 0:512],
                                                 scalar=b1[0:m, 0, j:j + 1], in1=gate[0:m, j, :],
                                                 op0=ALU.add, op1=ALU.mult).then_inc(s["hid_done"], 1)
                        if t == 0 and b + 1 < NB:
                            dve_eps(dve, slot[0], n + b + 1, b + 1, 1e-5)
                    if b + 1 < NB:
                        dve_finish(dve, slot[0], n + b + 1, b + 1, finish)
                    dve.wait_ge(s["w2_mm"], START + f + 1)
                    for p, o in ((slice(0, 64), 0), (slice(64, 128), 1)):
                        cols = slice(b * 512 + o, b * 512 + o + 512)
                        dve.scalar_tensor_tensor(out=XA[p, cols], in0=slot[b % 3 + 1][p, 0:512], scalar=ffn_cols[p, 2:3],
                                                 in1=XB[p, cols], op0=ALU.add, op1=ALU.add).then_inc(s["f_done"], 1)
            dve.wait_ge(s["f_done"], START + 2 * NB * DEPTH * (call + 1))
            for b in range(NB):
                for p, o in ((slice(0, 64), 0), (slice(64, 128), 1)):
                    dve.tensor_tensor(XM[p, b * 512:b * 512 + 512], XM[p, b * 512:b * 512 + 512],
                                      XA[p, b * 512 + o:b * 512 + o + 512], ALU.add).then_inc(s["xm_done"], 1)

        A_PE_ROWS = 24
        XM0 = 8 * ("S0" in stages)
        QB_UNITS = [4 * q + 4 for q in range(NB)]
        A_UNITS = sum(QB_UNITS)
        A_TILES = [(i, u) for i in range(NCH) for u in range(1 + (i >= 8))]
        PER_HEAD = len(A_TILES)

        def sp_setup(sp):
            sp.dma_start(consts[:, :], A["shape_constants"]).then_inc(s["consts_in"], 16)
            sp.dma_start(x_nat[:, :, :], A["x"][0].rearrange("(c p) d -> p c d", p=128)).then_inc(s["x_in"], 16)
            sp.dma_start(wqkv_nat[:, :, :], A["w_qkv"].rearrange("(c p) d -> p c d", p=128)).then_inc(s["wa_in"], 16)
            sp.dma_start(wout_nat[:, :], A["w_out"]).then_inc(s["wa_in"], 16)

        def pool_setup(pool):
            pool.memset(minus_half[:, :], -0.5).then_inc(s["setup_pool"], 1)
            pool.memset(ones[:, :], 1.0).then_inc(s["setup_pool"], 1)
            pool.memset(V4[:, :, :, :], 0.0).then_inc(s["setup_pool"], 1)
            pool.wait_ge(s["setup_pool"], START + 3)
            pool.memset(V4[:, :, :, 8:9], 1.0).then_inc(s["setup_pool"], 1)
            pool.wait_ge(s["setup_pool"], START + 4)

        def pe_setup(pe):
            pe.wait_ge(s["consts_in"], START + 16)
            pe.wait_ge(s["x_in"], START + 16)
            for c in range(NCH):
                mm = pe.transpose(slot[c // 8][:, (c % 8) * 128:(c % 8) * 128 + 128], x_nat[:, c, :], ident)
            mm.then_inc(s["tr_x"], 1)
            pe.wait_ge(s["wa_in"], START + 32)
            for c in range(3):
                mm = pe.transpose(slot[2][:, c * 128:(c + 1) * 128], wqkv_nat[:, c, :], ident)
            mm.then_inc(s["tr_x"], 1)
            pe.wait_ge(s["wa_rows"], START + 1)
            for g in range(4):
                mm = pe.transpose(slot[3][:, g * 128:(g + 1) * 128],
                                  wout_pad[:, 4 * g:4 * g + 4, :].rearrange("p h r -> p (h r)"), ident)
            mm.then_inc(s["tr_wo"], 1)

        def act_setup(act):
            act.wait_ge(s["tr_x"], START + 1)
            for i in range(2):
                act.activation(XM[:, i * 1024:(i + 1) * 1024], slot[i][:, :], ACT.Copy).then_inc(s["setup_act"], 1)
            act.wait_ge(s["tr_wo"], START + 1)
            act.activation(wout_rows[:, :, :].rearrange("p g n -> p (g n)"), slot[3][:, 0:512], ACT.Copy)\
               .then_inc(s["setup_act"], 1)

        def dve_setup(dve):
            dve.memset(wq_rows[:, :, :], 0.0)
            dve.memset(wk_rows[:, :, :], 0.0)
            dve.memset(wout_pad[:, :, :], 0.0)
            dve.memset(part_max[:, :, :], -3.0e38)
            dve.memset(neg_max[:, :], 0.0)
            dve.memset(XA[64:128, 0:1], 0.0)
            dve.memset(XB[64:128, 0:1], 0.0).then_inc(s["setup_dve"], 1)
            dve.wait_ge(s["setup_dve"], START + 1)
            dve.wait_ge(s["wa_in"], START + 32)
            dve.tensor_copy(wout_pad[:, :, 0:AH], wout_nat[:, :].rearrange("p (h d) -> p h d", d=AH))\
               .then_inc(s["wa_rows"], 1)
            dve.wait_ge(s["consts_in"], START + 16)
            dve.tensor_copy(ident_b[:, :], ident)
            dve.tensor_copy(mask_qk[:, :], const("mask_qk"))
            dve.tensor_copy(mask_kq[:, :], const("mask_kq"))
            dve.tensor_copy(mask_win[:, :, :], const("mask_win").rearrange("p (a k) -> p a k", a=2))\
               .then_inc(s["setup_dve"], 1)
            dve.wait_ge(s["tr_x"], START + 2)
            wt = slot[2][:, 0:384].rearrange("p (c h d) -> p c h d", c=3, d=AH)
            for rep in range(3):
                rows = slice(AH * rep, AH * rep + AH)
                dve.tensor_scalar(wq_rows[:, :, rows], wt[:, 0], AH ** -0.5, None, ALU.mult)
                dve.tensor_copy(wk_rows[:, :, rows], wt[:, 1])
            dve.tensor_copy(wv_cols[:, :], slot[2][:, 256:384]).then_inc(s["setup_dve"], 1)

        def sp_first(sp):
            with sp.Fori(0, 4) as g:
                sp.wait_ge(s["a_hi"], START + g + 1)
                sp.sem_inc(s["passed"], 1)
                sp.wait_ge(s["a_lo"], START + g + 1)
                for j, src in enumerate((neg_hi, neg_lo)):
                    sp.dma_start(rows_dram[j], src[:, :].bitcast(F32)).then_inc(s["a_rows"], 16)
                sp.wait_ge(s["a_rows"], START + 32 * (g + 1))
                for hh in range(4):
                    for j in range(2):
                        r = 32 * hh + A_PE_ROWS + j
                        sp.dma_start(QT[r:r + 1, :].bitcast(F32),
                                     rows_dram[j:j + 1, 16 * hh:16 * hh + 16, :].rearrange("a i t -> a (i t)"))\
                          .then_inc(s["a_dma"], 16)

        def pe_first(pe):
            pe_norm(pe, LN_A, lambda b: XM[:, b * 512:b * 512 + 512],
                    lambda b: (pe.wait_ge(s["setup_act"], START + 3), pe.wait_ge(s["setup_dve"], START + 3),
                               pe.wait_ge(s["setup_pool"], START + 4)))
            pe.wait_ge(s["ln_done"], START + NB)
            with pe.Fori(0, 4) as g:
                pe.wait_ge(s["a_w"], START + g + 1)
                for b in range(NB):
                    if b == 3:
                        pe.wait_ge(s["a_yadd"], START + 4 * g)
                    for i, w in enumerate((gq_w, gk_w)):
                        mm = pe.matmul(slot[b][:, i * 512:(i + 1) * 512], w[:, :], normed[:, b * 512:b * 512 + 512],
                                       start=True, stop=True)
                    mm.then_inc(s["a_qk"], 1)
                pe.wait_ge(s["a_split"], START + 4 * g + 1)
                for k in range(NCH):
                    mm = pe.matmul(slot[0][:, 32 * k:32 * k + 32], normed[:, k * 128:k * 128 + 128], gv_w[:, :],
                                   start=True, stop=True)
                mm.then_inc(s["a_v"], 1)
                pe.wait_ge(s["a_vsb"], START + g + 1)
                pe.wait_ge(s["a_split"], START + 4 * g + 4)
                n = 0
                for hh in range(4):
                    rows = slice(32 * hh, 32 * hh + A_PE_ROWS)
                    for i, u in A_TILES:
                        if n >= 4:
                            pe.wait_ge(s["a_max"], START + 4 * PER_HEAD * g + n - 3)
                        width = min(1024, 128 * (i + 1) - 1024 * u)
                        last = 128 * (i + 1) - 1024 * u <= 1024
                        for a in range(0, width, 512):
                            m = min(512, width - a)
                            diag = last and a + m == width
                            mm = pe.matmul(slot[n % 4][:, a:a + m], QT[rows, 128 * i:128 * i + 128],
                                           KT[rows, 1024 * u + a:1024 * u + a + m], start=True, stop=True)
                            if diag:
                                mm = pe.matmul(slot[n % 4][:, width - 128:width], ident_b[:, :], mask_qk[:, :],
                                               start=False, stop=True, skip_group_check=True)
                        mm.then_inc(s["a_s1"], 1)
                        n += 1
                pe.wait_ge(s["a_neg"], START + g + 1)
                pe.transpose(slot[0][:, 0:128], neg_max[:, :], ident).then_inc(s["a_nt"], 1)
                pe.wait_ge(s["a_dma"], START + 128 * (g + 1))
                units = [(qb, k) for qb in range(NB) for k in range(QB_UNITS[qb])]

                def scores(n):
                    qb, k = units[n]
                    c0 = max(0, 128 * (k - 4 * qb))
                    for half in range(2):
                        h2 = 2 * n + half
                        if h2 >= 3:
                            pe.wait_ge(s["a_exp"], START + 2 * A_UNITS * g + h2 - 2)
                        for e in range(2):
                            hh = 2 * half + e
                            rows = slice(32 * hh, 32 * hh + A_PE_ROWS + 2)
                            diag = k >= 4 * qb
                            o = slot[h2 % 3]
                            mm = pe.matmul(o[:, 512 * e + c0:512 * e + 512], KT[rows, 128 * k:128 * k + 128],
                                           QT[rows, 512 * qb + c0:512 * qb + 512], start=True, stop=True)
                            if diag:
                                mm = pe.matmul(o[:, 512 * e + c0:512 * e + c0 + 128], ident_b[:, :], mask_kq[:, :],
                                               start=False, stop=True, skip_group_check=True)
                        mm.then_inc(s["a_s"], 1)

                def values(n):
                    qb, k = units[n]
                    c0 = max(0, 128 * (k - 4 * qb))
                    pe.wait_ge(s["a_exp"], START + 2 * A_UNITS * g + 2 * n + 2)
                    if k == 0:
                        pe.wait_ge(s["a_osb"], START + 4 * g + qb)
                    for hh in range(4):
                        mm = pe.matmul(slot[3][32 * hh:32 * hh + 32, c0:512], V4[:, k, hh, :],
                                       Pa[:, (2 * n + hh // 2) % 4, 512 * (hh % 2) + c0:512 * (hh % 2) + 512],
                                       start=(k == 0), stop=(k >= 4 * qb), skip_group_check=True)
                    mm.then_inc(s["a_pv"], 1)

                def sums(qb):
                    pe.wait_ge(s["a_osb"], START + 4 * g + qb + 1)
                    pe.wait_ge(s["a_yadd"], START + 4 * g + qb)
                    pe.matmul(slot[3][:, 512:1024], const("sum_rows"), Oa[:, :], start=True, stop=True)\
                      .then_inc(s["a_bc"], 1)

                def project(qb):
                    pe.wait_ge(s["a_on"], START + 4 * g + qb + 1)
                    pe.matmul(slot[3][:, 512:1024], go_w[:, :], On[:, :], start=True, stop=True)\
                      .then_inc(s["a_y"], 1)

                scores(0)
                for n, (qb, k) in enumerate(units):
                    if n + 1 < len(units):
                        scores(n + 1)
                    values(n)
                    if qb >= 1 and k == 1:
                        sums(qb - 1)
                    if qb >= 1 and k == 5:
                        project(qb - 1)
                sums(NB - 1)
                project(NB - 1)

        def act_first(act):
            act.wait_ge(s["setup_pool"], START + 4)
            act_norm(act, LN_A)
            with act.Fori(0, 4) as g:
                for b in range(NB):
                    act.wait_ge(s["a_qk"], START + 4 * g + b + 1)
                    act.activation(rounded[:, b % 2, :], slot[b][:, :], ACT.Copy).then_inc(s["a_round"], 1)
                    act.wait_ge(s["a_round"], START + 4 * g + b + 1)
                    act.wait_ge(s["a_split"], START + 4 * g + (b - 1 if b >= 2 else 0))
                    act.activation(scaled[:, b % 2, 0:512], rounded[:, b % 2, 0:512].bitcast(F32), ACT.Copy,
                                   scale=const("rows")[:, 0:1])
                    act.activation(scaled[:, b % 2, 512:1024], rounded[:, b % 2, 512:1024].bitcast(F32),
                                   ACT.Identity, scale=const("rows")[:, 2:3], bias=const("rows")[:, 4:5])\
                       .then_inc(s["a_scaled"], 1)
                act.wait_ge(s["a_v"], START + g + 1)
                act.wait_ge(s["a_pv"], START + A_UNITS * g)
                act.activation(V4[:, :, :, 0:AH].rearrange("p k h d -> p (k h) d"),
                               slot[0][:, 0:512].rearrange("p (x d) -> p x d", d=AH), ACT.Copy)\
                   .then_inc(s["a_vsb"], 1)
                act.wait_ge(s["a_nt"], START + g + 1)
                act.wait_ge(s["a_dma"], START + 128 * g)
                act.activation(neg_hi[:, :], slot[0][0:64, 0:128], ACT.Copy).then_inc(s["a_hi"], 1)
                units = [(qb, k) for qb in range(NB) for k in range(QB_UNITS[qb])]

                def take_output(qb):
                    act.wait_ge(s["a_pv"], START + A_UNITS * g + sum(QB_UNITS[:qb + 1]))
                    act.wait_ge(s["a_on"], START + 4 * g + qb)
                    act.activation(Oa[:, :], slot[3][:, 0:512], ACT.Copy).then_inc(s["a_osb"], 1)
                for n, (qb, k) in enumerate(units):
                    c0 = max(0, 128 * (k - 4 * qb))
                    for half in range(2):
                        h2 = 2 * n + half
                        act.wait_ge(s["a_s"], START + 2 * A_UNITS * g + h2 + 1)
                        if n >= 2:
                            act.wait_ge(s["a_pv"], START + A_UNITS * g + n - 1)
                        act.activation(Pa[:, h2 % 4, :].rearrange("p (e q) -> p e q", e=2)[:, :, c0:512],
                                       slot[h2 % 3][:, :].rearrange("p (e q) -> p e q", e=2)[:, :, c0:512],
                                       ACT.Exp).then_inc(s["a_exp"], 1)
                    if qb >= 1 and k == 0:
                        take_output(qb - 1)
                take_output(NB - 1)

        def dve_first(dve):
            dve.wait_ge(s["setup_act"], START + 2)
            dve_norm(dve, LN_A, lambda b: XM[:, b * 512:b * 512 + 512], 1e-5, dve_plain(dve, LN_A, normed))
            dve.wait_ge(s["setup_act"], START + 3)
            dve.wait_ge(s["setup_dve"], START + 3)
            with dve.Fori(0, 4) as g:
                dve.wait_ge(s["a_y"], START + 4 * g)
                dve.tensor_copy(gq_w[:, :], wq_rows[:, :, :].rearrange("p h r -> p (h r)")[:, bass.ds(g * 128, 128)])
                dve.tensor_copy(gk_w[:, :], wk_rows[:, :, :].rearrange("p h r -> p (h r)")[:, bass.ds(g * 128, 128)])
                dve.tensor_copy(gv_w[:, :], wv_cols[:, bass.ds(g * 32, 32)])
                dve.tensor_copy(go_w[:, :], wout_rows[:, :, :].rearrange("p g n -> p (g n)")[:, bass.ds(g * 128, 128)])\
                   .then_inc(s["a_w"], 1)
                for b in range(NB):
                    dve.wait_ge(s["a_scaled"], START + 4 * g + b + 1)
                    cols = slice(b * 512, b * 512 + 512)
                    dve.scalar_tensor_tensor(out=QT[:, cols], in0=slot[b][:, 0:512], scalar=const("rows")[:, 1:2],
                                             in1=scaled[:, b % 2, 0:512], op0=ALU.mult, op1=ALU.add)
                    dve.scalar_tensor_tensor(out=KT[:, cols], in0=slot[b][:, 512:1024], scalar=const("rows")[:, 3:4],
                                             in1=scaled[:, b % 2, 512:1024], op0=ALU.mult, op1=ALU.add)\
                       .then_inc(s["a_split"], 1)
                n = 0
                for hh in range(4):
                    for i, u in A_TILES:
                        width = min(1024, 128 * (i + 1) - 1024 * u)
                        dve.wait_ge(s["a_s1"], START + 4 * PER_HEAD * g + n + 1)
                        dve.tensor_reduce(part_max[:, 16 * hh + i, u:u + 1], slot[n % 4][:, 0:width], AX.X, ALU.max)\
                           .then_inc(s["a_max"], 1)
                        n += 1
                dve.wait_ge(s["a_max"], START + 4 * PER_HEAD * (g + 1))
                dve.wait_ge(s["a_nt"], START + g)
                dve.tensor_tensor(neg_max[:, 0:64], part_max[:, :, 0], part_max[:, :, 1], ALU.max)\
                   .then_inc(s["a_comb"], 1)
                dve.wait_ge(s["a_comb"], START + g + 1)
                dve.tensor_scalar(neg_max[:, 0:64], neg_max[:, 0:64], -1.0, None, ALU.mult).then_inc(s["a_neg"], 1)
                dve.wait_ge(s["a_hi"], START + g + 1)
                dve.tensor_tensor(neg_lo[:, :], slot[0][0:64, 0:128], neg_hi[:, :].bitcast(F32), ALU.subtract)\
                   .then_inc(s["a_lo"], 1)
                for qb in range(NB):
                    dve.wait_ge(s["a_bc"], START + 4 * g + qb + 1)
                    dve.reciprocal(sum_inv[:, :], slot[3][:, 512:1024]).then_inc(s["a_inv"], 1)
                    dve.wait_ge(s["a_inv"], START + 4 * g + qb + 1)
                    dve.tensor_tensor(On[:, :], Oa[:, :], sum_inv[:, :], ALU.mult).then_inc(s["a_on"], 1)
                    dve.wait_ge(s["a_y"], START + 4 * g + qb + 1)
                    cols = slice(qb * 512, qb * 512 + 512)
                    dve.tensor_tensor(XM[:, cols], XM[:, cols], slot[3][:, 512:1024], ALU.add)\
                       .then_inc(s["a_yadd"], 1)

        def xm_ready(eng, call):
            if call == 0:
                eng.wait_ge(s["a_yadd"], START + (16 if "A" in stages else 0))
                eng.wait_ge(s["setup_act"], START + 3)
                eng.wait_ge(s["setup_dve"], START + 3)
            else:
                eng.wait_ge(s["b_yadd"], START + (32 if "B" in stages else 0))
                eng.wait_ge(s["xm_done"], START + XM0)

        def ln_into(call):
            return LN_S0 if call == 0 else LN_S1

        def pe_into(pe, call):
            pe_norm(pe, ln_into(call), lambda b: XM[:, b * 512:b * 512 + 512],
                    lambda b: xm_ready(pe, call))

        def dve_into(dve, call):
            n = ln_into(call)
            xm_ready(dve, call)

            def finish(b, c, r):
                dve.wait_ge(s["stack_in"], START + 8 * call)
                for p, o in ((slice(0, 64), 0), (slice(64, 128), 1)):
                    ins = dve.tensor_tensor(XA[p, b * 512 + o:b * 512 + o + 512], c[p], r[p], ALU.mult)
                    ins.then_inc(s["stack_in"], 1)
                dve.wait_ge(s["stack_in"], START + 8 * call + 2 * b + 2)
                dve.sem_inc(s["ln_half"], 1)
                dve.sem_inc(s["ln_done"], 1)
            dve_norm(dve, n, lambda b: XM[:, b * 512:b * 512 + 512], 1e-5, finish)
            dve.memset(kT[:, :, :], 0.0)
            dve.memset(V[1][:, :], 0.0).then_inc(s["stack_out"], 1)

        def sp_grouped(sp):
            sp.wait_ge(s["xm_done"], START + XM0)
            sp.dma_start(b_wq[:, :], A["Wq"]).then_inc(s["wb_in"], 16)
            sp.dma_start(b_wkv[:, :], A["Wkv"]).then_inc(s["wb_in"], 16)
            sp.dma_start(b_wout[:, :, :], A["Wout"].rearrange("(j p) n -> p j n", p=128)).then_inc(s["wb_in"], 16)
            for j, name in enumerate(("b_ln_scale", "b_ln_bias")):
                sp.dma_start(b_cols[:, j:j + 1], A[name].rearrange("(p a) -> p a", a=1)).then_inc(s["wb_in"], 16)
            for j, name in enumerate(("qn_scale", "qn_bias", "kn_scale", "kn_bias")):
                for r in range(2):
                    sp.dma_start(b_cols[64 * r:64 * r + 64, j + 2:j + 3], A[name].rearrange("(p a) -> p a", a=1))\
                      .then_inc(s["wb_in"], 16)
            def rows_of_pair(p, par):
                sp.wait_ge(s["b_his"], START + p + 1)
                sp.sem_inc(s["passed"], 1)
                sp.wait_ge(s["b_los"], START + p + 1)
                for j, src in enumerate((b_hi, b_lo)):
                    sp.dma_start(rows_dram[j, 0:32, :], src[:, :].bitcast(F32)).then_inc(s["b_rows"], 16)
                sp.wait_ge(s["b_rows"], START + 32 * (p + 1))
                for hh in range(2):
                    for j in range(2):
                        sp.dma_start(QB[par][hh][64 + j:65 + j, :].bitcast(F32),
                                     rows_dram[j:j + 1, 16 * hh:16 * hh + 16, :].rearrange("a i t -> a (i t)"))\
                          .then_inc(s["b_dma"], 16)

            with sp.Fori(0, 4) as kv:
                for pr in range(2):
                    rows_of_pair(kv * 2 + pr, pr)

        WB_IN = 16 * 13
        def ln_k(kv):
            return LN_B + 2 + 3 * kv

        def ln_q(kv, pr):
            return LN_B + 3 + 3 * kv + pr

        B_UNITS = 64

        def unit_y(n):
            return n // 16 - 1 if n >= 16 and n % 16 == 9 else None

        def pe_heads(pe, n, which, ready=lambda b: None):
            m = n * NB
            for b in range(NB):
                ready(b)
                pe.matmul(slot[b][:, 0:512], b_w[:, which, :], z2[:, b * 512:b * 512 + 512], start=True, stop=True)\
                  .then_inc(s["ln_mean"], 1)
            for b in range(NB):
                pe.wait_ge(s["ln_square"], START + m + b + 1)
                for c in range(4):
                    mm = pe.matmul(slot[b][:, 512 + 2 * c:514 + 2 * c], squares[:, b % 2, c * 128:c * 128 + 128],
                                   mean2[:, :], start=True, stop=True)
                mm.then_inc(s["ln_var"], 1)
            for b in range(NB):
                pe.wait_ge(s["ln_diag"], START + m + b + 1)
                for c in range(4):
                    mm = pe.matmul(slot[b][:, 512 + 128 * c:640 + 128 * c], diag[:, b % 2, 128 * c:128 * c + 128],
                                   ident, start=True, stop=True)
                mm.then_inc(s["ln_bc"], 1)

        def pool_heads(pool, n):
            for b in range(NB):
                pool.wait_ge(s["ln_eps"], START + n * NB + b + 1)
                pool.tensor_tensor(b_rstd[:, 8 * b:8 * b + 8], b_variance[:, 8 * b:8 * b + 8], minus_half[:, 0:8],
                                   ALU.pow).then_inc(s["ln_pow"], 1)

        def dve_heads(dve, n, g, bias):
            m = n * NB

            def eps(b):
                dve.wait_ge(s["ln_var"], START + m + b + 1)
                dve.tensor_scalar(b_variance[:, 8 * b:8 * b + 8], slot[b][:, 512:520], 1e-6, None, ALU.add)\
                   .then_inc(s["ln_eps"], 1)

            def spread(b):
                dve.wait_ge(s["ln_pow"], START + m + b + 1)
                dve.wait_ge(s["ln_bc"], START + (m + b - 1 if b >= 2 else m))
                dve.tensor_copy(diag[:, b % 2, :].rearrange("p (c t) -> p c t", c=8),
                                b_rstd[:, 8 * b:8 * b + 8].unsqueeze(2).to_broadcast([128, 8, 64]))\
                   .then_inc(s["ln_diag"], 1)

            finish = dve_affine(dve, n, normed, g, bias)
            for b in range(NB):
                dve.wait_ge(s["ln_mean"], START + m + b + 1)
                dve.tensor_copy(centred[:, b * 512:b * 512 + 512], slot[b][:, 0:512]).then_inc(s["ln_centred"], 1)
            eps(0)
            eps(1)
            spread(0)
            eps(2)
            spread(1)
            eps(3)
            for b in range(NB):
                dve_finish(dve, slot[b], m + b, b, finish)
                if b + 2 < NB:
                    spread(b + 2)

        def pe_max_unit(pe, p, par, keys, n, o):
            hh, i, u = n // 32, n // 2 % 16, n % 2
            kA, kB = keys
            if n % 32 == 0:
                pe_operands(pe, p, hh)
            for a in (0, 512):
                cols = slice(1024 * u + a, 1024 * u + a + 512)
                pe.matmul(o[:, a:a + 512], QA[par][hh][:, 128 * i:128 * i + 128], kA[:, cols], start=True, stop=False)
                mm = pe.matmul(o[:, a:a + 512], QB[par][hh][0:64, 128 * i:128 * i + 128], kB[0:64, cols],
                               start=False, stop=True)
            mm.then_inc(s["b_s1"], 1)

        def pe_operands(pe, p, hh):
            pe.wait_ge(s["b_qhi"], START + 3 * p + (3 if hh else 1))
            pe.wait_ge(s["b_qlo"], START + 3 * p + (3 if hh else 2))

        def pe_turn_maxima(pe, p):
            pe.wait_ge(s["b_neg"], START + p + 1)
            pe.transpose(slot[2][:, 512:640], b_nmax[:, :], ident).then_inc(s["b_nt"], 1)

        def pe_pair(pe, p, par, following):
            pe.wait_ge(s["b_dma"], START + 64 * (p + 1))
            pe.wait_ge(s["wo_done"], START + p + 1)

            def scores(n):
                if n >= 2:
                    pe.wait_ge(s["b_exp"], START + B_UNITS * p + n - 1)
                qb, k = n // 16, n % 16
                o = slot[n % 2]
                for hh in range(2):
                    pe.matmul(o[:, 512 * hh:512 * hh + 512], KA[:, 128 * k:128 * k + 128],
                              QA[par][hh][:, 512 * qb:512 * qb + 512], start=True, stop=False)
                    mm = pe.matmul(o[:, 512 * hh:512 * hh + 512], KB[:, 128 * k:128 * k + 128],
                                   QB[par][hh][:, 512 * qb:512 * qb + 512], start=False, stop=True)
                mm.then_inc(s["b_s"], 1)

            def values(n):
                qb, k = n // 16, n % 16
                pe.wait_ge(s["b_exp"], START + B_UNITS * p + n + 1)
                if k == 0:
                    pe.wait_ge(s["b_rnd"], START + NB * p + qb)
                for hh in range(2):
                    mm = pe.matmul(slot[3][64 * hh:64 * hh + 64, 0:512], Vb[:, k, :],
                                   Pb[:, n % B_RING, 512 * hh:512 * hh + 512], start=(k == 0), stop=(k == 15),
                                   skip_group_check=True)
                mm.then_inc(s["b_pv"], 1)

            def sums(qb):
                pe.wait_ge(s["b_psum"], START + 60 * p + 15 * (qb + 1))
                pe.wait_ge(s["b_invd"], START + 4 * (NB * p + qb))
                for hh in range(2):
                    mm = pe.matmul(slot[3][64 * hh:64 * hh + 64, 512:1024], ones[:, 0:64],
                                   b_sum[:, qb % 2, 512 * hh:512 * hh + 512], start=True, stop=True,
                                   skip_group_check=True)
                mm.then_inc(s["b_lsum"], 1)

            def project(qb, o):
                pe.wait_ge(s["b_on"], START + NB * p + qb + 1)
                pe.matmul(o, b_wo[:, :], Ob[:, :], start=True, stop=True).then_inc(s["b_y"], 1)

            for n in range(B_UNITS):
                scores(n)
                qb = unit_y(n)
                if following is not None:
                    q, q_par, keys = following
                    if n:
                        pe.wait_ge(s["b_max"], START + B_UNITS * q + n)
                if qb is not None:
                    project(qb, slot[2][:, 0:512])
                    pe.wait_ge(s["b_yadd"], START + NB * p + qb + 1)
                if following is not None:
                    pe_max_unit(pe, q, q_par, keys, n, slot[2])
                if n:
                    values(n - 1)
                if n >= 16 and n % 16 == 2:
                    sums(n // 16 - 1)
            values(B_UNITS - 1)
            if following is not None:
                pe_turn_maxima(pe, following[0])
            sums(NB - 1)
            pe.wait_ge(s["b_rnd"], START + NB * (p + 1))
            project(NB - 1, slot[3][:, 0:512])
            pe.wait_ge(s["b_yadd"], START + NB * (p + 1))
            if following is not None:
                pe.wait_ge(s["b_los"], START + following[0] + 1)

        def pe_grouped(pe):
            pe_norm(pe, LN_B, lambda b: XM[:, b * 512:b * 512 + 512],
                    lambda b: pe.wait_ge(s["xm_done"], START + XM0))
            pe_norm(pe, LN_B + 1, lambda b: normed[:, b * 512:b * 512 + 512],
                    lambda b: pe.wait_ge(s["ln_done"], START + (LN_B + 1) * NB))
            pe.wait_ge(s["ln_done"], START + (LN_B + 2) * NB)
            pe.wait_ge(s["wk_done"], START + 1)
            pe_heads(pe, ln_k(0), 0)
            pe.wait_ge(s["ln_done"], START + (ln_k(0) + 1) * NB)
            pe.wait_ge(s["wq_done"], START + 1)
            pe_heads(pe, ln_q(0, 0), 1)
            pe.wait_ge(s["b_klo"], START + 1)
            for n in range(B_UNITS):
                if n >= 4:
                    pe.wait_ge(s["b_max"], START + n - 3)
                pe_max_unit(pe, 0, 0, (KA_next, KB_next), n, slot[n % 4])
            pe_turn_maxima(pe, 0)
            pe.wait_ge(s["b_los"], START + 1)

            def group(kv, last):
                pe.wait_ge(s["wv_done"], START + kv + 1)
                for k in range(NCH):
                    mm = pe.matmul(slot[0][:, 64 * k:64 * k + 64], z2[:, k * 128:k * 128 + 128], b_w[:, 2, 0:64],
                                   start=True, stop=True)
                mm.then_inc(s["b_v"], 1)
                pe.wait_ge(s["b_vsb"], START + kv + 1)
                pe.wait_ge(s["wq_done"], START + kv * 2 + 2)
                pe_heads(pe, ln_q(kv, 1), 1)
                pe.wait_ge(s["b_kcur"], START + kv * 2 + 2)
                pe_pair(pe, kv * 2, 0, (kv * 2 + 1, 1, (KA, KB)))
                if not last:
                    pe.wait_ge(s["wk_done"], START + kv + 2)
                    pe_heads(pe, ln_k(kv + 1), 0)
                    pe.wait_ge(s["wq_done"], START + kv * 2 + 3)
                    pe_heads(pe, ln_q(kv + 1, 0), 1,
                             lambda b: pe.wait_ge(s["ln_done"], START + ln_k(kv + 1) * NB + b + 1))
                    pe.wait_ge(s["b_klo"], START + kv + 2)
                pe_pair(pe, kv * 2 + 1, 1, None if last else (kv * 2 + 2, 0, (KA_next, KB_next)))

            with pe.Fori(0, 3) as kv:
                group(kv, False)
            group(3, True)

        def act_heads(act, n):
            act_norm(act, n)

        def act_queries(act, n, p, par):
            act_norm(act, n)
            act.wait_ge(s["ln_done"], START + (n + 1) * NB)
            for hh in range(2):
                r = slice(64 * hh, 64 * hh + 64)
                act.activation(QA[par][hh][0:64, :], normed[r, :], ACT.Copy).then_inc(s["b_qhi"], 1)
            act.activation(QB[par][1][0:64, :], normed[64:128, :], ACT.Copy).then_inc(s["b_qhi"], 1)

        def act_keys(act, kv):
            act_norm(act, ln_k(kv))
            act.wait_ge(s["ln_done"], START + (ln_k(kv) + 1) * NB)
            act.activation(KA_next[:, :], normed[:, :], ACT.Copy).then_inc(s["b_khi"], 1)

        def act_maxima(act, p):
            act.wait_ge(s["b_nt"], START + p + 1)
            act.wait_ge(s["b_dma"], START + 64 * p)
            act.activation(b_hi[:, :], slot[2][0:32, 512:640], ACT.Copy).then_inc(s["b_his"], 1)

        def act_pair(act, p, following):
            def take_output(qb):
                act.wait_ge(s["b_pv"], START + B_UNITS * p + 16 * (qb + 1))
                act.wait_ge(s["b_on"], START + NB * p + qb)
                act.activation(Oc[:, :], slot[3][:, 0:512], ACT.Copy).then_inc(s["b_rnd"], 1)
            for n in range(B_UNITS):
                act.wait_ge(s["b_s"], START + B_UNITS * p + n + 1)
                if n >= B_RING:
                    m = n - B_RING
                    act.wait_ge(s["b_pv"], START + B_UNITS * p + m + 1)
                    act.wait_ge(s["b_psum"], START + 60 * p + 15 * (m // 16) + max(m % 16, 1))
                act.activation(Pb[:, n % B_RING, :], slot[n % 2][:, :], ACT.Exp).then_inc(s["b_exp"], 1)
                if n % 16 == 0 and n:
                    take_output(n // 16 - 1)
            take_output(NB - 1)
            if following is not None:
                act_maxima(act, following)

        def act_grouped(act):
            act_norm(act, LN_B)
            act_norm(act, LN_B + 1)
            act_keys(act, 0)
            act_queries(act, ln_q(0, 0), 0, 0)
            act_maxima(act, 0)

            def group(kv, last):
                act.wait_ge(s["b_v"], START + kv + 1)
                act.activation(Vb[:, :, :].rearrange("p k d -> p (k d)"), slot[0][:, :], ACT.Copy)\
                   .then_inc(s["b_vsb"], 1)
                act.activation(KA[:, :], KA_next[:, :].bitcast(F32), ACT.Copy).then_inc(s["b_kcur"], 1)
                act_queries(act, ln_q(kv, 1), kv * 2 + 1, 1)
                act_pair(act, kv * 2, kv * 2 + 1)
                if not last:
                    act_keys(act, kv + 1)
                    act_queries(act, ln_q(kv + 1, 0), kv * 2 + 2, 0)
                act_pair(act, kv * 2 + 1, None if last else kv * 2 + 2)

            with act.Fori(0, 3) as kv:
                group(kv, False)
            group(3, True)

        def pool_pair(pool, p):
            for qb in range(NB):
                for k in range(1, 16):
                    n = 16 * qb + k
                    done = 60 * p + 15 * qb + k - 1
                    pool.wait_ge(s["b_exp"], START + B_UNITS * p + n + 1)
                    if k == 1 and qb >= 2:
                        pool.wait_ge(s["b_lsum"], START + NB * p + qb - 1)
                    if k > 1:
                        pool.wait_ge(s["b_psum"], START + done)
                    pool.tensor_tensor(b_sum[:, qb % 2, :],
                                       Pb[:, (n - 1) % B_RING, :] if k == 1 else b_sum[:, qb % 2, :],
                                       Pb[:, n % B_RING, :], ALU.add).then_inc(s["b_psum"], 1)

        def pool_grouped(pool):
            for n in (LN_B, LN_B + 1):
                pool_norm(pool, n)
            pool_heads(pool, ln_k(0))
            pool_heads(pool, ln_q(0, 0))

            def group(kv, last):
                pool_heads(pool, ln_q(kv, 1))
                pool_pair(pool, kv * 2)
                if not last:
                    pool_heads(pool, ln_k(kv + 1))
                    pool_heads(pool, ln_q(kv + 1, 0))
                pool_pair(pool, kv * 2 + 1)

            with pool.Fori(0, 3) as kv:
                group(kv, False)
            group(3, True)

        def dve_queries(dve, n, p, par):
            dve_heads(dve, n, b_cols[:, 2:3], b_cols[:, 3:4])
            for hh in range(2):
                r = slice(64 * hh, 64 * hh + 64)
                dve.wait_ge(s["b_qhi"], START + 3 * p + hh + 1)
                dve.tensor_tensor(QA[par][hh][64:128, :], normed[r, :], QA[par][hh][0:64, :].bitcast(F32),
                                  ALU.subtract).then_inc(s["b_qlo"], 1)
                if hh == 0:
                    dve.tensor_copy(QB[par][0][0:64, :], QA[par][0][0:64, :].bitcast(F32)).then_inc(s["b_qlo"], 1)

        def dve_keys(dve, kv):
            dve_heads(dve, ln_k(kv), b_cols[:, 4:5], b_cols[:, 5:6])
            dve.wait_ge(s["b_khi"], START + kv + 1)
            dve.tensor_tensor(KB_next[:, :], normed[0:64, :], KA_next[0:64, :].bitcast(F32), ALU.subtract)\
               .then_inc(s["b_klo"], 1)

        def dve_key_weights(dve, kv):
            dve.tensor_copy(b_w[:, 0, 0:64], b_wkv[:, bass.ds(kv * 64, 64)])
            dve.tensor_copy(b_w[:, 0, 64:128], b_wkv[:, bass.ds(kv * 64, 64)]).then_inc(s["wk_done"], 1)

        def dve_query_weights(dve, p):
            dve.tensor_copy(b_w[:, 1, :], b_wq[:, bass.ds(p * 128, 128)]).then_inc(s["wq_done"], 1)

        def dve_out_weights(dve, p):
            dve.tensor_copy(b_wo[:, :], b_wout[:, :, :].rearrange("p j n -> p (j n)")[:, bass.ds(p * 128, 128)])\
               .then_inc(s["wo_done"], 1)

        def dve_max_unit(dve, p, n, o):
            dve.wait_ge(s["b_s1"], START + B_UNITS * p + n + 1)
            dve.tensor_reduce(b_pmax[:, n // 2, n % 2:n % 2 + 1], o[:, :], AX.X, ALU.max).then_inc(s["b_max"], 1)

        def dve_negate_maxima(dve, p):
            dve.wait_ge(s["b_max"], START + B_UNITS * (p + 1))
            dve.wait_ge(s["b_nt"], START + p)
            dve.tensor_tensor(b_nmax[:, 0:32], b_pmax[:, :, 0], b_pmax[:, :, 1], ALU.max).then_inc(s["b_comb"], 1)
            dve.wait_ge(s["b_comb"], START + p + 1)
            dve.tensor_scalar(b_nmax[:, 0:32], b_nmax[:, 0:32], -1.0, None, ALU.mult).then_inc(s["b_neg"], 1)

        def dve_maxima_rest(dve, p):
            dve.wait_ge(s["b_his"], START + p + 1)
            dve.tensor_tensor(b_lo[:, :], slot[2][0:32, 512:640], b_hi[:, :].bitcast(F32), ALU.subtract)\
               .then_inc(s["b_los"], 1)

        def dve_pair(dve, p, following):
            def invert(qb, j):
                if j == 0:
                    dve.wait_ge(s["b_lsum"], START + NB * p + qb + 1)
                cols = slice(128 * j, 128 * j + 128)
                dve.reciprocal(b_inv[:, cols], slot[3][:, 512 + 128 * j:640 + 128 * j]).then_inc(s["b_invd"], 1)

            def scale(qb):
                dve.wait_ge(s["b_rnd"], START + NB * p + qb + 1)
                dve.wait_ge(s["b_invd"], START + 4 * (NB * p + qb + 1))
                dve.wait_ge(s["b_y"], START + NB * p + qb)
                dve.tensor_tensor(Ob[:, :], Oc[:, :], b_inv[:, :], ALU.mult).then_inc(s["b_on"], 1)

            def add(qb, o):
                dve.wait_ge(s["b_y"], START + NB * p + qb + 1)
                cols = slice(qb * 512, qb * 512 + 512)
                dve.tensor_tensor(XM[:, cols], XM[:, cols], o, ALU.add).then_inc(s["b_yadd"], 1)

            for n in range(B_UNITS):
                qb = unit_y(n)
                if qb is not None:
                    add(qb, slot[2][:, 0:512])
                if following is not None:
                    dve_max_unit(dve, following, n, slot[2])
                if n >= 16 and 3 <= n % 16 < 7:
                    invert(n // 16 - 1, n % 16 - 3)
                if n >= 16 and n % 16 == 7:
                    scale(n // 16 - 1)
            if following is not None:
                dve_negate_maxima(dve, following)
            for j in range(4):
                invert(NB - 1, j)
            scale(NB - 1)
            if following is not None:
                dve_maxima_rest(dve, following)
            add(NB - 1, slot[3][:, 0:512])

        def dve_grouped(dve):
            dve.wait_ge(s["xm_done"], START + XM0)
            for j in range(2):
                dve.memset(mean2[:, j:j + 1], 0.0).then_inc(s["b_ones"], 1)
            dve.memset(b_nmax[:, :], 0.0)
            dve.memset(KB[64:66, :].bitcast(F32), 1.0).then_inc(s["b_ones"], 1)
            dve.wait_ge(s["b_ones"], START + 3)
            for j in range(2):
                dve.memset(mean2[64 * j:64 * j + 64, j:j + 1], 1.0 / DH).then_inc(s["b_ones"], 1)
            dve_norm(dve, LN_B, lambda b: XM[:, b * 512:b * 512 + 512], 1e-5, dve_plain(dve, LN_B, normed))
            dve.wait_ge(s["wb_in"], START + WB_IN)
            dve_norm(dve, LN_B + 1, lambda b: normed[:, b * 512:b * 512 + 512], 1e-6,
                     dve_affine(dve, LN_B + 1, z2, b_cols[:, 0:1], b_cols[:, 1:2]))
            parts = ((b_wmean[:, 0:16], b_wq[:, :].rearrange("p (h d) -> p h d", h=16)),
                     (b_wmean[:, 16:20], b_wkv[:, 0:256].rearrange("p (h d) -> p h d", h=4)))
            for m, w in parts:
                dve.tensor_reduce(m, w, AX.X, ALU.add).then_inc(s["wsum_done"], 1)
            dve.tensor_scalar(b_cols[:, 2:4], b_cols[:, 2:4], DH ** -0.5, None, ALU.mult).then_inc(s["b_ones"], 1)
            dve.wait_ge(s["wsum_done"], START + 2)
            dve.tensor_scalar(b_wmean[:, :], b_wmean[:, :], 1.0 / DH, None, ALU.mult).then_inc(s["wmean_done"], 1)
            dve.wait_ge(s["wmean_done"], START + 1)
            for m, w in parts:
                n = w.shape[1]
                dve.tensor_tensor(w, w, m.unsqueeze(2).to_broadcast([128, n, DH]), ALU.subtract)\
                   .then_inc(s["wcen_done"], 1)
            dve.wait_ge(s["wcen_done"], START + 2)
            dve.wait_ge(s["b_ones"], START + 6)
            dve_key_weights(dve, 0)
            dve_query_weights(dve, 0)
            dve_keys(dve, 0)
            dve_queries(dve, ln_q(0, 0), 0, 0)
            for n in range(B_UNITS):
                dve_max_unit(dve, 0, n, slot[n % 4])
            dve_negate_maxima(dve, 0)
            dve_maxima_rest(dve, 0)

            def group(kv, last):
                dve.tensor_copy(b_w[:, 2, 0:64], b_wkv[:, bass.ds(kv * 64 + 256, 64)]).then_inc(s["wv_done"], 1)
                dve_query_weights(dve, kv * 2 + 1)
                dve_out_weights(dve, kv * 2)
                dve.tensor_copy(KB[0:64, :], KB_next[:, :].bitcast(F32)).then_inc(s["b_kcur"], 1)
                dve_queries(dve, ln_q(kv, 1), kv * 2 + 1, 1)
                dve_pair(dve, kv * 2, kv * 2 + 1)
                dve_out_weights(dve, kv * 2 + 1)
                if not last:
                    dve_key_weights(dve, kv + 1)
                    dve_query_weights(dve, kv * 2 + 2)
                    dve_keys(dve, kv + 1)
                    dve_queries(dve, ln_q(kv + 1, 0), kv * 2 + 2, 0)
                dve_pair(dve, kv * 2 + 1, None if last else kv * 2 + 2)

            with dve.Fori(0, 3) as kv:
                group(kv, False)
            group(3, True)

        def final_ready(eng):
            if "S1" in stages:
                eng.wait_ge(s["xm_done"], START + 16)
            elif "B" in stages:
                eng.wait_ge(s["b_yadd"], START + 32)
            elif "S0" in stages:
                eng.wait_ge(s["xm_done"], START + XM0)
            else:
                eng.wait_ge(s["a_yadd"], START + 16)

        def pe_out(pe):
            final_ready(pe)
            for c in range(NCH):
                mm = pe.transpose(slot[c // 8][:, (c % 8) * 128:(c % 8) * 128 + 128], XM[:, c * 128:c * 128 + 128],
                                  ident)
                if c % 8 == 7:
                    mm.then_inc(s["tr_out"], 1)

        def act_out(act):
            final_ready(act)
            for i in range(2):
                act.wait_ge(s["tr_out"], START + i + 1)
                act.activation(out_nat[:, 8 * i:8 * i + 8, :].rearrange("p c d -> p (c d)"), slot[i][:, :], ACT.Copy)\
                   .then_inc(s["out_sb"], 1)

        def sp_out(sp):
            for i in range(2):
                sp.wait_ge(s["out_sb"], START + i + 1)
                sp.dma_start(out[0, 1024 * i:1024 * i + 1024, :].rearrange("(c p) d -> p c d", p=128),
                             out_nat[:, 8 * i:8 * i + 8, :]).then_inc(s["out_done"], 16)
            sp.wait_ge(s["out_done"], START + 32)

        def start_counts(eng, which):
            for name in names[which::5]:
                eng.sem_inc(s[name], START)

        @block.sync
        def _(sp):
            start_counts(sp, 0)
            sp_setup(sp)
            if "A" in stages:
                sp_first(sp)
            if "S0" in stages:
                sp.wait_ge(s["stack_in"], START + 8)
                sp_stack(sp, 0)
            if "B" in stages:
                sp_grouped(sp)
            if "S1" in stages:
                sp.wait_ge(s["stack_in"], START + 16)
                sp_stack(sp, 1)
            sp_out(sp)

        @block.gpsimd
        def _(pool):
            start_counts(pool, 1)
            pool_setup(pool)
            if "A" in stages:
                pool_norm(pool, LN_A)
            if "S0" in stages:
                pool_norm(pool, LN_S0)
                pool_stack(pool, 0)
            if "B" in stages:
                pool_grouped(pool)
            if "S1" in stages:
                pool_norm(pool, LN_S1)
                pool_stack(pool, 1)

        @block.scalar
        def _(act):
            start_counts(act, 2)
            act_setup(act)
            if "A" in stages:
                act_first(act)
            if "S0" in stages:
                act.wait_ge(s["setup_pool"], START + 4)
                act_norm(act, LN_S0)
                act.wait_ge(s["stack_out"], START + 1)
                act_stack(act, 0)
            if "B" in stages:
                act_grouped(act)
            if "S1" in stages:
                act_norm(act, LN_S1)
                act.wait_ge(s["stack_out"], START + 2)
                act_stack(act, 1)
            act_out(act)

        @block.vector
        def _(dve):
            start_counts(dve, 3)
            dve_setup(dve)
            if "A" in stages:
                dve_first(dve)
            if "S0" in stages:
                dve_into(dve, 0)
                dve_stack(dve, 0)
            if "B" in stages:
                dve_grouped(dve)
            if "S1" in stages:
                dve_into(dve, 1)
                dve_stack(dve, 1)

        @block.tensor
        def _(pe):
            start_counts(pe, 4)
            pe_setup(pe)
            if "A" in stages:
                pe_first(pe)
            if "S0" in stages:
                pe_into(pe, 0)
                pe_stack(pe, 0)
            if "B" in stages:
                pe_grouped(pe)
            if "S1" in stages:
                pe_into(pe, 1)
                pe_stack(pe, 1)
            pe_out(pe)


_INS = {"x": "L0_attn_a_x", "w_qkv": "L0_attn_a_w_qkv", "w_out": "L0_attn_a_w_out",
        "b_ln_scale": "L0_attn_b_ln_scale", "b_ln_bias": "L0_attn_b_ln_bias", "Wq": "L0_attn_b_Wq",
        "Wkv": "L0_attn_b_Wkv", "qn_scale": "L0_attn_b_qn_scale", "qn_bias": "L0_attn_b_qn_bias",
        "kn_scale": "L0_attn_b_kn_scale", "kn_bias": "L0_attn_b_kn_bias", "Wout": "L0_attn_b_Wout",
        "Wqkv": "L0_ffn_Wqkv", "q_scale": "L0_ffn_q_scale", "k_scale": "L0_ffn_k_scale", "Wo": "L0_ffn_Wo",
        "ln_g": "L0_ffn_ln_g", "ln_b": "L0_ffn_ln_b", "W1": "L0_ffn_W1", "b1": "L0_ffn_b1",
        "W2": "L0_ffn_W2", "b2": "L0_ffn_b2"}


def kernel(**inputs):
    import concourse.bacc as bacc
    from concourse.bass_utils import run_bass_kernel_spmd

    nc = bacc.Bacc("TRN2", target_bir_lowering=False, num_devices=1)
    nc.disable_value_cache = True
    table, place = shape_constants()
    arrays = {"in_shape_constants": np.ascontiguousarray(table)}
    for short, name in _INS.items():
        arrays[f"in_{short}"] = np.ascontiguousarray(inputs[name])
    A = {k[3:]: nc.dram_tensor(k, a.shape, mybir.dt.from_np(a.dtype), kind="ExternalInput").ap()
         for k, a in arrays.items()}
    out = nc.dram_tensor("out", (1, S, D), F32, kind="ExternalOutput").ap()
    build(nc, A, out, place)
    r = run_bass_kernel_spmd(nc, [arrays], core_ids=[0])
    return r.results[0]["out"]
```
